# Optimizing a Trainium2 kernel written in Bass

```python
import numpy as np
import jax
import jax.numpy as jnp

def _softmax(x, axis=-1):
    return jax.nn.softmax(x, axis=axis)

def _gelu(x):
    return jax.nn.gelu(x, approximate=True)

def _silu(x):
    return jax.nn.silu(x)

def _sigmoid(x):
    return jax.nn.sigmoid(x)

def _layernorm(x, axis=-1, eps=1e-05):
    m = jnp.mean(x, axis=axis, keepdims=True)
    v = jnp.var(x, axis=axis, keepdims=True)
    return (x - m) / jnp.sqrt(v + eps)

def _scatter_add(tgt, idx, src, axis=0):
    return tgt.at[idx].add(src)

def _segment_sum(src, seg, n):
    return jax.ops.segment_sum(src, seg, n)
kernel_name = 'mk_decoder_postln_d1_seqx_r4_b9fd68'

def setup_inputs(seed: int=0):
    np.random.seed(seed)
    _w = jnp.asarray

    def _rec_inputs():
        import jax
        import jax.numpy as jnp
        _rk = jax.random.key(seed)
        x = 7.22e-05 + 1 * jax.random.normal(jax.random.fold_in(_rk, 1), (4, 512, 512), jnp.float32)
        _lenS = 512 - jax.random.randint(jax.random.fold_in(_rk, 7), (4,), 0, max(1, 512 // 4) + 1, jnp.int32)
        _lenS2 = 64 - jax.random.randint(jax.random.fold_in(_rk, 8), (4,), 0, max(1, 64 // 4) + 1, jnp.int32)
        _ctx_1024P = jax.random.normal(jax.random.fold_in(_rk, 11), (4, 16, 256), jnp.float32)
        _ctx_1024c = jax.random.dirichlet(jax.random.fold_in(_rk, 511), 0.3 * jnp.ones((16,), jnp.float32), (4, 64))
        _ctx_1024t = jnp.einsum('bsk,bkd->bsd', _ctx_1024c, _ctx_1024P)
        _ctx_1024t = _ctx_1024t * jax.lax.rsqrt(jnp.mean(jnp.square(_ctx_1024t)) + 1e-12) * 0.953939
        ctx_1024 = -0.000673644 + 1.00013 * (_ctx_1024t + 0.3 * jax.random.normal(jax.random.fold_in(_rk, 611), (4, 64, 256), jnp.float32))
        return (x, ctx_1024)
    x, ctx_1024 = _rec_inputs()

    def _L0_attn_setup():
        import jax, jax.numpy as jnp
        import numpy as np
        B, T, D = (1, 512, 512)
        H, DK = (16, 128)
        ROPE, NOPE, VD = (64, 64, 128)
        KVR, QR = (128, 192)
        SCALE = DK ** (-0.5)
        EPS = float(np.finfo(np.float32).eps)

        def rms_norm(h, w):
            var = jnp.mean(h * h, axis=-1, keepdims=True)
            return h * jax.lax.rsqrt(var + EPS) * w

        def rope(x):
            half = ROPE // 2
            inv_freq = 1.0 / 10000.0 ** (jnp.arange(0, ROPE, 2, dtype=jnp.float32) / ROPE)
            t = jnp.arange(x.shape[-2], dtype=jnp.float32)
            freqs = jnp.outer(t, inv_freq)
            cos, sin = (jnp.cos(freqs), jnp.sin(freqs))
            x1, x2 = (x[..., :half], x[..., half:])
            return jnp.concatenate([x1 * cos - x2 * sin, x1 * sin + x2 * cos], axis=-1)
        key = jax.random.key(seed)
        ks = jax.random.split(key, 6)
        s = 0.02
        return {'x': jax.random.normal(ks[0], (B, T, D), jnp.float32), 'wq_a': jax.random.normal(ks[1], (D, QR), jnp.float32) * s, 'q_a_norm_w': jnp.ones((QR,), jnp.float32), 'wq_b': jax.random.normal(ks[2], (QR, H * DK), jnp.float32) * s, 'wkv_a': jax.random.normal(ks[3], (D, KVR + ROPE), jnp.float32) * s, 'kv_a_norm_w': jnp.ones((KVR,), jnp.float32), 'wkv_b': jax.random.normal(ks[4], (KVR, H * (NOPE + VD)), jnp.float32) * s, 'wo': jax.random.normal(ks[5], (H * VD, D), jnp.float32) * s}
    _L0_attn_all = _L0_attn_setup()
    _L0_attn_in = {k: v for k, v in _L0_attn_all.items() if k in ('wq_a', 'q_a_norm_w', 'wq_b', 'wkv_a', 'kv_a_norm_w', 'wkv_b', 'wo')}
    del _L0_attn_all

    def _L0_xattn_setup():
        import jax, jax.numpy as jnp
        import numpy as np
        B, S1, S2, DCA = (2, 512, 256, 16)
        QDIM, KDIM, H = (512, 256, 16)
        HD = QDIM // H
        SCALE = HD ** (-0.5)
        EPS = 1e-06
        DCA_WEIGHT = 1.0

        def _ln(t, w, b):
            m = jnp.mean(t, axis=-1, keepdims=True)
            v = jnp.var(t, axis=-1, keepdims=True)
            return (t - m) * jax.lax.rsqrt(v + EPS) * w + b

        def _attn(q, k, v):
            s = jnp.einsum('bhqd,bhkd->bhqk', q, k) * SCALE
            p = jax.nn.softmax(s, axis=-1)
            return jnp.einsum('bhqk,bhkd->bhqd', p, v)
        key = jax.random.key(seed)
        ks = jax.random.split(key, 8)
        w = lambda k, shape: jax.random.normal(k, shape, jnp.float32) * 0.02
        return {'x': jax.random.normal(ks[0], (B, S1, QDIM), jnp.float32), 'y': jax.random.normal(ks[1], (B, S2 + DCA, KDIM), jnp.float32), 'Wq': w(ks[2], (QDIM, QDIM)), 'bq': jnp.zeros((QDIM,), jnp.float32), 'Wk': w(ks[3], (KDIM, QDIM)), 'bk': jnp.zeros((QDIM,), jnp.float32), 'Wv': w(ks[4], (KDIM, QDIM)), 'bv': jnp.zeros((QDIM,), jnp.float32), 'Wkv_dca': w(ks[5], (KDIM, 2 * QDIM)), 'bkv_dca': jnp.zeros((2 * QDIM,), jnp.float32), 'qn_w': jnp.ones((HD,), jnp.float32), 'qn_b': jnp.zeros((HD,), jnp.float32), 'kn_w': jnp.ones((HD,), jnp.float32), 'kn_b': jnp.zeros((HD,), jnp.float32), 'kn_dca_w': jnp.ones((HD,), jnp.float32), 'kn_dca_b': jnp.zeros((HD,), jnp.float32), 'Wo': w(ks[6], (QDIM, QDIM)), 'bo': jnp.zeros((QDIM,), jnp.float32)}
    _L0_xattn_all = _L0_xattn_setup()
    _L0_xattn_in = {k: v for k, v in _L0_xattn_all.items() if k in ('Wq', 'bq', 'Wk', 'bk', 'Wv', 'bv', 'Wkv_dca', 'bkv_dca', 'qn_w', 'qn_b', 'kn_w', 'kn_b', 'kn_dca_w', 'kn_dca_b', 'Wo', 'bo')}
    del _L0_xattn_all

    def _L0_ffn_setup():
        import jax, jax.numpy as jnp
        import numpy as np
        B, S, D = (4, 512, 512)
        E = 8
        N_SHARE = 2
        N_ROUTED = E - N_SHARE
        H = 2048 // E
        key = jax.random.key(seed)
        ks = jax.random.split(key, 12)
        s = 0.02
        return {'x': jax.random.normal(ks[0], (B, S, D), jnp.float32), 'Wg': jax.random.normal(ks[1], (D, E), jnp.float32) * s, 'bg': jnp.zeros((E,), jnp.float32), 'Wgate': jax.random.normal(ks[2], (N_ROUTED, D, H), jnp.float32) * s, 'bgate': jnp.zeros((N_ROUTED, H), jnp.float32), 'Wup': jax.random.normal(ks[3], (N_ROUTED, D, H), jnp.float32) * s, 'bup': jnp.zeros((N_ROUTED, H), jnp.float32), 'Wdown': jax.random.normal(ks[4], (N_ROUTED, H, D), jnp.float32) * s, 'bdown': jnp.zeros((N_ROUTED, D), jnp.float32), 'Ws_up': jax.random.normal(ks[5], (D, N_SHARE * H), jnp.float32) * s, 'bs_up': jnp.zeros((N_SHARE * H,), jnp.float32), 'Ws_down': jax.random.normal(ks[6], (N_SHARE * H, D), jnp.float32) * s, 'bs_down': jnp.zeros((D,), jnp.float32)}
    _L0_ffn_all = _L0_ffn_setup()
    _L0_ffn_in = {k: v for k, v in _L0_ffn_all.items() if k in ('Wg', 'bg', 'Wgate', 'bgate', 'Wup', 'bup', 'Wdown', 'bdown', 'Ws_up', 'bs_up', 'Ws_down', 'bs_down')}
    del _L0_ffn_all
    return {'x': x, 'ctx_1024': ctx_1024, 'L0_attn_wq_a': _L0_attn_in['wq_a'], 'L0_attn_q_a_norm_w': _L0_attn_in['q_a_norm_w'], 'L0_attn_wq_b': _L0_attn_in['wq_b'], 'L0_attn_wkv_a': _L0_attn_in['wkv_a'], 'L0_attn_kv_a_norm_w': _L0_attn_in['kv_a_norm_w'], 'L0_attn_wkv_b': _L0_attn_in['wkv_b'], 'L0_attn_wo': _L0_attn_in['wo'], 'L0_xattn_Wq': _L0_xattn_in['Wq'], 'L0_xattn_bq': _L0_xattn_in['bq'], 'L0_xattn_Wk': _L0_xattn_in['Wk'], 'L0_xattn_bk': _L0_xattn_in['bk'], 'L0_xattn_Wv': _L0_xattn_in['Wv'], 'L0_xattn_bv': _L0_xattn_in['bv'], 'L0_xattn_Wkv_dca': _L0_xattn_in['Wkv_dca'], 'L0_xattn_bkv_dca': _L0_xattn_in['bkv_dca'], 'L0_xattn_qn_w': _L0_xattn_in['qn_w'], 'L0_xattn_qn_b': _L0_xattn_in['qn_b'], 'L0_xattn_kn_w': _L0_xattn_in['kn_w'], 'L0_xattn_kn_b': _L0_xattn_in['kn_b'], 'L0_xattn_kn_dca_w': _L0_xattn_in['kn_dca_w'], 'L0_xattn_kn_dca_b': _L0_xattn_in['kn_dca_b'], 'L0_xattn_Wo': _L0_xattn_in['Wo'], 'L0_xattn_bo': _L0_xattn_in['bo'], 'L0_ffn_Wg': _L0_ffn_in['Wg'], 'L0_ffn_bg': _L0_ffn_in['bg'], 'L0_ffn_Wgate': _L0_ffn_in['Wgate'], 'L0_ffn_bgate': _L0_ffn_in['bgate'], 'L0_ffn_Wup': _L0_ffn_in['Wup'], 'L0_ffn_bup': _L0_ffn_in['bup'], 'L0_ffn_Wdown': _L0_ffn_in['Wdown'], 'L0_ffn_bdown': _L0_ffn_in['bdown'], 'L0_ffn_Ws_up': _L0_ffn_in['Ws_up'], 'L0_ffn_bs_up': _L0_ffn_in['bs_up'], 'L0_ffn_Ws_down': _L0_ffn_in['Ws_down'], 'L0_ffn_bs_down': _L0_ffn_in['bs_down']}

def reference(x, ctx_1024, L0_attn_wq_a, L0_attn_q_a_norm_w, L0_attn_wq_b, L0_attn_wkv_a, L0_attn_kv_a_norm_w, L0_attn_wkv_b, L0_attn_wo, L0_xattn_Wq, L0_xattn_bq, L0_xattn_Wk, L0_xattn_bk, L0_xattn_Wv, L0_xattn_bv, L0_xattn_Wkv_dca, L0_xattn_bkv_dca, L0_xattn_qn_w, L0_xattn_qn_b, L0_xattn_kn_w, L0_xattn_kn_b, L0_xattn_kn_dca_w, L0_xattn_kn_dca_b, L0_xattn_Wo, L0_xattn_bo, L0_ffn_Wg, L0_ffn_bg, L0_ffn_Wgate, L0_ffn_bgate, L0_ffn_Wup, L0_ffn_bup, L0_ffn_Wdown, L0_ffn_bdown, L0_ffn_Ws_up, L0_ffn_bs_up, L0_ffn_Ws_down, L0_ffn_bs_down):
    import jax
    import jax.numpy as jnp

    def _L0_attn_ref(x, wq_a, q_a_norm_w, wq_b, wkv_a, kv_a_norm_w, wkv_b, wo):
        import jax, jax.numpy as jnp
        import numpy as np
        B, T, D = (1, 512, 512)
        H, DK = (16, 128)
        ROPE, NOPE, VD = (64, 64, 128)
        KVR, QR = (128, 192)
        SCALE = DK ** (-0.5)
        EPS = float(np.finfo(np.float32).eps)

        def rms_norm(h, w):
            var = jnp.mean(h * h, axis=-1, keepdims=True)
            return h * jax.lax.rsqrt(var + EPS) * w

        def rope(x):
            half = ROPE // 2
            inv_freq = 1.0 / 10000.0 ** (jnp.arange(0, ROPE, 2, dtype=jnp.float32) / ROPE)
            t = jnp.arange(x.shape[-2], dtype=jnp.float32)
            freqs = jnp.outer(t, inv_freq)
            cos, sin = (jnp.cos(freqs), jnp.sin(freqs))
            x1, x2 = (x[..., :half], x[..., half:])
            return jnp.concatenate([x1 * cos - x2 * sin, x1 * sin + x2 * cos], axis=-1)
        b, t, _ = x.shape
        q = rms_norm(x @ wq_a, q_a_norm_w) @ wq_b
        q = q.reshape(b, t, H, DK).transpose(0, 2, 1, 3)
        q_nope, q_pe = (q[..., :NOPE], q[..., NOPE:])
        ckv = x @ wkv_a
        c, k_pe = (ckv[..., :KVR], ckv[..., KVR:])
        kv = rms_norm(c, kv_a_norm_w) @ wkv_b
        kv = kv.reshape(b, t, H, NOPE + VD).transpose(0, 2, 1, 3)
        k_nope, v = (kv[..., :NOPE], kv[..., NOPE:])
        q_pe = rope(q_pe)
        k_pe = rope(k_pe[:, None])
        k_pe = jnp.broadcast_to(k_pe, (b, H, t, ROPE))
        qs = jnp.concatenate([q_nope, q_pe], axis=-1)
        ks = jnp.concatenate([k_nope, k_pe], axis=-1)
        scores = jnp.einsum('bhqd,bhkd->bhqk', qs, ks) * SCALE
        attn = jax.nn.softmax(scores, axis=-1)
        out = jnp.einsum('bhqk,bhkd->bhqd', attn, v)
        out = out.transpose(0, 2, 1, 3).reshape(b, t, H * VD)
        return out @ wo

    def _L0_xattn_ref(x, y, Wq, bq, Wk, bk, Wv, bv, Wkv_dca, bkv_dca, qn_w, qn_b, kn_w, kn_b, kn_dca_w, kn_dca_b, Wo, bo):
        import jax, jax.numpy as jnp
        import numpy as np
        B, S1, S2, DCA = (2, 512, 256, 16)
        QDIM, KDIM, H = (512, 256, 16)
        HD = QDIM // H
        SCALE = HD ** (-0.5)
        EPS = 1e-06
        DCA_WEIGHT = 1.0

        def _ln(t, w, b):
            m = jnp.mean(t, axis=-1, keepdims=True)
            v = jnp.var(t, axis=-1, keepdims=True)
            return (t - m) * jax.lax.rsqrt(v + EPS) * w + b

        def _attn(q, k, v):
            s = jnp.einsum('bhqd,bhkd->bhqk', q, k) * SCALE
            p = jax.nn.softmax(s, axis=-1)
            return jnp.einsum('bhqk,bhkd->bhqd', p, v)
        b, s1, _ = x.shape
        y_dca = y[:, -DCA:, :]
        y_main = y[:, :-DCA, :]
        kv_dca = (y_dca @ Wkv_dca + bkv_dca).reshape(b, DCA, 2, H, HD)
        k_dca = _ln(kv_dca[:, :, 0], kn_dca_w, kn_dca_b)
        v_dca = kv_dca[:, :, 1]
        s2 = y_main.shape[1]
        q = _ln((x @ Wq + bq).reshape(b, s1, H, HD), qn_w, qn_b)
        kv = jnp.concatenate([y_main @ Wk + bk, y_main @ Wv + bv], axis=-1)
        kv = kv.reshape(b, s2, H, 2 * HD)
        k = _ln(kv[..., :HD], kn_w, kn_b)
        v = kv[..., HD:]
        qT = q.transpose(0, 2, 1, 3)
        ctx = _attn(qT, k.transpose(0, 2, 1, 3), v.transpose(0, 2, 1, 3))
        ctx = ctx.transpose(0, 2, 1, 3).reshape(b, s1, QDIM)
        ctx_dca = _attn(qT, k_dca.transpose(0, 2, 1, 3), v_dca.transpose(0, 2, 1, 3))
        ctx_dca = ctx_dca.transpose(0, 2, 1, 3).reshape(b, s1, QDIM)
        ctx = ctx + DCA_WEIGHT * ctx_dca
        return ctx @ Wo + bo

    def _L0_ffn_ref(x, Wg, bg, Wgate, bgate, Wup, bup, Wdown, bdown, Ws_up, bs_up, Ws_down, bs_down):
        import jax, jax.numpy as jnp
        import numpy as np
        B, S, D = (4, 512, 512)
        E = 8
        N_SHARE = 2
        N_ROUTED = E - N_SHARE
        H = 2048 // E
        b, s, d = x.shape
        T = b * s
        n = Wgate.shape[0]
        xf = x.reshape(T, d)
        gate = xf @ Wg + bg
        vals, ids = jax.lax.top_k(gate, n)
        rows = jnp.arange(T)[:, None]
        masked = jnp.full_like(gate, -jnp.inf).at[rows, ids].set(vals)
        probs = jax.nn.softmax(masked, axis=-1)
        routed_mask = (ids[:, :, None] == jnp.arange(n)).any(axis=1)
        w = probs[:, :n] * routed_mask
        g = jnp.einsum('td,ndh->tnh', xf, Wgate) + bgate
        u = jnp.einsum('td,ndh->tnh', xf, Wup) + bup
        h = jax.nn.silu(g) * u
        eo = jnp.einsum('tnh,nhd->tnd', h, Wdown) + bdown
        routed_out = jnp.einsum('tnd,tn->td', eo, w)
        share = jax.nn.silu(xf @ Ws_up + bs_up) @ Ws_down + bs_down
        return (routed_out + share).reshape(b, s, d)
    x = _layernorm(x + _L0_attn_ref(x, L0_attn_wq_a, L0_attn_q_a_norm_w, L0_attn_wq_b, L0_attn_wkv_a, L0_attn_kv_a_norm_w, L0_attn_wkv_b, L0_attn_wo), axis=-1)
    x = _layernorm(x + _L0_xattn_ref(x, ctx_1024, L0_xattn_Wq, L0_xattn_bq, L0_xattn_Wk, L0_xattn_bk, L0_xattn_Wv, L0_xattn_bv, L0_xattn_Wkv_dca, L0_xattn_bkv_dca, L0_xattn_qn_w, L0_xattn_qn_b, L0_xattn_kn_w, L0_xattn_kn_b, L0_xattn_kn_dca_w, L0_xattn_kn_dca_b, L0_xattn_Wo, L0_xattn_bo), axis=-1)
    x = _layernorm(x + _L0_ffn_ref(x, L0_ffn_Wg, L0_ffn_bg, L0_ffn_Wgate, L0_ffn_bgate, L0_ffn_Wup, L0_ffn_bup, L0_ffn_Wdown, L0_ffn_bdown, L0_ffn_Ws_up, L0_ffn_bs_up, L0_ffn_Ws_down, L0_ffn_bs_down), axis=-1)
    return x

_drawn_inputs = setup_inputs


def setup_inputs(seed=0):
    import zlib

    import numpy as np

    out = dict(_drawn_inputs(seed))
    spreads = {'L0_attn_q_a_norm_w': (1.0, 0.6),
     'L0_attn_kv_a_norm_w': (1.0, 0.6),
     'L0_xattn_bq': (0.0, 0.665),
     'L0_xattn_bk': (0.0, 0.1),
     'L0_xattn_bv': (0.0, 0.1),
     'L0_xattn_bkv_dca': (0.0, 0.1),
     'L0_xattn_qn_w': (1.0, 0.6),
     'L0_xattn_qn_b': (0.0, 0.8),
     'L0_xattn_kn_w': (1.0, 0.6),
     'L0_xattn_kn_b': (0.0, 2.0),
     'L0_xattn_kn_dca_w': (1.0, 0.6),
     'L0_xattn_kn_dca_b': (0.0, 2.0),
     'L0_xattn_bo': (0.0, 0.1),
     'L0_ffn_bg': (0.0, 0.8),
     'L0_ffn_bgate': (0.0, 0.8),
     'L0_ffn_bup': (0.0, 0.8),
     'L0_ffn_bdown': (0.0, 0.392),
     'L0_ffn_bs_up': (0.0, 0.308),
     'L0_ffn_bs_down': (0.0, 0.1)}
    factors = {'L0_attn_wq_a': 8.0,
     'L0_attn_wq_b': 8.0,
     'L0_attn_wkv_a': 5.892,
     'L0_attn_wkv_b': 6.023,
     'L0_attn_wo': 5.994,
     'L0_ffn_Wgate': 4.382,
     'L0_ffn_Wup': 4.302,
     'L0_ffn_Wdown': 4.208}
    for name, (base, spread) in spreads.items():
        noise = np.random.default_rng([zlib.crc32(name.encode()), seed]).standard_normal(out[name].shape)
        drawn = base * np.exp(spread * noise) if base else spread * noise
        out[name] = jnp.asarray(drawn.astype(out[name].dtype))
    for name, factor in factors.items():
        out[name] = (out[name] * factor).astype(out[name].dtype)
    return out
```

```python
from contextlib import ExitStack

import concourse.bass as bass
import numpy as np
from concourse import mybir

F32 = mybir.dt.float32
F32R = mybir.dt.float32r
ACT = mybir.ActivationFunctionType
ALU = mybir.AluOpType
AX = mybir.AxisListType

P = 128
B, T, D = 4, 512, 512
TT = T // P
DT = D // P

H, DK, ROPE, NOPE, VD = 16, 128, 64, 64, 128
KVR, QR = 128, 192
QR2 = QR - P
HALF = ROPE // 2
A_SCALE = float(DK) ** -0.5
A_EPS = float(np.finfo(np.float32).eps)
AW = QR + KVR + ROPE
PAIRS = H // 2
STAGE = 2 * DK + 2 * DK + 2 * NOPE

XH, HD = 16, 32
KEYS, DCA = 64, 16
MAIN = KEYS - DCA
CD = 256
CT = CD // P
X_SCALE = float(HD) ** -0.5
X_EPS = 1e-06

N_EXP, TOP, NG = 8, 6, 8
EH = 256
HT = EH // P
QUAD = 32

LN_EPS = 1e-05


class Memory:

    def __init__(self, nc, ctx):
        self.nc, self.ctx = nc, ctx

    def sb(self, name, shape, dt=F32):
        return self.ctx.enter_context(self.nc.sbuf_tensor(name, shape, dt))

    def split(self, name, shape):
        return self.sb(name + "_hi", shape, F32R), self.sb(name + "_lo", shape, F32R)

    def banks(self, name, n):
        return [self.ctx.enter_context(self.nc.psum_tensor(f"{name}{i}", [P, 512], F32)) for i in range(n)]

    def sem(self, name):
        return self.ctx.enter_context(self.nc.semaphore(name))


def f32(ap):
    return ap.bitcast(F32)


def three(hi_lo_lhsT, hi_lo_rhs):
    (lh, ll), (rh, rl) = hi_lo_lhsT, hi_lo_rhs
    return [(lh, rh), (lh, rl), (ll, rh)]


def constants(nc, ctx):
    ident = ctx.enter_context(nc.sbuf_tensor("ident", [P, P], F32))
    with ExitStack() as inner:
        m = Memory(nc, inner)
        cleared, made = m.sem("ident_cleared"), m.sem("ident_made")
        block = inner.enter_context(nc.Block())

        @block.gpsimd
        def _(pool):
            pool.memset(ident[:, :], 0.0).then_inc(cleared, 1)
            pool.wait_ge(cleared, 1)
            pool.affine_select(out=ident[:, :], in_=ident[:, :], compare_op=ALU.not_equal, fill=1.0, base=0,
                               pattern=[[-1, P]], channel_multiplier=1).then_inc(made, 1)
            pool.wait_ge(made, 1)

    return {"ident": ident}


def attention_phase(nc, const, dram):
    ident = const["ident"]
    with ExitStack() as ctx:
        m = Memory(nc, ctx)
        wa_hi, wa_lo = m.split("wa", [P, DT, AW])
        wvo_hi, wvo_lo = m.split("wvo", [P, H, D])
        norm_w = m.sb("norm_w", [P, 3])
        tab = m.sb("tab", [P, 3, T])
        ktab = m.sb("ktab", [P, TT, 2, HALF])
        zero = m.sb("zero", [P, D], F32R)
        eps_a = m.sb("eps_a", [P, 2])
        x_in = m.sb("x_in", [P, TT, D])
        qc = m.sb("qc", [P, TT, AW])
        ssq = m.sb("ssq", [P, 2, TT])
        rms = m.sb("rms", [P, 2, TT])
        rstd = m.sb("rstd", [P, 2, TT])
        kpe = m.sb("kpe", [P, TT, 2 * ROPE])
        ktmp = m.sb("ktmp", [P, 4, TT, HALF])
        qaT_hi, qaT_lo = m.split("qaT", [P, 2, T])
        cT_hi, cT_lo = m.split("cT", [P, T])
        c_hi, c_lo = m.split("c", [P, TT, KVR])
        ws_raw = m.sb("ws_raw", [P, STAGE])
        ws_hi, ws_lo = m.split("ws", [P, STAGE])
        q_raw = m.sb("q_raw", [P, T])
        q_swap = m.sb("q_swap", [P, T])
        q_sin = m.sb("q_sin", [P, T])
        q_rot = m.sb("q_rot", [P, T])
        q_hi, q_lo = m.split("q", [P, 2, T])
        k_raw = m.sb("k_raw", [P, T])
        k_hi, k_lo = m.split("k", [P, 2, T])
        probs = m.sb("probs", [P, TT, T])
        pT_hi, pT_lo = m.split("pT", [P, 2, TT, T])
        o_hi, o_lo = m.split("o", [P, 2, T])
        wa_raw = qc
        wo_in, wvT, wv_in = probs[:, 0:2, :], probs[:, 2, :].rearrange("p (j n) -> p j n", n=KVR), \
            probs[:, 3, :].rearrange("p (j n) -> p j n", n=VD)
        sq_junk = q_sin
        xT_hi, xT_lo = pT_hi[:, 0, :, :], pT_lo[:, 0, :, :]
        x1 = probs
        neg_max = m.sb("neg_max", [P, 2, TT])
        total = m.sb("total", [P, 2, TT])
        inv = m.sb("inv", [P, 2, TT])
        bn = m.sb("bn", [P, TT, 6])
        mv = m.sb("mv", [P, TT, 2])
        sd = m.sb("sd", [P, TT])
        rs = m.sb("rs", [P, TT])

        Y = m.banks("Y", TT)
        S = m.banks("S", 2)
        (TR,) = m.banks("TR", 1)
        (M,) = m.banks("M", 1)
        QC = [S[0], S[1], TR, M]

        s = {n: m.sem(n) for n in (
            "wa_loaded", "small_loaded", "vo_loaded0", "vo_loaded1", "wa_split_hi", "wa_split_lo", "zeroed",
            "wv_turned", "wvT_kept", "wvo_done", "wvo_hi_kept", "wvo_lo_kept",
            "x_loaded", "xT_done", "xT_hi_kept", "xT_lo_kept", "qc_done", "qc_kept", "squared", "rooted",
            "inverted", "scaled", "c_split", "k_mults", "k_rot", "abT_done", "abT_hi_kept", "abT_lo_kept",
            "ws_loaded", "ws_hi_kept", "ws_lo_kept", "seeded",
            "q_done", "q_kept", "q_swapped", "q_mults", "q_turned", "q_hi_kept", "q_lo_kept",
            "k_done", "k_kept", "k_hi_kept", "k_lo_kept",
            "scores_done", "max_done", "exp_done", "inv_done", "probs_done", "turned", "pT_hi_kept", "pT_lo_kept",
            "pv_done", "o_hi_kept", "o_lo_kept", "y_done",
            "added", "bn_done", "aggregated", "sd_done", "rs_done", "x1_done", "x1_stored")}

        block = ctx.enter_context(nc.Block())

        @block.sync
        def _(sp):
            sp.dma_start(wa_raw[:, :, :], dram["wa"].rearrange("(k p) n -> p k n", p=P)).then_inc(s["wa_loaded"], 16)
            sp.dma_start(x_in[:, :, :], dram["x"][0].rearrange("(t p) d -> p t d", p=P)).then_inc(s["x_loaded"], 16)
            sp.dma_start(norm_w[:, :], dram["norm_w"]).then_inc(s["small_loaded"], 16)
            sp.dma_start(tab[:, :, :], dram["rope_T"]).then_inc(s["small_loaded"], 16)
            sp.dma_start(ktab[:, :, :, :], dram["rope_tok"]).then_inc(s["small_loaded"], 16)
            sp.dma_start(ws_raw[:, :], dram["ws"][0]).then_inc(s["ws_loaded"], 16)

            def vo_weights(j, h):
                sp.dma_start(wv_in[:, j, :], dram["wv"][h]).then_inc(s[f"vo_loaded{j}"], 16)
                sp.dma_start(wo_in[:, j, :], dram["wo"][h]).then_inc(s[f"vo_loaded{j}"], 16)

            vo_weights(0, 0)
            vo_weights(1, 1)
            with sp.Fori(1, PAIRS) as i:
                for j in range(2):
                    sp.wait_ge(s["wvo_done"], 2 * i + j - 1)
                    vo_weights(j, 2 * i + j)

            with sp.Fori(0, B - 1) as b:
                with sp.Fori(0, PAIRS - 1) as i:
                    sp.wait_ge(s["ws_lo_kept"], PAIRS * b + i + 1)
                    sp.dma_start(ws_raw[:, :], dram["ws"][i + 1]).then_inc(s["ws_loaded"], 16)
                sp.wait_ge(s["added"], TT * (b + 1))
                sp.dma_start(x_in[:, :, :], dram["x"].rearrange("b (t p) d -> b p t d", p=P)[b + 1])\
                  .then_inc(s["x_loaded"], 16)
                sp.wait_ge(s["x1_done"], TT * (b + 1))
                sp.dma_start(dram["x1"].rearrange("b (t p) d -> b p t d", p=P)[b], x1[:, :, :])\
                  .then_inc(s["x1_stored"], 16)
                sp.wait_ge(s["x1_stored"], 16 * b + 16)
                sp.dma_start(ws_raw[:, :], dram["ws"][0]).then_inc(s["ws_loaded"], 16)
            with sp.Fori(0, PAIRS - 1) as i:
                sp.wait_ge(s["ws_lo_kept"], PAIRS * (B - 1) + i + 1)
                sp.dma_start(ws_raw[:, :], dram["ws"][i + 1]).then_inc(s["ws_loaded"], 16)
            sp.wait_ge(s["x1_done"], TT * B)
            sp.dma_start(dram["x1"][B - 1].rearrange("(t p) d -> p t d", p=P), x1[:, :, :])\
              .then_inc(s["x1_stored"], 16)
            sp.wait_ge(s["x1_stored"], 16 * B)

        @block.tensor
        def _(pe):
            with pe.Fori(0, PAIRS) as i:
                for j in range(2):
                    pe.wait_ge(s[f"vo_loaded{j}"], 32 * i + 32)
                    if j:
                        pe.wait_ge(s["wvT_kept"], 2 * i + j)
                    pe.transpose(TR[:, 0:KVR], wv_in[:, j, :], ident[:, :]).then_inc(s["wv_turned"], 1)
                    pe.wait_ge(s["wvT_kept"], 2 * i + j + 1)
                    if j:
                        pe.wait_ge(s["wvo_lo_kept"], 2 * i + j)
                    pe.matmul(M[:, :], wvT[:, j, :], wo_in[:, j, :], start=True, stop=True)\
                      .then_inc(s["wvo_done"], 1)
                pe.wait_ge(s["wvo_lo_kept"], 2 * i + 2)

            def q_project(n, h_buf):
                e = h_buf
                steps = three((ws_hi[:, e * DK:(e + 1) * DK], ws_lo[:, e * DK:(e + 1) * DK]),
                              (qaT_hi[:, 0, :], qaT_lo[:, 0, :]))
                o = 2 * DK + e * DK
                steps += three((ws_hi[0:QR2, o:o + DK], ws_lo[0:QR2, o:o + DK]),
                               (qaT_hi[0:QR2, 1, :], qaT_lo[0:QR2, 1, :]))
                for j, (lhsT, rhs) in enumerate(steps):
                    mm = pe.matmul(M[:, :], lhsT, rhs, start=j == 0, stop=j == len(steps) - 1)
                mm.then_inc(s["q_done"], 1)

            def k_project():
                o = 4 * DK
                for j, (lhsT, rhs) in enumerate(three((ws_hi[:, o:o + DK], ws_lo[:, o:o + DK]),
                                                      (cT_hi[:, :], cT_lo[:, :]))):
                    mm = pe.matmul(M[:, :], lhsT, rhs, start=j == 0, stop=j == 2)
                mm.then_inc(s["k_done"], 1)

            def scores(n, e, t, free):
                if t == 0:
                    pe.wait_ge(s["q_lo_kept"], n + 1)
                    pe.wait_ge(s["k_lo_kept"], n + 1)
                if free:
                    pe.wait_ge(s["exp_done"], TT * n + t - 1)
                for j, (lhsT, rhs) in enumerate(three(
                        (q_hi[:, e, t * P:(t + 1) * P], q_lo[:, e, t * P:(t + 1) * P]),
                        (k_hi[:, e, :], k_lo[:, e, :]))):
                    mm = pe.matmul(S[t % 2][:, :], lhsT, rhs, start=j == 0, stop=j == 2)
                mm.then_inc(s["scores_done"], 1)

            def turn(n, t, free=True):
                pe.wait_ge(s["probs_done"], TT * n + t + 1)
                if free:
                    pe.wait_ge(s["pT_lo_kept"], TT * n + t)
                for k in range(TT):
                    mm = pe.transpose(TR[:, k * P:(k + 1) * P], probs[:, t, k * P:(k + 1) * P], ident[:, :])
                mm.then_inc(s["turned"], 1)

            def weigh(n, e, ks):
                if ks[0] == 0:
                    pe.wait_ge(s["pT_lo_kept"], TT * n + TT)
                for k in ks:
                    for j, (lhsT, rhs) in enumerate(three((c_hi[:, k, :], c_lo[:, k, :]),
                                                          (pT_hi[:, e, k, :], pT_lo[:, e, k, :]))):
                        mm = pe.matmul(M[:, :], lhsT, rhs, start=k == 0 and j == 0, stop=k == TT - 1 and j == 2)
                if ks[-1] == TT - 1:
                    mm.then_inc(s["pv_done"], 1)

            def output(n, h, e, t, last=False):
                if t == 0:
                    pe.wait_ge(s["o_lo_kept"], n + 1)
                for j, (lhsT, rhs) in enumerate(three(
                        (o_hi[:, e, t * P:(t + 1) * P], o_lo[:, e, t * P:(t + 1) * P]),
                        (wvo_hi[:, h, :], wvo_lo[:, h, :]))):
                    mm = pe.matmul(Y[t][:, :], lhsT, rhs, start=False, stop=last and j == 2)
                if t == TT - 1 or last:
                    mm.then_inc(s["y_done"], 1)

            def period(n, h, e, first, last):
                for t in range(TT):
                    turn(n, t)
                    if not (last and e == 1):
                        scores(n + 1, 1 - e, t, True)
                    if t == 0 and not last:
                        pe.wait_ge(s["ws_lo_kept"], pair["no"] + 2)
                        if first and e == 0:
                            pe.wait_ge(s["q_kept"], n + 2)
                        elif first:
                            pe.wait_ge(s["k_kept"], pair["no"] + 2)
                        else:
                            pe.wait_ge(s["o_lo_kept"], n - 1)
                        q_project(n + 2, e)
                    if t == 1 and e == 0 and not last:
                        pe.wait_ge(s["q_kept"], n + 3)
                        k_project()
                    if t >= 2 and not (first and e == 0):
                        if t == 2 and last:
                            pe.wait_ge(s["o_lo_kept"], n - 1)
                        elif t == 2 and e == 0:
                            pe.wait_ge(s["k_kept"], pair["no"] + 2)
                        elif t == 2:
                            pe.wait_ge(s["q_kept"], n + 3)
                        weigh(n - 1, 1 - e, range(2 * (t - 2), 2 * (t - 2) + 2))
                    if not first:
                        output(n - 2, h - 2, e, t)

            pair = {}

            pe.wait_ge(s["wa_split_lo"], 1)
            with pe.Fori(0, B) as b:
                pe.wait_ge(s["x_loaded"], 16 * (b + 1))
                for d in range(DT):
                    for t in range(TT):
                        mm = pe.transpose(Y[d][:, t * P:(t + 1) * P], x_in[:, t, d * P:(d + 1) * P], ident[:, :])
                    mm.then_inc(s["xT_done"], 1)
                for t in range(TT):
                    for d in range(DT):
                        if t == 0:
                            pe.wait_ge(s["xT_lo_kept"], DT * b + d + 1)
                        for j, (lhsT, rhs) in enumerate(three(
                                (xT_hi[:, d, t * P:(t + 1) * P], xT_lo[:, d, t * P:(t + 1) * P]),
                                (wa_hi[:, d, :], wa_lo[:, d, :]))):
                            mm = pe.matmul(QC[t][:, 0:AW], lhsT, rhs, start=d == 0 and j == 0,
                                           stop=d == DT - 1 and j == 2)
                    mm.then_inc(s["qc_done"], 1)
                pe.wait_ge(s["scaled"], 2 * TT * (b + 1))
                for t in range(TT):
                    pe.transpose(Y[0][:, t * P:(t + 1) * P], qc[:, t, 0:P], ident[:, :])
                for t in range(TT):
                    pe.transpose(Y[1][0:QR2, t * P:(t + 1) * P], qc[:, t, P:QR], ident[:, :])
                for t in range(TT):
                    mm = pe.transpose(Y[2][:, t * P:(t + 1) * P], qc[:, t, QR:QR + KVR], ident[:, :])
                mm.then_inc(s["abT_done"], 1)
                pe.wait_ge(s["k_rot"], 2 * (b + 1))
                for t in range(TT):
                    mm = pe.transpose(Y[3][:, t * P:(t + 1) * P], kpe[:, t, :], ident[:, :])
                mm.then_inc(s["abT_done"], 1)

                pe.wait_ge(s["abT_lo_kept"], 5 * (b + 1))
                pe.wait_ge(s["ws_lo_kept"], PAIRS * b + 1)
                n0 = H * b
                q_project(n0, 0)
                pe.wait_ge(s["q_kept"], n0 + 1)
                k_project()
                pe.wait_ge(s["k_kept"], PAIRS * b + 1)
                q_project(n0 + 1, 1)
                for t in range(TT):
                    mm = pe.matmul(Y[t][:, :], zero[:, 0:P], zero[:, :], start=True, stop=False)
                for t in range(TT):
                    scores(n0, 0, t, t >= 2)
                pair["no"] = PAIRS * b
                period(n0, 0, 0, True, False)
                period(n0 + 1, 1, 1, True, False)
                with pe.Fori(1, PAIRS - 1) as i:
                    pair["no"] = PAIRS * b + i
                    for e in range(2):
                        period(H * b + 2 * i + e, 2 * i + e, e, False, False)
                for e in range(2):
                    period(n0 + H - 2 + e, H - 2 + e, e, False, True)
                pe.wait_ge(s["o_lo_kept"], n0 + H - 1)
                weigh(n0 + H - 1, 1, range(TT))
                for t in range(TT):
                    output(n0 + H - 2, H - 2, 0, t)
                for t in range(TT):
                    output(n0 + H - 1, H - 1, 1, t, last=True)

        @block.scalar
        def _(act):
            act.wait_ge(s["small_loaded"], 48)
            act.wait_ge(s["zeroed"], 2)
            with act.Fori(0, PAIRS) as i:
                for j in range(2):
                    act.wait_ge(s["wv_turned"], 2 * i + j + 1)
                    act.activation(wvT[:, j, :], TR[:, 0:KVR], ACT.Copy).then_inc(s["wvT_kept"], 1)
                    act.wait_ge(s["wvo_done"], 2 * i + j + 1)
                    act.activation(wvo_hi[:, 2 * i + j, :], M[:, :], ACT.Copy, scale=norm_w[:, 2:3])\
                       .then_inc(s["wvo_hi_kept"], 1)

            def keep_q(n):
                act.wait_ge(s["q_done"], n + 1)
                act.activation(q_raw[:, :], M[:, :], ACT.Copy, scale=A_SCALE).then_inc(s["q_kept"], 1)

            def swap_q(n, e):
                r = P // 2 if e == 0 else 0
                act.wait_ge(s["q_kept"], n + 1)
                act.activation(q_swap[r:r + HALF, :], q_raw[r + HALF:r + ROPE, :], ACT.Copy)
                act.activation(q_swap[r + HALF:r + ROPE, :], q_raw[r:r + HALF, :], ACT.Copy)\
                   .then_inc(s["q_swapped"], 1)

            def keep_k(no):
                act.wait_ge(s["k_done"], no + 1)
                act.activation(k_raw[:, :], M[:, :], ACT.Copy).then_inc(s["k_kept"], 1)

            def keep_o(n, e):
                act.wait_ge(s["pv_done"], n + 1)
                act.activation(o_hi[:, e, :], M[:, :], ACT.Copy).then_inc(s["o_hi_kept"], 1)

            def softmax(n, e, t):
                act.wait_ge(s["max_done"], TT * n + t + 1)
                act.activation(probs[:, t, :], S[t % 2][:, :], ACT.Exp, bias=neg_max[:, e, t:t + 1], scale=1.0,
                               accum_out=total[:, e, t:t + 1]).then_inc(s["exp_done"], 1)

            def keep_turned(n, e, t):
                act.wait_ge(s["turned"], TT * n + t + 1)
                act.activation(pT_hi[:, e, :, t * P:(t + 1) * P], TR[:, :].rearrange("p (k q) -> p k q", k=TT),
                               ACT.Copy).then_inc(s["pT_hi_kept"], 1)

            def period(n, e, first, last):
                for t in range(TT):
                    keep_turned(n, e, t)
                    if t == 1 and not last:
                        swap_q(n + 2, e)
                    if t == 1 and e == 0 and not last:
                        act.wait_ge(s["k_lo_kept"], n + 2)
                        keep_k(pair["no"] + 1)
                    if t == 3 and not (first and e == 0):
                        keep_o(n - 1, 1 - e)
                    if not (last and e == 1):
                        softmax(n + 1, 1 - e, t)
                    if t == 0 and not last:
                        act.wait_ge(s["q_lo_kept"], n + 2)
                        keep_q(n + 2)

            pair = {}
            with act.Fori(0, B) as b:
                for d in range(DT):
                    act.wait_ge(s["xT_done"], DT * b + d + 1)
                    act.activation(xT_hi[:, d, :], Y[d][:, :], ACT.Copy).then_inc(s["xT_hi_kept"], 1)
                for t in range(TT):
                    act.wait_ge(s["qc_kept"], TT * b + t + 1)
                    for j, (o, w) in enumerate(((0, QR), (QR, KVR))):
                        act.activation(sq_junk[:, 0:w], qc[:, t, o:o + w], ACT.Square,
                                       accum_out=ssq[:, j, t:t + 1]).then_inc(s["squared"], 1)
                        act.wait_ge(s["squared"], 2 * TT * b + 2 * t + j + 1)
                for j, w in enumerate((QR, KVR)):
                    act.activation(rms[:, j, :], ssq[:, j, :], ACT.Sqrt, bias=eps_a[:, 0:1], scale=1.0 / w)\
                       .then_inc(s["rooted"], 1)
                act.wait_ge(s["abT_done"], 2 * b + 1)
                act.activation(qaT_hi[:, 0, :], Y[0][:, :], ACT.Copy, scale=norm_w[:, 0:1])\
                   .then_inc(s["abT_hi_kept"], 1)
                act.activation(qaT_hi[0:QR2, 1, :], Y[1][0:QR2, :], ACT.Copy, scale=norm_w[0:QR2, 1:2])\
                   .then_inc(s["abT_hi_kept"], 1)
                act.activation(cT_hi[:, :], Y[2][:, :], ACT.Copy, scale=norm_w[:, 2:3])\
                   .then_inc(s["abT_hi_kept"], 1)
                act.wait_ge(s["abT_done"], 2 * b + 2)
                for e, r in ((0, ROPE), (1, 0)):
                    act.activation(k_hi[r:r + ROPE, e, :], Y[3][r:r + ROPE, :], ACT.Copy)\
                       .then_inc(s["abT_hi_kept"], 1)
                n0 = H * b
                keep_q(n0)
                swap_q(n0, 0)
                keep_k(PAIRS * b)
                act.wait_ge(s["q_lo_kept"], n0 + 1)
                keep_q(n0 + 1)
                swap_q(n0 + 1, 1)
                for t in range(TT):
                    softmax(n0, 0, t)
                pair["no"] = PAIRS * b
                period(n0, 0, True, False)
                period(n0 + 1, 1, True, False)
                with act.Fori(1, PAIRS - 1) as i:
                    pair["no"] = PAIRS * b + i
                    for e in range(2):
                        period(H * b + 2 * i + e, e, False, False)
                for e in range(2):
                    period(n0 + H - 2 + e, e, False, True)
                keep_o(n0 + H - 1, 1)
                act.wait_ge(s["aggregated"], TT * (b + 1))
                act.activation(sd[:, :], mv[:, :, 1], ACT.Sqrt, bias=eps_a[:, 1:2], scale=1.0)\
                   .then_inc(s["sd_done"], 1)

        @block.vector
        def _(dve):
            dve.memset(eps_a[:, 0:1], A_EPS)
            dve.memset(eps_a[:, 1:2], LN_EPS)
            dve.memset(q_raw[:, :], 0.0).then_inc(s["zeroed"], 1)
            dve.wait_ge(s["zeroed"], 1)
            dve.tensor_copy(zero[:, :], q_raw[:, :]).then_inc(s["zeroed"], 1)
            dve.wait_ge(s["wa_loaded"], 16)
            dve.tensor_copy(wa_hi[:, :, :], wa_raw[:, :, :]).then_inc(s["wa_split_hi"], 1)
            dve.wait_ge(s["wa_split_hi"], 1)
            dve.tensor_tensor(wa_lo[:, :, :], wa_raw[:, :, :], f32(wa_hi[:, :, :]), ALU.subtract)\
               .then_inc(s["wa_split_lo"], 1)
            with dve.Fori(0, PAIRS) as i:
                for j in range(2):
                    dve.wait_ge(s["wvo_hi_kept"], 2 * i + j + 1)
                    dve.scalar_tensor_tensor(out=wvo_lo[:, 2 * i + j, :], in0=M[:, :], scalar=norm_w[:, 2:3],
                                             in1=f32(wvo_hi[:, 2 * i + j, :]), op0=ALU.mult, op1=ALU.subtract)\
                       .then_inc(s["wvo_lo_kept"], 1)

            def split_ws(no):
                dve.wait_ge(s["ws_loaded"], 16 * (no + 1))
                dve.tensor_copy(ws_hi[:, :], ws_raw[:, :]).then_inc(s["ws_hi_kept"], 1)

            def split_q(n, e):
                dve.wait_ge(s["q_turned"], n + 1)
                dve.tensor_copy(q_hi[:, e, :], q_rot[:, :]).then_inc(s["q_hi_kept"], 1)

            def split_k(n, e):
                r = e * NOPE
                dve.wait_ge(s["k_kept"], pair["k"] + 1)
                dve.tensor_copy(k_hi[r:r + NOPE, e, :], k_raw[r:r + NOPE, :]).then_inc(s["k_hi_kept"], 1)

            def row_max(n, e, t):
                dve.wait_ge(s["scores_done"], TT * n + t + 1)
                dve.tensor_reduce(neg_max[:, e, t:t + 1], S[t % 2][:, :], AX.X, ALU.max, negate=True)\
                   .then_inc(s["max_done"], 1)

            def normalise(n, e, t):
                dve.wait_ge(s["exp_done"], TT * n + t + 1)
                dve.reciprocal(inv[:, e, t:t + 1], total[:, e, t:t + 1]).then_inc(s["inv_done"], 1)
                dve.wait_ge(s["inv_done"], TT * n + t + 1)
                dve.tensor_scalar(probs[:, t, :], probs[:, t, :], inv[:, e, t:t + 1], None, ALU.mult)\
                   .then_inc(s["probs_done"], 1)

            def keep_turned(n, e, t):
                dve.wait_ge(s["pT_hi_kept"], TT * n + t + 1)
                dve.tensor_tensor(pT_lo[:, e, :, t * P:(t + 1) * P], TR[:, :].rearrange("p (k q) -> p k q", k=TT),
                                  f32(pT_hi[:, e, :, t * P:(t + 1) * P]), ALU.subtract)\
                   .then_inc(s["pT_lo_kept"], 1)

            def keep_o(n, e):
                dve.wait_ge(s["o_hi_kept"], n + 1)
                dve.tensor_tensor(o_lo[:, e, :], M[:, :], f32(o_hi[:, e, :]), ALU.subtract)\
                   .then_inc(s["o_lo_kept"], 1)

            def period(n, e, first, last, more=True):
                for t in range(TT):
                    keep_turned(n, e, t)
                    if not (last and e == 1):
                        row_max(n + 1, 1 - e, t)
                        if t == 2 and not last:
                            pair["k"] = pair["no"] + 1
                            split_k(n + 2, e)
                        if t == 3 and not (first and e == 0):
                            keep_o(n - 1, 1 - e)
                        normalise(n + 1, 1 - e, t)
                    if t == 2 and not last:
                        split_q(n + 2, e)
                    if t == 1 and e == 1 and more:
                        dve.wait_ge(s["q_done"], n + 3)
                        split_ws(pair["no"] + 2)
                    if t == 3 and last and e == 1:
                        keep_o(n - 1, 1 - e)

            pair = {}
            dve.wait_ge(s["small_loaded"], 48)
            with dve.Fori(0, B) as b:
                for d in range(DT):
                    dve.wait_ge(s["xT_hi_kept"], DT * b + d + 1)
                    dve.tensor_tensor(xT_lo[:, d, :], Y[d][:, :], f32(xT_hi[:, d, :]), ALU.subtract)\
                       .then_inc(s["xT_lo_kept"], 1)
                for t in range(TT):
                    dve.wait_ge(s["qc_done"], TT * b + t + 1)
                    dve.tensor_copy(qc[:, t, :], QC[t][:, 0:AW]).then_inc(s["qc_kept"], 1)
                dve.wait_ge(s["rooted"], 2 * b + 2)
                dve.reciprocal(rstd[:, :, :], rms[:, :, :]).then_inc(s["inverted"], 1)
                dve.wait_ge(s["inverted"], b + 1)
                for t in range(TT):
                    for j, (o, w) in enumerate(((0, QR), (QR, KVR))):
                        dve.tensor_scalar(qc[:, t, o:o + w], qc[:, t, o:o + w], rstd[:, j, t:t + 1], None, ALU.mult)\
                           .then_inc(s["scaled"], 1)
                dve.wait_ge(s["scaled"], 2 * TT * (b + 1))
                dve.tensor_copy(c_hi[:, :, :], qc[:, :, QR:QR + KVR]).then_inc(s["c_split"], 1)
                dve.wait_ge(s["c_split"], 2 * b + 1)
                dve.tensor_tensor(c_lo[:, :, :], qc[:, :, QR:QR + KVR], f32(c_hi[:, :, :]), ALU.subtract)\
                   .then_inc(s["c_split"], 1)
                split_ws(PAIRS * b)
                for j, (dst, hi, src, w) in enumerate((
                        (qaT_lo[:, 0, :], qaT_hi[:, 0, :], Y[0][:, :], norm_w[:, 0:1]),
                        (qaT_lo[0:QR2, 1, :], qaT_hi[0:QR2, 1, :], Y[1][0:QR2, :], norm_w[0:QR2, 1:2]),
                        (cT_lo[:, :], cT_hi[:, :], Y[2][:, :], norm_w[:, 2:3]))):
                    dve.wait_ge(s["abT_hi_kept"], 5 * b + j + 1)
                    dve.scalar_tensor_tensor(out=dst, in0=src, scalar=w, in1=f32(hi), op0=ALU.mult,
                                             op1=ALU.subtract).then_inc(s["abT_lo_kept"], 1)
                for e, r in ((0, ROPE), (1, 0)):
                    dve.wait_ge(s["abT_hi_kept"], 5 * b + 4 + e)
                    dve.tensor_tensor(k_lo[r:r + ROPE, e, :], Y[3][r:r + ROPE, :], f32(k_hi[r:r + ROPE, e, :]),
                                      ALU.subtract).then_inc(s["abT_lo_kept"], 1)
                n0 = H * b
                split_q(n0, 0)
                pair["k"] = PAIRS * b
                split_k(n0, 0)
                split_k(n0 + 1, 1)
                split_q(n0 + 1, 1)
                dve.wait_ge(s["q_done"], n0 + 2)
                split_ws(PAIRS * b + 1)
                for t in range(TT):
                    row_max(n0, 0, t)
                    normalise(n0, 0, t)
                pair["no"] = PAIRS * b
                period(n0, 0, True, False)
                period(n0 + 1, 1, True, False)
                with dve.Fori(1, PAIRS - 2) as i:
                    pair["no"] = PAIRS * b + i
                    for e in range(2):
                        period(H * b + 2 * i + e, e, False, False)
                pair["no"] = PAIRS * b + PAIRS - 2
                for e in range(2):
                    period(n0 + H - 4 + e, e, False, False, more=False)
                for e in range(2):
                    period(n0 + H - 2 + e, e, False, True, more=False)
                keep_o(n0 + H - 1, 1)
                for t in range(TT):
                    dve.wait_ge(s["y_done"], (H - 1 + TT) * b + H - 1 + t + 1)
                    dve.tensor_tensor(x1[:, t, :], Y[t][:, :], x_in[:, t, :], ALU.add).then_inc(s["added"], 1)
                    dve.wait_ge(s["added"], TT * b + t + 1)
                    dve.bn_stats(bn[:, t, :], x1[:, t, :]).then_inc(s["bn_done"], 1)
                    dve.wait_ge(s["bn_done"], TT * b + t + 1)
                    dve.memset(rs[:, t:t + 1], 0.0)
                    dve.bn_aggr(mv[:, t, :], bn[:, t, :]).then_inc(s["aggregated"], 1)
                dve.wait_ge(s["sd_done"], b + 1)
                dve.reciprocal(rs[:, :], sd[:, :]).then_inc(s["rs_done"], 1)
                dve.wait_ge(s["rs_done"], b + 1)
                for t in range(TT):
                    dve.tensor_scalar(x1[:, t, :], x1[:, t, :], mv[:, t, 0:1], rs[:, t:t + 1], ALU.subtract,
                                      ALU.mult).then_inc(s["x1_done"], 1)

        @block.gpsimd
        def _(pool):
            pool.wait_ge(s["small_loaded"], 48)

            def split_ws(no):
                pool.wait_ge(s["ws_hi_kept"], no + 1)
                pool.tensor_tensor(ws_lo[:, :], ws_raw[:, :], f32(ws_hi[:, :]), ALU.subtract)\
                    .then_inc(s["ws_lo_kept"], 1)
                pool.wait_ge(s["ws_lo_kept"], no + 1)

            def turn_q(n, e):
                r = P // 2 if e == 0 else 0
                pool.wait_ge(s["q_kept"], n + 1)
                pool.tensor_tensor(q_rot[:, :], q_raw[:, :], tab[:, e, :], ALU.mult).then_inc(s["q_mults"], 1)
                pool.wait_ge(s["q_mults"], 2 * n + 1)
                pool.wait_ge(s["q_swapped"], n + 1)
                pool.tensor_tensor(q_sin[r:r + ROPE, :], q_swap[r:r + ROPE, :], tab[r:r + ROPE, 2, :], ALU.mult)\
                    .then_inc(s["q_mults"], 1)
                pool.wait_ge(s["q_mults"], 2 * n + 2)
                pool.tensor_tensor(q_rot[r:r + ROPE, :], q_rot[r:r + ROPE, :], q_sin[r:r + ROPE, :], ALU.add)\
                    .then_inc(s["q_turned"], 1)
                pool.wait_ge(s["q_turned"], n + 1)

            def split_q(n, e):
                pool.wait_ge(s["q_hi_kept"], n + 1)
                pool.tensor_tensor(q_lo[:, e, :], q_rot[:, :], f32(q_hi[:, e, :]), ALU.subtract)\
                    .then_inc(s["q_lo_kept"], 1)

            def split_k(n, e):
                r = e * NOPE
                pool.wait_ge(s["k_hi_kept"], n + 1)
                pool.tensor_tensor(k_lo[r:r + NOPE, e, :], k_raw[r:r + NOPE, :], f32(k_hi[r:r + NOPE, e, :]),
                                   ALU.subtract).then_inc(s["k_lo_kept"], 1)
                pool.wait_ge(s["k_lo_kept"], n + 1)

            def period(n, e, last, more=True):
                if not last:
                    turn_q(n + 2, e)
                if e == 1 and more:
                    split_ws(pair["no"] + 2)
                if not last:
                    split_k(n + 2, e)
                    split_q(n + 2, e)

            pair = {}
            with pool.Fori(0, B) as b:
                pool.wait_ge(s["qc_kept"], TT * (b + 1))
                k1, k2 = qc[:, :, QR + KVR:QR + KVR + HALF], qc[:, :, QR + KVR + HALF:AW]
                for j, (k, c) in enumerate(((k1, 0), (k2, 1), (k1, 1), (k2, 0))):
                    pool.tensor_tensor(ktmp[:, j, :, :], k, ktab[:, :, c, :], ALU.mult).then_inc(s["k_mults"], 1)
                pool.wait_ge(s["k_mults"], 4 * (b + 1))
                for c in range(2):
                    o = c * ROPE
                    pool.tensor_tensor(kpe[:, :, o:o + HALF], ktmp[:, 0, :, :], ktmp[:, 1, :, :], ALU.subtract)
                    op = pool.tensor_tensor(kpe[:, :, o + HALF:o + ROPE], ktmp[:, 2, :, :], ktmp[:, 3, :, :], ALU.add)
                    op.then_inc(s["k_rot"], 1)
                pool.wait_ge(s["k_rot"], 2 * (b + 1))
                split_ws(PAIRS * b)
                n0 = H * b
                turn_q(n0, 0)
                split_q(n0, 0)
                pool.wait_ge(s["q_lo_kept"], n0 + 1)
                split_k(n0, 0)
                split_k(n0 + 1, 1)
                turn_q(n0 + 1, 1)
                split_q(n0 + 1, 1)
                pool.wait_ge(s["q_lo_kept"], n0 + 2)
                split_ws(PAIRS * b + 1)
                pair["no"] = PAIRS * b
                for e in range(2):
                    period(n0 + e, e, False)
                with pool.Fori(1, PAIRS - 2) as i:
                    pair["no"] = PAIRS * b + i
                    for e in range(2):
                        period(H * b + 2 * i + e, e, False)
                for e in range(2):
                    period(n0 + H - 4 + e, e, False, more=False)


def cross_phase(nc, const, dram):
    ident = const["ident"]
    G = TT + 2
    with ExitStack() as ctx:
        m = Memory(nc, ctx)
        wq_hi, wq_lo = m.split("xwq", [P, DT, D])
        wo_hi, wo_lo = m.split("xwo", [P, DT, D])
        wkv = m.sb("xwkv", [P, CT, 4, D])
        rows = m.sb("xrows", [P, 6, D])
        ln_wb = m.sb("xln_wb", [P, 2, 3, HD])
        masks = m.sb("xmasks", [P, 2])
        kmask = m.sb("kmask", [P, 4])
        vmask = m.sb("vmask", [P, 2, P])
        eps = m.sb("xeps", [P, 2])
        x_in = m.sb("xx_in", [P, TT, D])
        xbo = m.sb("xbo", [P, TT, D])
        ctx_in = m.sb("ctx_in", [KEYS, CD])
        ctxT = m.sb("ctxT", [P, CT, P])
        xT_hi, xT_lo = m.split("xxT", [P, DT, T])
        ln = m.sb("ln", [P, G, D])
        sq = m.sb("sq", [P, G, D])
        stat = m.sb("stat", [P, 4, G * XH])
        v_in = m.sb("v_in", [P, 2, D])
        v_sel = m.sb("v_sel", [P, D])
        v_wide = m.sb("v_wide", [P, DT, 2, P])
        vb_hi, vb_lo = m.split("vb", [P, DT, 2, P])
        kT = m.sb("kT", [P, DT, KEYS])
        kb_hi, kb_lo = m.split("kb", [P, DT, 4, KEYS])
        qT_hi, qT_lo = m.split("xqT", [P, DT, T])
        ex = m.sb("ex", [P, 2, XH, KEYS])
        mx = m.sb("mx", [P, 2, 2, XH])
        sm = m.sb("sm", [P, 2, 2, XH])
        iv = m.sb("iv", [P, 2, 2, XH])
        pT_hi, pT_lo = m.split("xpT", [P, XH // 2, T])
        bn = m.sb("xbn", [P, TT, 6])
        mv = m.sb("xmv", [P, TT, 2])
        sd = m.sb("xsd", [P, TT])
        rs = m.sb("xrs", [P, TT])
        cT_hi, cT_lo = xT_hi, xT_lo
        k_wide = v_wide[:, :, :, :].rearrange("p d a (h k) -> p d (a h) k", k=KEYS)
        x2 = xbo
        groups = ((0, MAIN, 0), (MAIN, KEYS, 1))

        G2 = [ctx.enter_context(nc.psum_tensor(f"G{i}", [P, 2, 512], F32)) for i in range(4)]
        Y = [G2[d // 2][:, d % 2, :] for d in range(4)]
        Z = [G2[2 + d // 2][:, d % 2, :] for d in range(4)]

        s = {n: m.sem("x_" + n) for n in (
            "wq_loaded", "wo_loaded", "small_loaded", "w_hi", "w_lo", "set",
            "x_loaded", "xbo_done", "turned_x", "turned_ctx", "ctx_kept", "hi", "lo", "q_done", "kv_done",
            "biased", "centred", "squared", "stats", "rooted", "scaled", "weighted", "normed",
            "v_steps", "turned_k", "kT_kept", "k_steps", "turned_q", "qT_hi", "qT_lo",
            "scores_done", "max_done", "sub_done", "exp_done", "sum_done", "inv_done", "probs_done",
            "turned_p", "pT_hi", "pT_lo", "ctx_done", "cT_hi", "cT_lo", "out_done", "added", "bn_done",
            "aggregated", "sd_done", "rs_done", "x2_done", "x2_stored")}

        block = ctx.enter_context(nc.Block())

        @block.sync
        def _(sp):
            sp.sem_inc(s["x2_stored"], 16)
            sp.dma_start(ln[:, 0:DT, :], dram["xwq"].rearrange("(k p) n -> p k n", p=P)).then_inc(s["wq_loaded"], 16)
            sp.dma_start(sq[:, 0:DT, :], dram["xwo"].rearrange("(k p) n -> p k n", p=P)).then_inc(s["wo_loaded"], 16)
            x1 = dram["x1"].rearrange("b (t p) d -> b p t d", p=P)
            sp.dma_start(wkv[:, :, :, :], dram["xwkv"].rearrange("(k p) j n -> p k j n", p=P))\
              .then_inc(s["small_loaded"], 16)
            sp.dma_start(rows[:, :, :], dram["xrows"].partition_broadcast(P)).then_inc(s["small_loaded"], 16)
            sp.dma_start(ln_wb[:, :, :, :], dram["xln_wb"].partition_broadcast(P)).then_inc(s["small_loaded"], 16)
            sp.dma_start(masks[:, :], dram["xmasks"]).then_inc(s["small_loaded"], 16)
            sp.dma_start(kmask[:, :], dram["kmask"]).then_inc(s["small_loaded"], 16)
            sp.dma_start(vmask[:, :, :], dram["vmask"]).then_inc(s["small_loaded"], 16)
            sp.dma_start(x_in[:, :, :], x1[0]).then_inc(s["x_loaded"], 16)
            sp.dma_start(ctx_in[:, :], dram["ctx"][0]).then_inc(s["x_loaded"], 16)
            with sp.Fori(0, B - 1) as b:
                sp.wait_ge(s["turned_ctx"], b + 1)
                sp.wait_ge(s["xbo_done"], b + 1)
                sp.dma_start(x_in[:, :, :], x1[b + 1]).then_inc(s["x_loaded"], 16)
                sp.dma_start(ctx_in[:, :], dram["ctx"][b + 1]).then_inc(s["x_loaded"], 16)
                sp.wait_ge(s["x2_done"], TT * (b + 1))
                sp.dma_start(dram["x2"].rearrange("b (t p) d -> b p t d", p=P)[b], x2[:, :, :])\
                  .then_inc(s["x2_stored"], 16)
            sp.wait_ge(s["x2_done"], TT * B)
            sp.dma_start(dram["x2"].rearrange("b (t p) d -> b p t d", p=P)[B - 1], x2[:, :, :])\
              .then_inc(s["x2_stored"], 16)
            sp.wait_ge(s["x2_stored"], 16 * (B + 1))

        @block.tensor
        def _(pe):
            pe.wait_ge(s["w_lo"], 2)
            pe.wait_ge(s["small_loaded"], 96)

            def product(out, pairs):
                steps = [p for lhsT, rhs in pairs for p in three(lhsT, rhs)]
                for j, (lhsT, rhs) in enumerate(steps):
                    mm = pe.matmul(out, lhsT, rhs, start=j == 0, stop=j == len(steps) - 1)
                return mm

            with pe.Fori(0, B) as b:
                pe.wait_ge(s["added"], TT * (b + 1))
                pe.wait_ge(s["x_loaded"], 32 * (b + 1))
                for d in range(DT):
                    for t in range(TT):
                        mm = pe.transpose(Y[d][:, t * P:(t + 1) * P], x_in[:, t, d * P:(d + 1) * P], ident[:, :])
                    mm.then_inc(s["turned_x"], 1)
                for k in range(CT):
                    mm = pe.transpose(Z[0][:, k * KEYS:(k + 1) * KEYS], ctx_in[:, k * P:(k + 1) * P],
                                      ident[0:KEYS, 0:KEYS])
                mm.then_inc(s["turned_ctx"], 1)
                pe.wait_ge(s["ctx_kept"], b + 1)
                pe.wait_ge(s["lo"], DT * (b + 1))
                for j in range(4):
                    for k in range(CT):
                        mm = pe.matmul(Y[j], ctxT[:, k, :], wkv[:, k, j, :], start=k == 0, stop=k == CT - 1)
                    mm.then_inc(s["kv_done"], 1)
                for t in range(TT):
                    product(Z[t], [((xT_hi[:, d, t * P:(t + 1) * P], xT_lo[:, d, t * P:(t + 1) * P]),
                                    (wq_hi[:, d, :], wq_lo[:, d, :])) for d in range(DT)]).then_inc(s["q_done"], 1)
                pe.wait_ge(s["normed"], 3 * (b + 1))
                for d in range(DT):
                    for t in range(TT):
                        mm = pe.transpose(Z[d][:, t * P:(t + 1) * P], ln[:, t, d * P:(d + 1) * P], ident[:, :])
                    mm.then_inc(s["turned_q"], 1)
                    if d:
                        continue
                    for k in range(DT):
                        for g in range(2):
                            mm = pe.transpose(Y[0][:, (2 * k + g) * KEYS:(2 * k + g + 1) * KEYS],
                                              ln[0:KEYS, TT + g, k * P:(k + 1) * P], ident[0:KEYS, 0:KEYS])
                    mm.then_inc(s["turned_k"], 1)

                def turn_probs(t):
                    pe.wait_ge(s["probs_done"], 2 * TT * b + 2 * t + 2)
                    if t >= 2:
                        pe.wait_ge(s["pT_lo"], TT * b + t - 1)
                    for h2 in range(XH // 2):
                        mm = pe.transpose(
                            G2[2 + t % 2][:, h2 // 4, (h2 % 4) * P:(h2 % 4 + 1) * P],
                            ex[:, t % 2, 2 * h2:2 * h2 + 2, :].rearrange("p h k -> p (h k)"), ident[:, :])
                    mm.then_inc(s["turned_p"], 1)

                pe.wait_ge(s["k_steps"], 3 * (b + 1))
                pe.wait_ge(s["qT_lo"], DT * (b + 1))
                for t in range(TT):
                    if t >= 2:
                        pe.wait_ge(s["sub_done"], 2 * TT * b + 2 * (t - 1))
                    for d in range(DT):
                        mm = product(G2[t % 2][:, d // 2, (d % 2) * 4 * KEYS:(d % 2 + 1) * 4 * KEYS],
                                     [((qT_hi[:, d, t * P:(t + 1) * P], qT_lo[:, d, t * P:(t + 1) * P]),
                                       (kb_hi[:, d, :, :].rearrange("p h k -> p (h k)"),
                                        kb_lo[:, d, :, :].rearrange("p h k -> p (h k)")))])
                    mm.then_inc(s["scores_done"], 1)
                    if t >= 1:
                        turn_probs(t - 1)
                turn_probs(TT - 1)
                pe.wait_ge(s["pT_lo"], TT * (b + 1))
                for d in range(DT):
                    product(Y[d], [((vb_hi[:, d, j, :], vb_lo[:, d, j, :]),
                                    (pT_hi[:, 2 * d + j, :], pT_lo[:, 2 * d + j, :])) for j in range(2)])\
                        .then_inc(s["ctx_done"], 1)
                pe.wait_ge(s["cT_lo"], DT * (b + 1))
                for t in range(TT):
                    product(Z[t], [((cT_hi[:, d, t * P:(t + 1) * P], cT_lo[:, d, t * P:(t + 1) * P]),
                                    (wo_hi[:, d, :], wo_lo[:, d, :])) for d in range(DT)]).then_inc(s["out_done"], 1)

        @block.scalar
        def _(act):
            act.wait_ge(s["wq_loaded"], 16)
            act.activation(wq_hi[:, :, :], ln[:, 0:DT, :], ACT.Copy).then_inc(s["w_hi"], 1)
            act.wait_ge(s["wo_loaded"], 16)
            act.activation(wo_hi[:, :, :], sq[:, 0:DT, :], ACT.Copy).then_inc(s["w_hi"], 1)
            act.wait_ge(s["set"], 1)
            act.wait_ge(s["w_lo"], 2)
            with act.Fori(0, B) as b:
                for d in range(DT):
                    act.wait_ge(s["turned_x"], DT * b + d + 1)
                    act.activation(xT_hi[:, d, :], Y[d], ACT.Copy).then_inc(s["hi"], 1)
                act.wait_ge(s["turned_ctx"], b + 1)
                for c in range(2):
                    op = act.activation(ctxT[:, :, c * KEYS:(c + 1) * KEYS],
                                        Z[0][:, 0:CT * KEYS].rearrange("p (k n) -> p k n", n=KEYS), ACT.Copy)
                op.then_inc(s["ctx_kept"], 1)
                act.wait_ge(s["centred"], b + 1)
                act.activation(sq[:, :, :], ln[:, :, :], ACT.Square).then_inc(s["squared"], 1)
                act.wait_ge(s["stats"], 3 * b + 3)
                act.activation(stat[:, 2, :], stat[:, 1, :], ACT.Sqrt, bias=eps[:, 0:1], scale=1.0 / HD)\
                   .then_inc(s["rooted"], 1)
                act.wait_ge(s["turned_k"], b + 1)
                for o, e, g in groups:
                    op = act.activation(kT[:, :, o:e],
                                        Y[0].rearrange("p (d g k) -> p d g k", g=2, k=KEYS)[:, :, g, o:e], ACT.Copy)
                op.then_inc(s["kT_kept"], 1)
                for d in range(DT):
                    act.wait_ge(s["turned_q"], DT * b + d + 1)
                    act.activation(qT_hi[:, d, :], Z[d], ACT.Copy).then_inc(s["qT_hi"], 1)

                def keep_turned(t):
                    act.wait_ge(s["turned_p"], TT * b + t + 1)
                    act.activation(pT_hi[:, :, t * P:(t + 1) * P],
                                   G2[2 + t % 2][:, :, :].rearrange("p a (h q) -> p (a h) q", q=P), ACT.Copy)\
                       .then_inc(s["pT_hi"], 1)

                for t in range(TT):
                    act.wait_ge(s["sub_done"], 2 * TT * b + 2 * t + 2)
                    act.activation(ex[:, t % 2, :, :], ex[:, t % 2, :, :], ACT.Exp, scale=X_SCALE)\
                       .then_inc(s["exp_done"], 1)
                    if t >= 1:
                        keep_turned(t - 1)
                keep_turned(TT - 1)
                for d in range(DT):
                    act.wait_ge(s["ctx_done"], DT * b + d + 1)
                    act.activation(cT_hi[:, d, :], Y[d], ACT.Copy).then_inc(s["cT_hi"], 1)
                act.wait_ge(s["aggregated"], TT * (b + 1))
                act.activation(sd[:, :], mv[:, :, 1], ACT.Sqrt, bias=eps[:, 1:2], scale=1.0).then_inc(s["sd_done"], 1)

        @block.vector
        def _(dve):
            dve.sem_inc(s["added"], TT)
            dve.memset(eps[:, 0:1], X_EPS)
            dve.memset(eps[:, 1:2], LN_EPS).then_inc(s["set"], 1)
            dve.wait_ge(s["w_hi"], 1)
            dve.tensor_tensor(wq_lo[:, :, :], ln[:, 0:DT, :], f32(wq_hi[:, :, :]), ALU.subtract).then_inc(s["w_lo"], 1)
            dve.wait_ge(s["w_hi"], 2)
            dve.tensor_tensor(wo_lo[:, :, :], sq[:, 0:DT, :], f32(wo_hi[:, :, :]), ALU.subtract).then_inc(s["w_lo"], 1)
            dve.wait_ge(s["small_loaded"], 96)
            dve.wait_ge(s["w_lo"], 2)

            def heads(ap):
                return ap.rearrange("p g (h d) -> p (g h) d", d=HD)

            def wide(ap, n):
                return ap.unsqueeze(2).to_broadcast([P, ap.shape[1], n])

            with dve.Fori(0, B) as b:
                for d in range(DT):
                    dve.wait_ge(s["hi"], DT * b + d + 1)
                    dve.tensor_tensor(xT_lo[:, d, :], Y[d], f32(xT_hi[:, d, :]), ALU.subtract).then_inc(s["lo"], 1)
                for j in range(4):
                    dst = ln[:, TT + j, :] if j < 2 else v_in[:, j - 2, :]
                    dve.wait_ge(s["kv_done"], 4 * b + j + 1)
                    dve.tensor_tensor(dst, Y[j], rows[:, 1 + j, :], ALU.add).then_inc(s["biased"], 1)
                for t in range(TT):
                    dve.wait_ge(s["q_done"], TT * b + t + 1)
                    dve.tensor_tensor(ln[:, t, :], Z[t], rows[:, 0, :], ALU.add).then_inc(s["biased"], 1)
                dve.wait_ge(s["biased"], 8 * (b + 1))
                dve.tensor_reduce(stat[:, 0, :], heads(ln[:, :, :]), AX.X, ALU.add).then_inc(s["stats"], 1)
                dve.wait_ge(s["stats"], 3 * b + 1)
                dve.tensor_scalar(stat[:, 0, :], stat[:, 0, :], 1.0 / HD, None, ALU.mult).then_inc(s["stats"], 1)
                dve.wait_ge(s["stats"], 3 * b + 2)
                dve.tensor_tensor(heads(ln[:, :, :]), heads(ln[:, :, :]), wide(stat[:, 0, :], HD), ALU.subtract)\
                   .then_inc(s["centred"], 1)
                dve.tensor_scalar(v_sel[:, :], v_in[:, 0, :], masks[:, 0:1], None, ALU.mult).then_inc(s["v_steps"], 1)
                dve.wait_ge(s["v_steps"], 5 * b + 1)
                dve.scalar_tensor_tensor(out=v_sel[:, :], in0=v_in[:, 1, :], scalar=masks[:, 1:2], in1=v_sel[:, :],
                                         op0=ALU.mult, op1=ALU.add).then_inc(s["v_steps"], 1)
                dve.wait_ge(s["v_steps"], 5 * b + 2)
                dve.tensor_tensor(
                    v_wide[:, :, :, :],
                    v_sel[:, :].rearrange("p (d c) -> p d c", d=DT).unsqueeze(2).to_broadcast([P, DT, 2, P]),
                    vmask[:, :, :].unsqueeze(1).to_broadcast([P, DT, 2, P]), ALU.mult).then_inc(s["v_steps"], 1)
                dve.wait_ge(s["v_steps"], 5 * b + 3)
                dve.tensor_copy(vb_hi[:, :, :, :], v_wide[:, :, :, :]).then_inc(s["v_steps"], 1)
                dve.wait_ge(s["v_steps"], 5 * b + 4)
                dve.tensor_tensor(vb_lo[:, :, :, :], v_wide[:, :, :, :], f32(vb_hi[:, :, :, :]), ALU.subtract)\
                   .then_inc(s["v_steps"], 1)
                dve.wait_ge(s["squared"], b + 1)
                dve.tensor_reduce(stat[:, 1, :], heads(sq[:, :, :]), AX.X, ALU.add).then_inc(s["stats"], 1)
                dve.wait_ge(s["rooted"], b + 1)
                dve.reciprocal(stat[:, 3, :], stat[:, 2, :]).then_inc(s["scaled"], 1)
                dve.wait_ge(s["scaled"], 2 * b + 1)
                dve.tensor_tensor(heads(ln[:, :, :]), heads(ln[:, :, :]), wide(stat[:, 3, :], HD), ALU.mult)\
                   .then_inc(s["scaled"], 1)
                dve.wait_ge(s["kT_kept"], b + 1)
                dve.wait_ge(s["v_steps"], 5 * b + 5)
                dve.tensor_tensor(k_wide[:, :, :, :], kT[:, :, :].unsqueeze(2).to_broadcast([P, DT, 4, KEYS]),
                                  kmask[:, :].unsqueeze(1).unsqueeze(3).to_broadcast([P, DT, 4, KEYS]), ALU.mult)\
                   .then_inc(s["k_steps"], 1)
                dve.wait_ge(s["k_steps"], 3 * b + 1)
                dve.tensor_copy(kb_hi[:, :, :, :], k_wide[:, :, :, :]).then_inc(s["k_steps"], 1)
                dve.wait_ge(s["k_steps"], 3 * b + 2)
                dve.tensor_tensor(kb_lo[:, :, :, :], k_wide[:, :, :, :], f32(kb_hi[:, :, :, :]), ALU.subtract)\
                   .then_inc(s["k_steps"], 1)
                for d in range(DT):
                    dve.wait_ge(s["qT_hi"], DT * b + d + 1)
                    dve.tensor_tensor(qT_lo[:, d, :], Z[d], f32(qT_hi[:, d, :]), ALU.subtract).then_inc(s["qT_lo"], 1)

                def keep_turned(t):
                    dve.wait_ge(s["pT_hi"], TT * b + t + 1)
                    dve.tensor_tensor(pT_lo[:, :, t * P:(t + 1) * P],
                                      G2[2 + t % 2][:, :, :].rearrange("p a (h q) -> p (a h) q", q=P),
                                      f32(pT_hi[:, :, t * P:(t + 1) * P]), ALU.subtract).then_inc(s["pT_lo"], 1)

                for t in range(TT):
                    scores = G2[t % 2][:, :, :].rearrange("p a (h k) -> p (a h) k", k=KEYS)
                    dve.wait_ge(s["scores_done"], TT * b + t + 1)
                    if t >= 2:
                        dve.wait_ge(s["turned_p"], TT * b + t - 1)
                    for o, e, g in groups:
                        dve.tensor_reduce(mx[:, t % 2, g, :], scores[:, :, o:e], AX.X, ALU.max)\
                           .then_inc(s["max_done"], 1)
                    dve.wait_ge(s["max_done"], 2 * TT * b + 2 * t + 2)
                    for o, e, g in groups:
                        dve.tensor_tensor(ex[:, t % 2, :, o:e], scores[:, :, o:e], wide(mx[:, t % 2, g, :], e - o),
                                          ALU.subtract).then_inc(s["sub_done"], 1)
                    dve.wait_ge(s["exp_done"], TT * b + t + 1)
                    for o, e, g in groups:
                        dve.tensor_reduce(sm[:, t % 2, g, :], ex[:, t % 2, :, o:e], AX.X, ALU.add)\
                           .then_inc(s["sum_done"], 1)
                    dve.wait_ge(s["sum_done"], 2 * TT * b + 2 * t + 2)
                    dve.reciprocal(iv[:, t % 2, :, :], sm[:, t % 2, :, :]).then_inc(s["inv_done"], 1)
                    if t >= 1:
                        keep_turned(t - 1)
                keep_turned(TT - 1)
                for d in range(DT):
                    dve.wait_ge(s["cT_hi"], DT * b + d + 1)
                    dve.tensor_tensor(cT_lo[:, d, :], Y[d], f32(cT_hi[:, d, :]), ALU.subtract).then_inc(s["cT_lo"], 1)
                for t in range(TT):
                    dve.wait_ge(s["out_done"], TT * b + t + 1)
                    dve.tensor_tensor(x2[:, t, :], Z[t], xbo[:, t, :], ALU.add).then_inc(s["added"], 1)
                    dve.wait_ge(s["added"], TT * (b + 1) + t + 1)
                    dve.bn_stats(bn[:, t, :], x2[:, t, :]).then_inc(s["bn_done"], 1)
                    dve.wait_ge(s["bn_done"], TT * b + t + 1)
                    dve.memset(rs[:, t:t + 1], 0.0)
                    dve.bn_aggr(mv[:, t, :], bn[:, t, :]).then_inc(s["aggregated"], 1)
                dve.wait_ge(s["sd_done"], b + 1)
                dve.reciprocal(rs[:, :], sd[:, :]).then_inc(s["rs_done"], 1)
                dve.wait_ge(s["rs_done"], b + 1)
                for t in range(TT):
                    dve.tensor_scalar(x2[:, t, :], x2[:, t, :], mv[:, t, 0:1], rs[:, t:t + 1], ALU.subtract,
                                      ALU.mult).then_inc(s["x2_done"], 1)

        @block.gpsimd
        def _(pool):
            pool.wait_ge(s["small_loaded"], 96)
            with pool.Fori(0, B) as b:
                pool.wait_ge(s["x_loaded"], 32 * (b + 1))
                pool.wait_ge(s["x2_stored"], 16 * (b + 1))
                pool.tensor_tensor(xbo[:, :, :], x_in[:, :, :], rows[:, 5:6, :].to_broadcast([P, TT, D]), ALU.add)\
                    .then_inc(s["xbo_done"], 1)
                parts = [(ln[:, 0:TT, :].rearrange("p g (h d) -> p (g h) d", d=HD), TT * XH, 0),
                         (ln[:, TT, :].rearrange("p (h d) -> p h d", d=HD), XH, 1),
                         (ln[:, TT + 1, :].rearrange("p (h d) -> p h d", d=HD), XH, 2)]
                pool.wait_ge(s["scaled"], 2 * b + 2)
                for part, n, c in parts:
                    pool.tensor_tensor(part, part, ln_wb[:, 0, c:c + 1, :].to_broadcast([P, n, HD]), ALU.mult)\
                        .then_inc(s["weighted"], 1)
                pool.wait_ge(s["weighted"], 3 * (b + 1))
                for part, n, c in parts:
                    pool.tensor_tensor(part, part, ln_wb[:, 1, c:c + 1, :].to_broadcast([P, n, HD]), ALU.add)\
                        .then_inc(s["normed"], 1)
                for t in range(TT):
                    pool.wait_ge(s["inv_done"], TT * b + t + 1)
                    for o, e, g in groups:
                        pool.tensor_tensor(ex[:, t % 2, :, o:e], ex[:, t % 2, :, o:e],
                                           iv[:, t % 2, g, :].unsqueeze(2).to_broadcast([P, XH, e - o]), ALU.mult)\
                            .then_inc(s["probs_done"], 1)


def ffn_phase(nc, const, dram):
    ident = const["ident"]
    with ExitStack() as ctx:
        m = Memory(nc, ctx)
        acc = m.sb("acc", [P, B * TT, D])
        xT_hi, xT_lo = m.split("fxT", [P, DT, B * T])
        gu_raw = m.sb("gu_raw", [P, DT, 2 * EH])
        gu_hi, gu_lo = m.split("gu", [P, 2, DT, 2 * EH])
        dn_raw = m.sb("dn_raw", [P, HT, D])
        dn_hi, dn_lo = m.split("dn", [P, 2, HT, D])
        silu = m.sb("silu", [P, HT, T])
        h = m.sb("h", [P, HT, T])
        h_hi, h_lo = m.split("fh", [P, 2, HT, T])
        bias_raw = m.sb("bias_raw", [P, 2, HT])
        bias = m.sb("bias", [P, 2, 2, HT])
        wg_raw = m.sb("wg_raw", [P, DT, NG])
        wg_hi, wg_lo = m.split("wg", [P, DT, NG])
        bg = m.sb("bg", [P, NG])
        before = m.sb("before", [P, NG, NG])
        gate = m.sb("gate", [P, B * TT, NG])
        keep = m.sb("keep", [P, B * TT, NG])
        row = m.sb("row", [P, 3, B * TT])
        w = m.sb("w", [P, B * TT, NG])
        w3 = m.sb("w3", [P, B * TT, QUAD])
        w_hi = m.sb("w_hi", [P, B * TT, NG], F32R)
        quads = m.sb("quads", [P, 4])
        bd_raw = m.sb("bd_raw", [P, D])
        bd_hi = m.sb("bd_hi", [P, D], F32R)
        bd_mask = m.sb("bd_mask", [P, 2])
        bd3 = m.sb("bd3", [P, D], F32R)
        wT3 = m.sb("wT3", [P, B * TT, P], F32R)
        eps = m.sb("feps", [P, 1])
        bn = m.sb("fbn", [P, B * TT, 6])
        mv = m.sb("fmv", [P, B * TT, 2])
        sd = m.sb("fsd", [P, B * TT])
        rs = m.sb("frs", [P, B * TT])
        pairs = h[:, :, :].rearrange("p a (n i j) -> p (a n) i j", i=NG, j=NG)
        ties = silu[:, :, :].rearrange("p a (n i j) -> p (a n) i j", i=NG, j=NG)
        w_wide = h[:, :, :].rearrange("p a (n q r) -> p (a n) q r", q=4, r=QUAD)
        w_turned = silu[:, :, :].rearrange("p a (n c) -> p (a n) c", c=P)

        GU = m.banks("GU", 4)
        DN = m.banks("DN", TT)

        s = {n: m.sem("f_" + n) for n in (
            "x_loaded0", "x_loaded1", "x_loaded2", "x_loaded3", "small_loaded", "gu_loaded", "dn_loaded", "set",
            "turned_x", "xT_hi", "xT_lo", "wg_split", "gate_done", "route", "routed", "bd_steps", "wide_steps",
            "gu_hi", "gu_lo", "dn_hi", "dn_lo",
            "gate_up_done", "silu_done", "h_done", "h_hi", "h_lo", "down_done", "acc_done",
            "bn_done", "aggregated", "sd_done", "rs_done", "out_done", "stored")}

        EXPERTS = N_EXP - 2
        block = ctx.enter_context(nc.Block())

        @block.sync
        def _(sp):
            x2 = dram["x2"].rearrange("b (t p) d -> b p t d", p=P)
            for c in range(B):
                sp.dma_start(acc[:, c * TT:(c + 1) * TT, :], x2[c]).then_inc(s[f"x_loaded{c}"], 16)
            for dst, name in ((wg_raw[:, :, :], "wg"), (quads[:, :], "quads"),
                              (bd_raw[:, :], "bd"), (bd_mask[:, :], "bd_mask")):
                src = dram[name].rearrange("(k p) n -> p k n", p=P) if name == "wg" else dram[name]
                sp.dma_start(dst, src).then_inc(s["small_loaded"], 16)
            sp.dma_start(bg[:, :], dram["bg"].partition_broadcast(P)).then_inc(s["small_loaded"], 16)
            sp.dma_start(before[:, :, :], dram["before"].partition_broadcast(P)).then_inc(s["small_loaded"], 16)

            def load(k, gu, dn, width=2 * EH):
                sp.dma_start(bias_raw[:, :, :], dram["fbias"][k]).then_inc(s["gu_loaded"], 16)
                sp.dma_start(gu_raw[:, :, 0:width], gu.rearrange("(k p) n -> p k n", p=P)).then_inc(s["gu_loaded"], 16)
                sp.dma_start(dn_raw[:, :, :], dn.rearrange("(k p) n -> p k n", p=P)).then_inc(s["dn_loaded"], 16)

            load(0, dram["wgu"][0], dram["wdn"][0])
            with sp.Fori(1, EXPERTS) as k:
                sp.wait_ge(s["gu_lo"], k)
                sp.wait_ge(s["dn_lo"], k)
                load(k, dram["wgu"][k], dram["wdn"][k])
            for j in range(2):
                sp.wait_ge(s["gu_lo"], EXPERTS + j)
                sp.wait_ge(s["dn_lo"], EXPERTS + j)
                load(EXPERTS + j, dram["wsu"][j], dram["wsd"][j], EH)
            for c in range(B):
                sp.wait_ge(s["out_done"], TT * (c + 1))
                sp.dma_start(dram["out"][c].rearrange("(t p) d -> p t d", p=P), acc[:, c * TT:(c + 1) * TT, :])\
                  .then_inc(s["stored"], 16)
            sp.wait_ge(s["stored"], 16 * B)

        @block.tensor
        def _(pe):
            def turn_x(c):
                pe.wait_ge(s[f"x_loaded{c}"], 16)
                for d in range(DT):
                    if c:
                        pe.wait_ge(s["xT_lo"], DT * (c - 1) + d + 1)
                    for t in range(TT):
                        mm = pe.transpose(GU[d][:, t * P:(t + 1) * P], acc[:, c * TT + t, d * P:(d + 1) * P],
                                          ident[:, :])
                    mm.then_inc(s["turned_x"], 1)

            def logits(c):
                pe.wait_ge(s["xT_lo"], DT * (c + 1))
                for n in range(c * TT, (c + 1) * TT):
                    for d in range(DT):
                        for j, (lhsT, rhs) in enumerate(three(
                                (xT_hi[:, d, n * P:(n + 1) * P], xT_lo[:, d, n * P:(n + 1) * P]),
                                (wg_hi[:, d, :], wg_lo[:, d, :]))):
                            mm = pe.matmul(DN[0][:, n * NG:(n + 1) * NG], lhsT, rhs, start=d == 0 and j == 0,
                                           stop=d == DT - 1 and j == 2)
                mm.then_inc(s["gate_done"], 1)

            pe.wait_ge(s["wg_split"], 2)
            for c in range(B):
                turn_x(c)
                if c:
                    logits(c - 1)
            logits(B - 1)

            def gate_up(n, k, j, c, a, shared, first=False):
                if c == 0 and a == 0:
                    pe.wait_ge(s["gu_lo"], k + 1)
                if not first:
                    pe.wait_ge(s["silu_done"], 2 * n + a - 1)
                    if not shared:
                        pe.wait_ge(s["h_done"], 2 * n + a - 1)
                for u in range(1 if shared else 2):
                    o = u * EH + a * P
                    steps = [p for d in range(DT) for p in three(
                        (gu_hi[:, j, d, o:o + P], gu_lo[:, j, d, o:o + P]),
                        (xT_hi[:, d, c * T:(c + 1) * T], xT_lo[:, d, c * T:(c + 1) * T]))]
                    for i, (lhsT, rhs) in enumerate(steps):
                        mm = pe.matmul(GU[2 * a + u][:, :], lhsT, rhs, start=i == 0, stop=i == len(steps) - 1)
                mm.then_inc(s["gate_up_done"], 1)

            def down(n, k, j, c, t, bias=False, first=False):
                if t == 0:
                    pe.wait_ge(s["h_lo"], 2 * n + 2)
                    if c == 0:
                        pe.wait_ge(s["dn_lo"], k + 1)
                if not first:
                    pe.wait_ge(s["acc_done"], TT * (n - 1) + t + 1)
                elif t == 0:
                    pe.wait_ge(s["route"], 1)
                steps = [p for a in range(HT) for p in three(
                    (h_hi[:, c % 2, a, t * P:(t + 1) * P], h_lo[:, c % 2, a, t * P:(t + 1) * P]),
                    (dn_hi[:, j, a, :], dn_lo[:, j, a, :]))]
                if bias:
                    steps.append((wT3[:, c * TT + t, :], bd3[:, :]))
                for i, (lhsT, rhs) in enumerate(steps):
                    mm = pe.matmul(DN[t][:, :], lhsT, rhs, start=i == 0, stop=i == len(steps) - 1)
                mm.then_inc(s["down_done"], 1)

            def steps(n0, k0, shared, next_shared, first=False, last=False):
                for j in range(2):
                    for c in range(B):
                        n = n0 + j * B + c
                        end = j == 1 and c == B - 1
                        nj, nc_ = (j, c + 1) if c < B - 1 else (1 - j, 0)
                        nk = k0 + j + (c == B - 1)
                        for a in range(HT):
                            if not (last and end):
                                gate_up(n + 1, nk, nj, nc_, a, next_shared if end else shared)
                            for t in (2 * a, 2 * a + 1):
                                down(n, k0 + j, j, c, t, bias=shared and j == 1, first=first and j == 0 and c == 0)

            for a in range(HT):
                gate_up(0, 0, 0, 0, a, False, first=True)
            steps(0, 0, False, False, first=True)
            with pe.Fori(1, EXPERTS // 2 - 1) as i:
                steps(2 * B * i, 2 * i, False, False)
            steps(2 * B * (EXPERTS // 2 - 1), EXPERTS - 2, False, True)
            pe.wait_ge(s["wide_steps"], 8)
            steps(B * EXPERTS, EXPERTS, True, True, last=True)

        @block.scalar
        def _(act):
            for n in range(B * DT):
                act.wait_ge(s["turned_x"], n + 1)
                c, d = divmod(n, DT)
                act.activation(xT_hi[:, d, c * T:(c + 1) * T], GU[d][:, :], ACT.Copy).then_inc(s["xT_hi"], 1)
            act.wait_ge(s["route"], 6)
            act.activation(w[:, :, :], gate[:, :, :], ACT.Exp).then_inc(s["routed"], 1)
            act.wait_ge(s["small_loaded"], 16 * 6)
            act.wait_ge(s["wide_steps"], 8)

            def hidden(n, j, a, shared, first=False):
                act.wait_ge(s["gate_up_done"], 2 * n + a + 1)
                if shared:
                    act.wait_ge(s["h_lo"], 2 * n + a - 1)
                dst = h if shared else silu
                act.activation(dst[:, a, :], GU[2 * a][:, :], ACT.Silu, bias=bias[:, j, 0, a:a + 1], scale=1.0)\
                   .then_inc(s["silu_done"], 1)

            def finish(c):
                act.wait_ge(s["aggregated"], TT * (c + 1))
                act.activation(sd[:, c * TT:(c + 1) * TT], mv[:, c * TT:(c + 1) * TT, 1], ACT.Sqrt,
                               bias=eps[:, 0:1], scale=1.0).then_inc(s["sd_done"], 1)

            def steps(n0, k0, shared, next_shared, last=False):
                for j in range(2):
                    for c in range(B):
                        end = j == 1 and c == B - 1
                        for a in range(0 if last and end else HT):
                            hidden(n0 + j * B + c + 1, j if c < B - 1 else 1 - j, a, next_shared if end else shared)
                        if last and j == 1:
                            finish(c)

            for a in range(HT):
                hidden(0, 0, a, False)
            with act.Fori(0, EXPERTS // 2 - 1) as i:
                steps(2 * B * i, 2 * i, False, False)
            steps(2 * B * (EXPERTS // 2 - 1), EXPERTS - 2, False, True)
            steps(B * EXPERTS, EXPERTS, True, True, last=True)

        @block.vector
        def _(dve):
            dve.memset(eps[:, :], LN_EPS).then_inc(s["set"], 1)
            dve.memset(w3[:, :, :], 0.0).then_inc(s["set"], 1)
            dve.wait_ge(s["small_loaded"], 16 * 6)
            dve.tensor_copy(wg_hi[:, :, :], wg_raw[:, :, :]).then_inc(s["wg_split"], 1)
            dve.wait_ge(s["wg_split"], 1)
            dve.tensor_tensor(wg_lo[:, :, :], wg_raw[:, :, :], f32(wg_hi[:, :, :]), ALU.subtract)\
               .then_inc(s["wg_split"], 1)

            def split_gu(k, j, width=2 * EH):
                dve.wait_ge(s["gu_loaded"], 32 * (k + 1))
                dve.tensor_copy(bias[:, j, :, :], bias_raw[:, :, :])
                dve.tensor_copy(gu_hi[:, j, :, 0:width], gu_raw[:, :, 0:width]).then_inc(s["gu_hi"], 1)

            def split_dn(k, j):
                dve.wait_ge(s["dn_loaded"], 16 * (k + 1))
                dve.tensor_copy(dn_hi[:, j, :, :], dn_raw[:, :, :]).then_inc(s["dn_hi"], 1)

            split_gu(0, 0)
            split_dn(0, 0)
            for n in range(B * DT):
                dve.wait_ge(s["xT_hi"], n + 1)
                c, d = divmod(n, DT)
                dve.tensor_tensor(xT_lo[:, d, c * T:(c + 1) * T], GU[d][:, :], f32(xT_hi[:, d, c * T:(c + 1) * T]),
                                  ALU.subtract).then_inc(s["xT_lo"], 1)

            N = B * TT
            cube = [P, N, NG, NG]
            dve.wait_ge(s["gate_done"], B)
            dve.tensor_tensor(gate[:, :, :], DN[0][:, 0:N * NG].rearrange("p (n e) -> p n e", e=NG),
                              bg[:, :].unsqueeze(1).to_broadcast([P, N, NG]), ALU.add).then_inc(s["route"], 1)
            dve.wait_ge(s["route"], 1)
            other, own = gate[:, :, :].unsqueeze(2).to_broadcast(cube), gate[:, :, :].unsqueeze(3).to_broadcast(cube)
            dve.tensor_tensor(pairs[:, :, :, :], other, own, ALU.is_gt).then_inc(s["route"], 1)
            dve.tensor_tensor(ties[:, :, :, :], other, own, ALU.is_equal).then_inc(s["route"], 1)
            dve.tensor_reduce(row[:, 0, :], gate[:, :, :], AX.X, ALU.max).then_inc(s["route"], 1)
            dve.wait_ge(s["route"], 4)
            dve.tensor_tensor(ties[:, :, :, :], ties[:, :, :, :], before[:, :, :].unsqueeze(1).to_broadcast(cube),
                              ALU.mult).then_inc(s["route"], 1)
            dve.tensor_tensor(gate[:, :, :], gate[:, :, :], row[:, 0, :].unsqueeze(2).to_broadcast([P, N, NG]),
                              ALU.subtract).then_inc(s["route"], 1)
            dve.wait_ge(s["route"], 5)
            dve.tensor_tensor(pairs[:, :, :, :], pairs[:, :, :, :], ties[:, :, :, :], ALU.add).then_inc(s["route"], 1)
            dve.wait_ge(s["route"], 7)
            dve.tensor_reduce(keep[:, :, :], pairs[:, :, :, :], AX.X, ALU.add).then_inc(s["route"], 1)
            dve.wait_ge(s["route"], 8)
            dve.tensor_scalar(keep[:, :, :], keep[:, :, :], TOP - 0.5, None, ALU.is_lt).then_inc(s["route"], 1)
            dve.wait_ge(s["route"], 9)
            dve.wait_ge(s["routed"], 1)
            dve.tensor_tensor(w[:, :, :], w[:, :, :], keep[:, :, :], ALU.mult).then_inc(s["route"], 1)
            dve.wait_ge(s["route"], 10)
            dve.tensor_reduce(row[:, 1, :], w[:, :, :], AX.X, ALU.add).then_inc(s["route"], 1)
            dve.wait_ge(s["route"], 11)
            dve.reciprocal(row[:, 2, :], row[:, 1, :]).then_inc(s["route"], 1)
            dve.wait_ge(s["route"], 12)
            dve.tensor_tensor(w[:, :, :], w[:, :, :], row[:, 2, :].unsqueeze(2).to_broadcast([P, N, NG]), ALU.mult)\
               .then_inc(s["route"], 1)
            dve.wait_ge(s["route"], 13)
            dve.memset(w[:, :, TOP:TOP + 1], 1.0).then_inc(s["route"], 1)
            dve.memset(w[:, :, TOP + 1:NG], 0.0).then_inc(s["route"], 1)
            dve.wait_ge(s["route"], 15)
            dve.wait_ge(s["set"], 2)
            dve.tensor_copy(w_hi[:, :, :], w[:, :, :]).then_inc(s["wide_steps"], 1)
            dve.wait_ge(s["wide_steps"], 1)
            for j in range(2):
                dve.tensor_copy(w3[:, :, j * NG:(j + 1) * NG], f32(w_hi[:, :, :])).then_inc(s["wide_steps"], 1)
            dve.tensor_tensor(w3[:, :, 2 * NG:3 * NG], w[:, :, :], f32(w_hi[:, :, :]), ALU.subtract)\
               .then_inc(s["wide_steps"], 1)
            dve.wait_ge(s["wide_steps"], 4)
            for q in range(2):
                half = slice(q * N // 2, (q + 1) * N // 2)
                dve.tensor_tensor(w_wide[:, :, :, :], w3[:, half, :].unsqueeze(2).to_broadcast([P, N // 2, 4, QUAD]),
                                  quads[:, :].unsqueeze(1).unsqueeze(3).to_broadcast([P, N // 2, 4, QUAD]), ALU.mult)\
                   .then_inc(s["bd_steps"], 1)
                dve.wait_ge(s["bd_steps"], 2 * q + 1)
                dve.transpose(w_turned[:, :, :].rearrange("p n c -> p (n c)"),
                              w_wide[:, :, :, :].rearrange("p n q r -> p (n q r)")).then_inc(s["bd_steps"], 1)
                dve.wait_ge(s["bd_steps"], 2 * q + 2)
                dve.tensor_copy(wT3[:, half, :], w_turned[:, :, :]).then_inc(s["wide_steps"], 1)
                dve.wait_ge(s["wide_steps"], 5 + q)
            dve.tensor_copy(bd_hi[:, :], bd_raw[:, :]).then_inc(s["bd_steps"], 1)
            dve.wait_ge(s["bd_steps"], 5)
            dve.tensor_tensor(bd_raw[:, :], bd_raw[:, :], f32(bd_hi[:, :]), ALU.subtract).then_inc(s["bd_steps"], 1)
            dve.wait_ge(s["bd_steps"], 6)
            dve.tensor_scalar(bd_raw[:, :], bd_raw[:, :], bd_mask[:, 1:2], None, ALU.mult).then_inc(s["wide_steps"], 1)
            dve.wait_ge(s["wide_steps"], 7)
            dve.scalar_tensor_tensor(out=bd3[:, :], in0=f32(bd_hi[:, :]), scalar=bd_mask[:, 0:1], in1=bd_raw[:, :],
                                     op0=ALU.mult, op1=ALU.add).then_inc(s["wide_steps"], 1)

            def hidden(n, j, a, par, shared, first=False):
                dve.wait_ge(s["silu_done"], 2 * n + a + 1)
                if not shared:
                    if not first:
                        dve.wait_ge(s["h_lo"], 2 * n + a - 1)
                    dve.scalar_tensor_tensor(out=h[:, a, :], in0=GU[2 * a + 1][:, :], scalar=bias[:, j, 1, a:a + 1],
                                             in1=silu[:, a, :], op0=ALU.add, op1=ALU.mult).then_inc(s["h_done"], 1)
                    dve.wait_ge(s["h_done"], 2 * n + a + 1)
                dve.tensor_copy(h_hi[:, par, a, :], h[:, a, :]).then_inc(s["h_hi"], 1)

            def accumulate(n, k, c, t, shared):
                dve.wait_ge(s["down_done"], TT * n + t + 1)
                tile = acc[:, c * TT + t, :]
                if shared:
                    dve.tensor_tensor(tile, DN[t][:, :], tile, ALU.add).then_inc(s["acc_done"], 1)
                else:
                    dve.scalar_tensor_tensor(out=tile, in0=DN[t][:, :], scalar=w[:, c * TT + t, bass.ts(k, 1)], in1=tile,
                                             op0=ALU.mult, op1=ALU.add).then_inc(s["acc_done"], 1)

            def finish(c):
                n = B * N_EXP - B + c
                for t in range(TT):
                    i = c * TT + t
                    dve.wait_ge(s["acc_done"], TT * n + t + 1)
                    dve.bn_stats(bn[:, i, :], acc[:, i, :]).then_inc(s["bn_done"], 1)
                    dve.wait_ge(s["bn_done"], i + 1)
                    dve.bn_aggr(mv[:, i, :], bn[:, i, :]).then_inc(s["aggregated"], 1)
                dve.wait_ge(s["sd_done"], c + 1)
                dve.reciprocal(rs[:, c * TT:(c + 1) * TT], sd[:, c * TT:(c + 1) * TT]).then_inc(s["rs_done"], 1)
                dve.wait_ge(s["rs_done"], c + 1)
                for t in range(TT):
                    i = c * TT + t
                    dve.tensor_scalar(acc[:, i, :], acc[:, i, :], mv[:, i, 0:1], rs[:, i:i + 1], ALU.subtract,
                                      ALU.mult).then_inc(s["out_done"], 1)

            def steps(n0, k0, shared, next_shared, last=False):
                for j in range(2):
                    for c in range(B):
                        n = n0 + j * B + c
                        end = j == 1 and c == B - 1
                        for a in range(HT):
                            if not (last and end):
                                hidden(n + 1, j if c < B - 1 else 1 - j, a, (c + 1) % 2,
                                       next_shared if end else shared)
                            for t in (2 * a, 2 * a + 1):
                                accumulate(n, k0 + j, c, t, shared)
                        if not (last and j == 1):
                            width = EH if shared or (next_shared and j == 1) else 2 * EH
                            if c == 0:
                                split_gu(k0 + j + 1, 1 - j, width)
                            if c == 1:
                                split_dn(k0 + j + 1, 1 - j)
                        if last and j == 1:
                            finish(c)

            for a in range(HT):
                hidden(0, 0, a, 0, False, first=True)
            with dve.Fori(0, EXPERTS // 2 - 1) as i:
                steps(2 * B * i, 2 * i, False, False)
            steps(2 * B * (EXPERTS // 2 - 1), EXPERTS - 2, False, True)
            steps(B * EXPERTS, EXPERTS, True, True, last=True)

        @block.gpsimd
        def _(pool):
            def split_gu(k, j, width=2 * EH):
                pool.wait_ge(s["gu_hi"], k + 1)
                pool.tensor_tensor(gu_lo[:, j, :, 0:width], gu_raw[:, :, 0:width], f32(gu_hi[:, j, :, 0:width]),
                                   ALU.subtract).then_inc(s["gu_lo"], 1)

            def split_dn(k, j):
                pool.wait_ge(s["dn_hi"], k + 1)
                pool.tensor_tensor(dn_lo[:, j, :, :], dn_raw[:, :, :], f32(dn_hi[:, j, :, :]), ALU.subtract)\
                    .then_inc(s["dn_lo"], 1)

            def low(n, a, par):
                pool.wait_ge(s["h_hi"], 2 * n + a + 1)
                pool.tensor_tensor(h_lo[:, par, a, :], h[:, a, :], f32(h_hi[:, par, a, :]), ALU.subtract)\
                    .then_inc(s["h_lo"], 1)

            def steps(n0, k0, shared, next_shared, last=False):
                for j in range(2):
                    for c in range(B):
                        if last and j == 1 and c == B - 1:
                            continue
                        for a in range(HT):
                            low(n0 + j * B + c + 1, a, (c + 1) % 2)
                        if not (last and j == 1):
                            width = EH if shared or (next_shared and j == 1) else 2 * EH
                            if c == 0:
                                split_gu(k0 + j + 1, 1 - j, width)
                            if c == 1:
                                split_dn(k0 + j + 1, 1 - j)

            split_gu(0, 0)
            split_dn(0, 0)
            for a in range(HT):
                low(0, a, 0)
            with pool.Fori(0, EXPERTS // 2 - 1) as i:
                steps(2 * B * i, 2 * i, False, False)
            steps(2 * B * (EXPERTS // 2 - 1), EXPERTS - 2, False, True)
            steps(B * EXPERTS, EXPERTS, True, True, last=True)


def build(nc, dram):
    with ExitStack() as ctx:
        const = constants(nc, ctx)
        attention_phase(nc, const, dram)
        cross_phase(nc, const, dram)
        ffn_phase(nc, const, dram)


def rope_tables():
    inv_freq = np.float32(1.0) / np.float32(10000.0) ** (np.arange(0, ROPE, 2, dtype=np.float32) / np.float32(ROPE))
    freqs = np.outer(np.arange(T, dtype=np.float32), inv_freq).astype(np.float32)
    cos, sin = np.cos(freqs).T, np.sin(freqs).T
    one = np.ones((ROPE, T), np.float32)
    even = np.concatenate([one, cos, cos])
    odd = np.concatenate([cos, cos, one])
    signed = np.concatenate([-sin, sin, -sin, sin])
    by_dim = np.stack([even, odd, signed], axis=1).astype(np.float32)
    tok = np.stack([np.cos(freqs), np.sin(freqs)], axis=1).astype(np.float32)
    return np.ascontiguousarray(by_dim), np.ascontiguousarray(tok.reshape(TT, P, 2, HALF).transpose(1, 0, 2, 3))


def cross_masks():
    p = np.arange(P)
    main = p % KEYS < MAIN
    head = p // HD == np.arange(P // HD)[:, None]
    half, own = np.arange(2)[:, None], p[:, None, None] // KEYS
    cols = (p // HD == 2 * half[None] + own)
    masks = {"xmasks": np.stack([main, ~main], axis=1), "kmask": head.T, "vmask": cols}
    return {n: v.astype(np.float32) for n, v in masks.items()}


def ffn_masks():
    p, e = np.arange(P), np.arange(NG)
    part = p % QUAD // NG
    masks = {"before": e[None, :] < e[:, None], "quads": p[:, None] // QUAD == np.arange(4),
             "bd_mask": np.stack([(part == 0) | (part == 2), part == 1], axis=1)}
    return {n: v.astype(np.float32) for n, v in masks.items()}


def lay_out(inputs):
    a = {n: np.asarray(v) for n, v in inputs.items()}
    out = {"x": a["x"]}
    out["wa"] = np.concatenate([a["L0_attn_wq_a"], a["L0_attn_wkv_a"]], axis=1)
    kv = a["L0_attn_wkv_b"].reshape(KVR, H, NOPE + VD)
    out["wv"] = kv[:, :, NOPE:].transpose(1, 0, 2)
    out["wo"] = a["L0_attn_wo"].reshape(H, VD, D)
    q = a["L0_attn_wq_b"].reshape(QR, PAIRS, 2, 2, DK // 2)
    q = np.stack([q[:, :, 0], q[:, :, 1, ::-1]], axis=2).reshape(QR, PAIRS, 2 * DK).transpose(1, 0, 2)
    k = kv[:, :, :NOPE].reshape(KVR, PAIRS, 2 * NOPE).transpose(1, 0, 2)
    rest = np.zeros((PAIRS, P, 2 * DK), np.float32)
    rest[:, :QR2] = q[:, P:]
    out["ws"] = np.concatenate([q[:, :P], rest, k], axis=2)
    qn = a["L0_attn_q_a_norm_w"]
    rest = np.zeros(P, np.float32)
    rest[:QR2] = qn[P:]
    out["norm_w"] = np.stack([qn[:P], rest, a["L0_attn_kv_a_norm_w"]], axis=1)
    out["rope_T"], out["rope_tok"] = rope_tables()
    out["ctx"] = a["ctx_1024"]
    out["xwq"], out["xwo"] = a["L0_xattn_Wq"], a["L0_xattn_Wo"]
    wk_dca, wv_dca = a["L0_xattn_Wkv_dca"][:, :D], a["L0_xattn_Wkv_dca"][:, D:]
    bk_dca, bv_dca = a["L0_xattn_bkv_dca"][:D], a["L0_xattn_bkv_dca"][D:]
    w = np.concatenate([a["L0_xattn_Wk"], a["L0_xattn_Wv"]], axis=1).reshape(CD, XH, 2, HD)
    bias = np.concatenate([a["L0_xattn_bk"], a["L0_xattn_bv"]]).reshape(XH, 2, HD)
    wk, wv = w[:, :, 0].reshape(CD, D), w[:, :, 1].reshape(CD, D)
    bk, bv = bias[:, 0].reshape(D), bias[:, 1].reshape(D)
    out["xwkv"] = np.stack([wk, wk_dca, wv, wv_dca], axis=1)
    out["xrows"] = np.stack([a["L0_xattn_bq"], bk, bk_dca, bv, bv_dca, a["L0_xattn_bo"]])
    out["xln_wb"] = np.stack([np.stack([a[f"L0_xattn_{n}_{p}"] for n in ("qn", "kn", "kn_dca")]) for p in "wb"])
    out.update(cross_masks())
    f = {n[7:]: v for n, v in a.items() if n.startswith("L0_ffn_")}
    out["wg"], out["bg"] = f["Wg"], f["bg"]
    out["wgu"], out["wdn"] = np.concatenate([f["Wgate"], f["Wup"]], axis=2), f["Wdown"]
    out["wsu"] = f["Ws_up"].reshape(D, 2, EH).transpose(1, 0, 2)
    out["wsd"] = f["Ws_down"].reshape(2, EH, D)
    none = np.zeros((2, EH), np.float32)
    by_gate = np.concatenate([f["bgate"], f["bs_up"].reshape(2, EH)])
    by_up = np.concatenate([f["bup"], none])
    out["fbias"] = np.stack([by_gate, by_up]).reshape(2, N_EXP, HT, P).transpose(1, 3, 0, 2)
    rest = np.zeros((1, D), np.float32)
    down = np.concatenate([f["bdown"], f["bs_down"][None], rest])
    rest = np.zeros((QUAD - 3 * NG, D), np.float32)
    out["bd"] = np.concatenate([down, down, down, rest] * 4)
    out.update(ffn_masks())
    return {n: np.ascontiguousarray(v) for n, v in out.items()}


def kernel(**inputs):
    import concourse.bacc as bacc
    from concourse.bass_utils import run_bass_kernel_spmd

    nc = bacc.Bacc("TRN2", target_bir_lowering=False, num_devices=1)
    arrays = {f"in_{n}_dram": v for n, v in lay_out(inputs).items()}
    dram = {n[3:-5]: nc.dram_tensor(n, v.shape, mybir.dt.from_np(v.dtype), kind="ExternalInput").ap()
            for n, v in arrays.items()}
    dram["x1"] = nc.dram_tensor("x1_dram", (B, T, D), F32, kind="Internal").ap()
    dram["x2"] = nc.dram_tensor("x2_dram", (B, T, D), F32, kind="Internal").ap()
    dram["out"] = nc.dram_tensor("out_0_dram", (B, T, D), F32, kind="ExternalOutput").ap()
    build(nc, dram)
    r = run_bass_kernel_spmd(nc, [arrays], core_ids=[0])
    return r.results[0]["out_0_dram"]
```

```python
from contextlib import ExitStack

import concourse.bass as bass
import numpy as np
from concourse import mybir

F32 = mybir.dt.float32
F32R = mybir.dt.float32r
ACT = mybir.ActivationFunctionType
ALU = mybir.AluOpType
AX = mybir.AxisListType

P = 128
B, T, D = 4, 512, 512
TT = T // P
DT = D // P

H, DK, ROPE, NOPE, VD = 16, 128, 64, 64, 128
KVR, QR = 128, 192
QR2 = QR - P
HALF = ROPE // 2
A_SCALE = float(DK) ** -0.5
A_EPS = float(np.finfo(np.float32).eps)
AW = QR + KVR + ROPE
PAIRS = H // 2
STAGE = 2 * DK + 2 * DK + 2 * NOPE

XH, HD = 16, 32
KEYS, DCA = 64, 16
MAIN = KEYS - DCA
CD = 256
CT = CD // P
X_SCALE = float(HD) ** -0.5
X_EPS = 1e-06

N_EXP, TOP, NG = 8, 6, 8
EH = 256
HT = EH // P
QUAD = 32

LN_EPS = 1e-05


class Memory:

    def __init__(self, nc, ctx):
        self.nc, self.ctx = nc, ctx

    def sb(self, name, shape, dt=F32):
        return self.ctx.enter_context(self.nc.sbuf_tensor(name, shape, dt))

    def split(self, name, shape):
        return self.sb(name + "_hi", shape, F32R), self.sb(name + "_lo", shape, F32R)

    def banks(self, name, n):
        return [self.ctx.enter_context(self.nc.psum_tensor(f"{name}{i}", [P, 512], F32)) for i in range(n)]

    def sem(self, name):
        return self.ctx.enter_context(self.nc.semaphore(name))


def f32(ap):
    return ap.bitcast(F32)


def three(hi_lo_lhsT, hi_lo_rhs):
    (lh, ll), (rh, rl) = hi_lo_lhsT, hi_lo_rhs
    return [(lh, rh), (lh, rl), (ll, rh)]


def constants(nc, ctx):
    ident = ctx.enter_context(nc.sbuf_tensor("ident", [P, P], F32))
    with ExitStack() as inner:
        m = Memory(nc, inner)
        cleared, made = m.sem("ident_cleared"), m.sem("ident_made")
        block = inner.enter_context(nc.Block())

        @block.gpsimd
        def _(pool):
            pool.memset(ident[:, :], 0.0).then_inc(cleared, 1)
            pool.wait_ge(cleared, 1)
            pool.affine_select(out=ident[:, :], in_=ident[:, :], compare_op=ALU.not_equal, fill=1.0, base=0,
                               pattern=[[-1, P]], channel_multiplier=1).then_inc(made, 1)
            pool.wait_ge(made, 1)

    return {"ident": ident}


def attention_phase(nc, const, dram):
    ident = const["ident"]
    with ExitStack() as ctx:
        m = Memory(nc, ctx)
        wa_hi, wa_lo = m.split("wa", [P, DT, AW])
        wvo_hi, wvo_lo = m.split("wvo", [P, H, D])
        norm_w = m.sb("norm_w", [P, 3])
        tab = m.sb("tab", [P, 3, T])
        ktab = m.sb("ktab", [P, TT, 2, HALF])
        eps_a = m.sb("eps_a", [P, 2])
        x_in = m.sb("x_in", [P, TT, D])
        qc = m.sb("qc", [P, TT, AW])
        ssq = m.sb("ssq", [P, TT, 2])
        rms = m.sb("rms", [P, TT, 2])
        rstd = m.sb("rstd", [P, TT, 2])
        kpe = m.sb("kpe", [P, TT, 2 * ROPE])
        ktmp = m.sb("ktmp", [P, 4, TT, HALF])
        qaT_hi, qaT_lo = m.split("qaT", [P, 2, T])
        cT_hi, cT_lo = m.split("cT", [P, T])
        c_hi, c_lo = m.split("c", [P, TT, KVR])
        ws_raw = m.sb("ws_raw", [P, STAGE])
        ws_hi, ws_lo = m.split("ws", [P, STAGE])
        q_raw = m.sb("q_raw", [P, T])
        q_swap = m.sb("q_swap", [P, T])
        q_sin = m.sb("q_sin", [P, T])
        q_rot = m.sb("q_rot", [P, T])
        q_hi, q_lo = m.split("q", [P, 2, T])
        k_raw = m.sb("k_raw", [P, T])
        k_hi, k_lo = m.split("k", [P, 2, T])
        probs = m.sb("probs", [P, TT, T])
        pT_hi, pT_lo = m.split("pT", [P, 2, TT, T])
        o_hi, o_lo = m.split("o", [P, 2, T])
        x1 = m.sb("x1", [P, TT, D])
        wa_raw = qc
        VO = 4
        wo_in = [[probs[:, k, :] for k in range(VO)], [q_raw[:, :], q_swap[:, :], q_sin[:, :], q_rot[:, :]]]
        wv_in = [k_raw[:, :].rearrange("p (k n) -> p k n", k=VO),
                 ws_raw[:, 0:VO * VD].rearrange("p (k n) -> p k n", k=VO)]
        wvT = [kpe[:, :, :], ktmp[:, :, :, :].rearrange("p j t n -> p j (t n)")]
        sq_junk = q_sin
        xT_hi, xT_lo = pT_hi[:, 0, :, :], pT_lo[:, 0, :, :]
        neg_max = m.sb("neg_max", [P, 2, TT])
        total = m.sb("total", [P, 2, TT])
        inv = m.sb("inv", [P, 2, TT])
        bn = m.sb("bn", [P, TT, 6])
        mv = m.sb("mv", [P, TT, 2])
        sd = m.sb("sd", [P, TT])
        rs = m.sb("rs", [P, TT])

        Y = m.banks("Y", TT)
        S = m.banks("S", 2)
        (TR,) = m.banks("TR", 1)
        (M,) = m.banks("M", 1)
        QC = [S[0], S[1], TR, M]

        s = {n: m.sem(n) for n in (
            "wa_loaded", "small_loaded", "vo_loaded0", "vo_loaded1", "wa_split_hi", "wa_split_lo", "set",
            "wv_turned", "wvT_kept", "wvo_done", "wvo_hi_kept", "wvo_lo_kept",
            "x_loaded", "xT_done", "xT_hi_kept", "xT_lo_kept", "qc_done", "squared", "rooted",
            "inverted", "scaled", "pe_kept", "c_split", "k_mults", "k_rot", "abT_done", "abT_hi_kept", "abT_lo_kept",
            "ws_loaded", "ws_hi_kept", "ws_lo_kept", "seeded",
            "q_done", "q_kept", "q_swapped", "q_mults", "q_turned", "q_hi_kept", "q_lo_kept",
            "k_done", "k_kept", "k_hi_kept", "k_lo_kept",
            "scores_done", "max_done", "exp_done", "inv_done", "probs_done", "turned", "pT_hi_kept", "pT_lo_kept",
            "pv_done", "o_hi_kept", "o_lo_kept", "y_done",
            "bn_done", "aggregated", "sd_done", "rs_done", "x1_done", "x1_stored")}

        block = ctx.enter_context(nc.Block())

        @block.sync
        def _(sp):
            def vo_weights(j, g):
                done = s[f"vo_loaded{j}"]
                heads = dram["wv"].rearrange("(g k) p n -> g p k n", k=VO)[g]
                sp.dma_start(wv_in[j], heads).then_inc(done, 16)
                if j == 0:
                    sp.dma_start(probs[:, :, :], dram["wo"].rearrange("(g k) p n -> g p k n", k=VO)[g])\
                      .then_inc(done, 16)
                else:
                    for k in range(VO):
                        sp.dma_start(wo_in[j][k], dram["wo"].rearrange("(g k) p n -> k g p n", k=VO)[k][g])\
                          .then_inc(done, 16)

            vo_weights(0, 0)
            sp.dma_start(norm_w[:, :], dram["norm_w"]).then_inc(s["small_loaded"], 16)
            vo_weights(1, 1)
            sp.dma_start(wa_raw[:, :, :], dram["wa"].rearrange("(k p) n -> p k n", p=P)).then_inc(s["wa_loaded"], 16)
            with sp.Fori(1, H // (2 * VO)) as i:
                for j in range(2):
                    sp.wait_ge(s["wvo_done"], 2 * VO * i + VO * j - VO)
                    vo_weights(j, 2 * i + j)
            sp.dma_start(x_in[:, :, :], dram["x"][0].rearrange("(t p) d -> p t d", p=P)).then_inc(s["x_loaded"], 16)
            sp.dma_start(tab[:, :, :], dram["rope_T"]).then_inc(s["small_loaded"], 16)
            sp.dma_start(ktab[:, :, :, :], dram["rope_tok"]).then_inc(s["small_loaded"], 16)
            sp.wait_ge(s["wv_turned"], H // VO)
            sp.dma_start(ws_raw[:, :], dram["ws"][0]).then_inc(s["ws_loaded"], 16)

            def batch(b, more):
                x_tokens = dram["x"].rearrange("b (t p) d -> b p t d", p=P)
                if more:
                    sp.wait_ge(s["seeded"], b + 1)
                    sp.dma_start(x_in[:, :, :], x_tokens[b + 1]).then_inc(s["x_loaded"], 16)
                with sp.Fori(0, PAIRS - 1) as i:
                    sp.wait_ge(s["ws_lo_kept"], PAIRS * b + i + 1)
                    sp.dma_start(ws_raw[:, :], dram["ws"][i + 1]).then_inc(s["ws_loaded"], 16)
                sp.wait_ge(s["ws_lo_kept"], PAIRS * b + PAIRS)
                sp.dma_start(ws_raw[:, :], dram["ws"][0]).then_inc(s["ws_loaded"], 16)
                sp.wait_ge(s["x1_done"], TT * (b + 1))
                sp.dma_start(dram["x1"].rearrange("b (t p) d -> b p t d", p=P)[b], x1[:, :, :])\
                  .then_inc(s["x1_stored"], 16)

            sp.sem_inc(s["x1_stored"], 16)
            with sp.Fori(0, B - 1) as b:
                batch(b, True)
            batch(B - 1, False)
            sp.wait_ge(s["x1_stored"], 16 * (B + 1))

        @block.tensor
        def _(pe):
            with pe.Fori(0, H // (2 * VO)) as i:
                for j in range(2):
                    g = 2 * i + j
                    pe.wait_ge(s[f"vo_loaded{j}"], (32 if j == 0 else 16 * (1 + VO)) * (i + 1))
                    for k in range(VO):
                        mm = pe.transpose(TR[:, k * KVR:(k + 1) * KVR], wv_in[j][:, k, :], ident[:, :])
                    mm.then_inc(s["wv_turned"], 1)
                    pe.wait_ge(s["wvT_kept"], g + 1)
                    for k in range(VO):
                        pe.wait_ge(s["wvo_lo_kept"], VO * g + k + 1)
                        pe.matmul(Y[k][:, :], wvT[j][:, k, :], wo_in[j][k], start=True, stop=True)\
                          .then_inc(s["wvo_done"], 1)
            pe.wait_ge(s["wvo_lo_kept"], H + VO)

            def q_project(n, h_buf):
                e = h_buf
                steps = three((ws_hi[:, e * DK:(e + 1) * DK], ws_lo[:, e * DK:(e + 1) * DK]),
                              (qaT_hi[:, 0, :], qaT_lo[:, 0, :]))
                o = 2 * DK + e * DK
                steps += three((ws_hi[0:QR2, o:o + DK], ws_lo[0:QR2, o:o + DK]),
                               (qaT_hi[0:QR2, 1, :], qaT_lo[0:QR2, 1, :]))
                for j, (lhsT, rhs) in enumerate(steps):
                    mm = pe.matmul(M[:, :], lhsT, rhs, start=j == 0, stop=j == len(steps) - 1)
                mm.then_inc(s["q_done"], 1)

            def k_project():
                o = 4 * DK
                for j, (lhsT, rhs) in enumerate(three((ws_hi[:, o:o + DK], ws_lo[:, o:o + DK]),
                                                      (cT_hi[:, :], cT_lo[:, :]))):
                    mm = pe.matmul(M[:, :], lhsT, rhs, start=j == 0, stop=j == 2)
                mm.then_inc(s["k_done"], 1)

            def scores(n, e, t, free):
                if t == 0:
                    pe.wait_ge(s["q_lo_kept"], n + 1)
                    pe.wait_ge(s["k_lo_kept"], n + 1)
                if free:
                    pe.wait_ge(s["exp_done"], TT * n + t - 1)
                for j, (lhsT, rhs) in enumerate(three(
                        (q_hi[:, e, t * P:(t + 1) * P], q_lo[:, e, t * P:(t + 1) * P]),
                        (k_hi[:, e, :], k_lo[:, e, :]))):
                    mm = pe.matmul(S[t % 2][:, :], lhsT, rhs, start=j == 0, stop=j == 2)
                mm.then_inc(s["scores_done"], 1)

            def turn(n, t, free=True):
                pe.wait_ge(s["probs_done"], TT * n + t + 1)
                if free:
                    pe.wait_ge(s["pT_lo_kept"], TT * n + t)
                for k in range(TT):
                    mm = pe.transpose(TR[:, k * P:(k + 1) * P], probs[:, t, k * P:(k + 1) * P], ident[:, :])
                mm.then_inc(s["turned"], 1)

            def weigh(n, e, ks):
                if ks[0] == 0:
                    pe.wait_ge(s["pT_lo_kept"], TT * n + TT)
                for k in ks:
                    for j, (lhsT, rhs) in enumerate(three((c_hi[:, k, :], c_lo[:, k, :]),
                                                          (pT_hi[:, e, k, :], pT_lo[:, e, k, :]))):
                        mm = pe.matmul(M[:, :], lhsT, rhs, start=k == 0 and j == 0, stop=k == TT - 1 and j == 2)
                if ks[-1] == TT - 1:
                    mm.then_inc(s["pv_done"], 1)

            def output(n, h, e, t, last=False):
                if t == 0:
                    pe.wait_ge(s["o_lo_kept"], n + 1)
                for j, (lhsT, rhs) in enumerate(three(
                        (o_hi[:, e, t * P:(t + 1) * P], o_lo[:, e, t * P:(t + 1) * P]),
                        (wvo_hi[:, h, :], wvo_lo[:, h, :]))):
                    mm = pe.matmul(Y[t][:, :], lhsT, rhs, start=False, stop=last and j == 2)
                if t == TT - 1 or last:
                    mm.then_inc(s["y_done"], 1)

            def period(n, h, e, first, last):
                for t in range(TT):
                    turn(n, t)
                    if not (last and e == 1):
                        scores(n + 1, 1 - e, t, True)
                    if t == 0 and not last:
                        pe.wait_ge(s["ws_lo_kept"], pair["no"] + 2)
                        if first and e == 0:
                            pe.wait_ge(s["q_kept"], n + 2)
                        elif first:
                            pe.wait_ge(s["k_kept"], pair["no"] + 2)
                        else:
                            pe.wait_ge(s["o_lo_kept"], n - 1)
                        q_project(n + 2, e)
                    if t == 1 and e == 0 and not last:
                        pe.wait_ge(s["q_kept"], n + 3)
                        k_project()
                    if t >= 2 and not (first and e == 0):
                        if t == 2 and last:
                            pe.wait_ge(s["o_lo_kept"], n - 1)
                        elif t == 2 and e == 0:
                            pe.wait_ge(s["k_kept"], pair["no"] + 2)
                        elif t == 2:
                            pe.wait_ge(s["q_kept"], n + 3)
                        weigh(n - 1, 1 - e, range(2 * (t - 2), 2 * (t - 2) + 2))
                    if not first:
                        output(n - 2, h - 2, e, t)

            pair = {}

            pe.wait_ge(s["wa_split_lo"], 1)

            def turn_x(b, d):
                if d >= 2:
                    pe.wait_ge(s["xT_lo_kept"], DT * b + d - 1)
                for t in range(TT):
                    mm = pe.transpose(S[d % 2][:, t * P:(t + 1) * P], x_in[:, t, d * P:(d + 1) * P], ident[:, :])
                mm.then_inc(s["xT_done"], 1)

            def project_x(b):
                pe.wait_ge(s["xT_lo_kept"], DT * (b + 1))
                for t in range(TT):
                    for d in range(DT):
                        for j, (lhsT, rhs) in enumerate(three(
                                (xT_hi[:, d, t * P:(t + 1) * P], xT_lo[:, d, t * P:(t + 1) * P]),
                                (wa_hi[:, d, :], wa_lo[:, d, :]))):
                            mm = pe.matmul(QC[t][:, 0:AW], lhsT, rhs, start=d == 0 and j == 0,
                                           stop=d == DT - 1 and j == 2)
                    mm.then_inc(s["qc_done"], 1)

            def begin(b, first):
                pe.wait_ge(s["scaled"], 2 * TT * (b + 1))
                for t in range(TT):
                    pe.transpose(QC[0][:, t * P:(t + 1) * P], qc[:, t, 0:P], ident[:, :])
                for t in range(TT):
                    pe.transpose(QC[1][0:QR2, t * P:(t + 1) * P], qc[:, t, P:QR], ident[:, :])
                for t in range(TT):
                    mm = pe.transpose(QC[2][:, t * P:(t + 1) * P], qc[:, t, QR:QR + KVR], ident[:, :])
                mm.then_inc(s["abT_done"], 1)
                pe.wait_ge(s["k_rot"], 2 * (b + 1))
                for t in range(TT):
                    mm = pe.transpose(QC[3][:, t * P:(t + 1) * P], kpe[:, t, :], ident[:, :])
                mm.then_inc(s["abT_done"], 1)

                pe.wait_ge(s["abT_lo_kept"], 5 * (b + 1))
                pe.wait_ge(s["ws_lo_kept"], PAIRS * b + 1)
                n0 = H * b
                q_project(n0, 0)
                pe.wait_ge(s["q_kept"], n0 + 1)
                k_project()
                pe.wait_ge(s["k_kept"], PAIRS * b + 1)
                q_project(n0 + 1, 1)
                for t in range(TT):
                    scores(n0, 0, t, t >= 2)
                    if t == 1:
                        if not first:
                            pe.wait_ge(s["x1_done"], TT * b)
                        for u in range(TT):
                            mm = pe.matmul(Y[u][:, :], ident[:, :], x_in[:, u, :], start=True, stop=False)
                        mm.then_inc(s["seeded"], 1)

            def heads(b):
                n0 = H * b
                pair["no"] = PAIRS * b
                period(n0, 0, 0, True, False)
                pe.wait_ge(s["c_split"], 2 * (b + 1))
                period(n0 + 1, 1, 1, True, False)
                with pe.Fori(1, PAIRS - 1) as i:
                    pair["no"] = PAIRS * b + i
                    for e in range(2):
                        period(H * b + 2 * i + e, 2 * i + e, e, False, False)
                for e in range(2):
                    period(n0 + H - 2 + e, H - 2 + e, e, False, True)

            def end(b, more):
                n0 = H * b
                if more:
                    pe.wait_ge(s["x_loaded"], 16 * (b + 2))
                    pe.wait_ge(s["exp_done"], TT * (n0 + H))
                    turn_x(b + 1, 0)
                    turn_x(b + 1, 1)
                pe.wait_ge(s["o_lo_kept"], n0 + H - 1)
                weigh(n0 + H - 1, 1, range(TT))
                if more:
                    turn_x(b + 1, 2)
                    turn_x(b + 1, 3)
                for t in range(TT):
                    output(n0 + H - 2, H - 2, 0, t)
                if more:
                    pe.wait_ge(s["o_lo_kept"], n0 + H)
                    project_x(b + 1)
                for t in range(TT):
                    output(n0 + H - 1, H - 1, 1, t, last=True)
                if more:
                    begin(b + 1, False)

            pe.wait_ge(s["x_loaded"], 16)
            for d in range(DT):
                turn_x(0, d)
            project_x(0)
            begin(0, True)
            with pe.Fori(0, B - 1) as b:
                heads(b)
                end(b, True)
            heads(B - 1)
            end(B - 1, False)

        @block.scalar
        def _(act):
            act.wait_ge(s["small_loaded"], 16)
            act.wait_ge(s["set"], 1)
            with act.Fori(0, H // (2 * VO)) as i:
                for j in range(2):
                    g = 2 * i + j
                    act.wait_ge(s["wv_turned"], g + 1)
                    act.activation(wvT[j], TR[:, :].rearrange("p (k n) -> p k n", k=VO), ACT.Copy)\
                       .then_inc(s["wvT_kept"], 1)
                    for k in range(VO):
                        act.wait_ge(s["wvo_done"], VO * g + k + 1)
                        act.activation(wvo_hi[:, VO * g + k, :], Y[k][:, :], ACT.Copy, scale=norm_w[:, 2:3])\
                           .then_inc(s["wvo_hi_kept"], 1)
            act.wait_ge(s["small_loaded"], 48)

            def keep_q(n):
                act.wait_ge(s["q_done"], n + 1)
                act.activation(q_raw[:, :], M[:, :], ACT.Copy, scale=A_SCALE).then_inc(s["q_kept"], 1)

            def swap_q(n, e):
                r = P // 2 if e == 0 else 0
                act.wait_ge(s["q_kept"], n + 1)
                act.activation(q_swap[r:r + HALF, :], q_raw[r + HALF:r + ROPE, :], ACT.Copy)
                act.activation(q_swap[r + HALF:r + ROPE, :], q_raw[r:r + HALF, :], ACT.Copy)\
                   .then_inc(s["q_swapped"], 1)

            def keep_k(no):
                act.wait_ge(s["k_done"], no + 1)
                act.activation(k_raw[:, :], M[:, :], ACT.Copy).then_inc(s["k_kept"], 1)

            def keep_o(n, e):
                act.wait_ge(s["pv_done"], n + 1)
                act.activation(o_hi[:, e, :], M[:, :], ACT.Copy).then_inc(s["o_hi_kept"], 1)

            def softmax(n, e, t):
                act.wait_ge(s["max_done"], TT * n + t + 1)
                act.activation(probs[:, t, :], S[t % 2][:, :], ACT.Exp, bias=neg_max[:, e, t:t + 1], scale=1.0,
                               accum_out=total[:, e, t:t + 1]).then_inc(s["exp_done"], 1)

            def keep_turned(n, e, t):
                act.wait_ge(s["turned"], TT * n + t + 1)
                act.activation(pT_hi[:, e, :, t * P:(t + 1) * P], TR[:, :].rearrange("p (k q) -> p k q", k=TT),
                               ACT.Copy).then_inc(s["pT_hi_kept"], 1)

            def period(n, e, first, last):
                for t in range(TT):
                    keep_turned(n, e, t)
                    if t == 1 and not last:
                        swap_q(n + 2, e)
                    if t == 1 and e == 0 and not last:
                        act.wait_ge(s["k_lo_kept"], n + 2)
                        keep_k(pair["no"] + 1)
                    if t == 3 and not (first and e == 0):
                        keep_o(n - 1, 1 - e)
                    if not (last and e == 1):
                        softmax(n + 1, 1 - e, t)
                    if t == 0 and not last:
                        act.wait_ge(s["q_lo_kept"], n + 2)
                        keep_q(n + 2)

            pair = {}

            def keep_x(b, d):
                act.wait_ge(s["xT_done"], DT * b + d + 1)
                act.activation(xT_hi[:, d, :], S[d % 2][:, :], ACT.Copy).then_inc(s["xT_hi_kept"], 1)

            def root_mean_squares(b, t):
                act.wait_ge(s["qc_done"], TT * b + t + 1)
                parts = ((0, QR), (QR, KVR))
                for j, (o, w) in enumerate(parts):
                    act.activation(sq_junk[:, o:o + w], QC[t][:, o:o + w], ACT.Square,
                                   accum_out=ssq[:, t, j:j + 1]).then_inc(s["squared"], 1)
                for j, (o, w) in enumerate(parts):
                    act.wait_ge(s["squared"], 2 * TT * b + 2 * t + 1 + j)
                    act.activation(rms[:, t, j:j + 1], ssq[:, t, j:j + 1], ACT.Sqrt, bias=eps_a[:, 0:1],
                                   scale=1.0 / w).then_inc(s["rooted"], 1)

            def begin(b, first):
                act.wait_ge(s["scaled"], 2 * TT * (b + 1))
                act.activation(c_hi[:, :, :], qc[:, :, QR:QR + KVR], ACT.Copy).then_inc(s["c_split"], 1)
                act.wait_ge(s["abT_done"], 2 * b + 1)
                act.activation(qaT_hi[:, 0, :], QC[0][:, :], ACT.Copy, scale=norm_w[:, 0:1])\
                   .then_inc(s["abT_hi_kept"], 1)
                act.activation(qaT_hi[0:QR2, 1, :], QC[1][0:QR2, :], ACT.Copy, scale=norm_w[0:QR2, 1:2])\
                   .then_inc(s["abT_hi_kept"], 1)
                act.activation(cT_hi[:, :], QC[2][:, :], ACT.Copy, scale=norm_w[:, 2:3])\
                   .then_inc(s["abT_hi_kept"], 1)
                act.wait_ge(s["abT_done"], 2 * b + 2)
                for e, r in ((0, ROPE), (1, 0)):
                    act.activation(k_hi[r:r + ROPE, e, :], QC[3][r:r + ROPE, :], ACT.Copy)\
                       .then_inc(s["abT_hi_kept"], 1)
                if not first:
                    deviation(b - 1)
                n0 = H * b
                keep_q(n0)
                swap_q(n0, 0)
                keep_k(PAIRS * b)
                act.wait_ge(s["q_lo_kept"], n0 + 1)
                keep_q(n0 + 1)
                swap_q(n0 + 1, 1)
                for t in range(TT):
                    softmax(n0, 0, t)

            def heads(b):
                n0 = H * b
                pair["no"] = PAIRS * b
                period(n0, 0, True, False)
                period(n0 + 1, 1, True, False)
                with act.Fori(1, PAIRS - 1) as i:
                    pair["no"] = PAIRS * b + i
                    for e in range(2):
                        period(H * b + 2 * i + e, e, False, False)
                for e in range(2):
                    period(n0 + H - 2 + e, e, False, True)

            def deviation(b):
                act.wait_ge(s["aggregated"], TT * (b + 1))
                act.activation(sd[:, :], mv[:, :, 1], ACT.Sqrt, bias=eps_a[:, 1:2], scale=1.0)\
                   .then_inc(s["sd_done"], 1)

            def end(b, more):
                if more:
                    keep_x(b + 1, 0)
                    keep_x(b + 1, 1)
                keep_o(H * b + H - 1, 1)
                if more:
                    keep_x(b + 1, 2)
                    keep_x(b + 1, 3)
                    for t in range(TT):
                        root_mean_squares(b + 1, t)
                    begin(b + 1, False)
                else:
                    deviation(b)

            pair = {}
            for d in range(DT):
                keep_x(0, d)
            for t in range(TT):
                root_mean_squares(0, t)
            begin(0, True)
            with act.Fori(0, B - 1) as b:
                heads(b)
                end(b, True)
            heads(B - 1)
            end(B - 1, False)

        @block.vector
        def _(dve):
            dve.sem_inc(s["wvo_lo_kept"], VO)
            dve.memset(eps_a[:, 0:1], A_EPS)
            dve.memset(eps_a[:, 1:2], LN_EPS).then_inc(s["set"], 1)
            dve.wait_ge(s["small_loaded"], 16)
            with dve.Fori(0, H // (2 * VO)) as i:
                for j in range(2):
                    for k in range(VO):
                        h = 2 * VO * i + VO * j + k
                        dve.wait_ge(s["wvo_hi_kept"], h + 1)
                        dve.scalar_tensor_tensor(out=wvo_lo[:, h, :], in0=Y[k][:, :], scalar=norm_w[:, 2:3],
                                                 in1=f32(wvo_hi[:, h, :]), op0=ALU.mult, op1=ALU.subtract)\
                           .then_inc(s["wvo_lo_kept"], 1)
            dve.wait_ge(s["wa_loaded"], 16)
            dve.tensor_copy(wa_hi[:, :, :], wa_raw[:, :, :]).then_inc(s["wa_split_hi"], 1)
            dve.wait_ge(s["wa_split_hi"], 1)
            dve.tensor_tensor(wa_lo[:, :, :], wa_raw[:, :, :], f32(wa_hi[:, :, :]), ALU.subtract)\
               .then_inc(s["wa_split_lo"], 1)

            def split_ws(no):
                dve.wait_ge(s["ws_loaded"], 16 * (no + 1))
                dve.tensor_copy(ws_hi[:, :], ws_raw[:, :]).then_inc(s["ws_hi_kept"], 1)

            def split_q(n, e):
                dve.wait_ge(s["q_turned"], n + 1)
                dve.tensor_copy(q_hi[:, e, :], q_rot[:, :]).then_inc(s["q_hi_kept"], 1)

            def split_k(n, e):
                r = e * NOPE
                dve.wait_ge(s["k_kept"], pair["k"] + 1)
                dve.tensor_copy(k_hi[r:r + NOPE, e, :], k_raw[r:r + NOPE, :]).then_inc(s["k_hi_kept"], 1)

            def row_max(n, e, t):
                dve.wait_ge(s["scores_done"], TT * n + t + 1)
                dve.tensor_reduce(neg_max[:, e, t:t + 1], S[t % 2][:, :], AX.X, ALU.max, negate=True)\
                   .then_inc(s["max_done"], 1)

            def normalise(n, e, t):
                dve.wait_ge(s["exp_done"], TT * n + t + 1)
                dve.reciprocal(inv[:, e, t:t + 1], total[:, e, t:t + 1]).then_inc(s["inv_done"], 1)
                dve.wait_ge(s["inv_done"], TT * n + t + 1)
                dve.tensor_scalar(probs[:, t, :], probs[:, t, :], inv[:, e, t:t + 1], None, ALU.mult)\
                   .then_inc(s["probs_done"], 1)

            def keep_turned(n, e, t):
                dve.wait_ge(s["pT_hi_kept"], TT * n + t + 1)
                dve.tensor_tensor(pT_lo[:, e, :, t * P:(t + 1) * P], TR[:, :].rearrange("p (k q) -> p k q", k=TT),
                                  f32(pT_hi[:, e, :, t * P:(t + 1) * P]), ALU.subtract)\
                   .then_inc(s["pT_lo_kept"], 1)

            def keep_o(n, e):
                dve.wait_ge(s["o_hi_kept"], n + 1)
                dve.tensor_tensor(o_lo[:, e, :], M[:, :], f32(o_hi[:, e, :]), ALU.subtract)\
                   .then_inc(s["o_lo_kept"], 1)

            def period(n, e, first, last, more=True):
                for t in range(TT):
                    keep_turned(n, e, t)
                    if not (last and e == 1):
                        row_max(n + 1, 1 - e, t)
                        if t == 2 and not last:
                            pair["k"] = pair["no"] + 1
                            split_k(n + 2, e)
                        if t == 3 and not (first and e == 0):
                            keep_o(n - 1, 1 - e)
                        normalise(n + 1, 1 - e, t)
                    if t == 2 and not last:
                        split_q(n + 2, e)
                    if t == 1 and e == 1 and more:
                        dve.wait_ge(s["q_done"], n + 3)
                        split_ws(pair["no"] + 2)
                    if t == 3 and last and e == 1:
                        keep_o(n - 1, 1 - e)

            pair = {}
            dve.wait_ge(s["small_loaded"], 48)

            def split_x(b, d):
                dve.wait_ge(s["xT_hi_kept"], DT * b + d + 1)
                dve.tensor_tensor(xT_lo[:, d, :], S[d % 2][:, :], f32(xT_hi[:, d, :]), ALU.subtract)\
                   .then_inc(s["xT_lo_kept"], 1)

            def scale(b, t):
                dve.wait_ge(s["rooted"], 2 * TT * b + 2 * t + 2)
                dve.reciprocal(rstd[:, t, :], rms[:, t, :]).then_inc(s["inverted"], 1)
                dve.tensor_copy(qc[:, t, QR + KVR:AW], QC[t][:, QR + KVR:AW]).then_inc(s["pe_kept"], 1)
                dve.wait_ge(s["inverted"], TT * b + t + 1)
                for j, (o, w) in enumerate(((0, QR), (QR, KVR))):
                    dve.tensor_scalar(qc[:, t, o:o + w], QC[t][:, o:o + w], rstd[:, t, j:j + 1], None, ALU.mult)\
                       .then_inc(s["scaled"], 1)

            def turn_k(b):
                dve.wait_ge(s["pe_kept"], TT * (b + 1))
                k1, k2 = qc[:, :, QR + KVR:QR + KVR + HALF], qc[:, :, QR + KVR + HALF:AW]
                for j, (k, c) in enumerate(((k1, 0), (k2, 1), (k1, 1), (k2, 0))):
                    dve.tensor_tensor(ktmp[:, j, :, :], k, ktab[:, :, c, :], ALU.mult).then_inc(s["k_mults"], 1)
                dve.wait_ge(s["k_mults"], 4 * (b + 1))
                for c in range(2):
                    o = c * ROPE
                    dve.tensor_tensor(kpe[:, :, o:o + HALF], ktmp[:, 0, :, :], ktmp[:, 1, :, :], ALU.subtract)
                    dve.tensor_tensor(kpe[:, :, o + HALF:o + ROPE], ktmp[:, 2, :, :], ktmp[:, 3, :, :], ALU.add)\
                       .then_inc(s["k_rot"], 1)

            def turn_q(n):
                r = P // 2
                dve.wait_ge(s["q_kept"], n + 1)
                dve.tensor_tensor(q_rot[:, :], q_raw[:, :], tab[:, 0, :], ALU.mult).then_inc(s["q_mults"], 1)
                dve.wait_ge(s["q_swapped"], n + 1)
                dve.tensor_tensor(q_sin[r:r + ROPE, :], q_swap[r:r + ROPE, :], tab[r:r + ROPE, 2, :], ALU.mult)\
                   .then_inc(s["q_mults"], 1)
                dve.wait_ge(s["q_mults"], 2 * n + 2)
                dve.tensor_tensor(q_rot[r:r + ROPE, :], q_rot[r:r + ROPE, :], q_sin[r:r + ROPE, :], ALU.add)\
                   .then_inc(s["q_turned"], 1)

            def begin(b, first):
                for t in range(TT):
                    scale(b, t)
                turn_k(b)
                if not first:
                    for t in range(TT):
                        moments(b - 1, t)
                for j, (dst, hi, src, w) in enumerate((
                        (qaT_lo[:, 0, :], qaT_hi[:, 0, :], QC[0][:, :], norm_w[:, 0:1]),
                        (qaT_lo[0:QR2, 1, :], qaT_hi[0:QR2, 1, :], QC[1][0:QR2, :], norm_w[0:QR2, 1:2]),
                        (cT_lo[:, :], cT_hi[:, :], QC[2][:, :], norm_w[:, 2:3]))):
                    dve.wait_ge(s["abT_hi_kept"], 5 * b + j + 1)
                    dve.scalar_tensor_tensor(out=dst, in0=src, scalar=w, in1=f32(hi), op0=ALU.mult,
                                             op1=ALU.subtract).then_inc(s["abT_lo_kept"], 1)
                for e, r in ((0, ROPE), (1, 0)):
                    dve.wait_ge(s["abT_hi_kept"], 5 * b + 4 + e)
                    dve.tensor_tensor(k_lo[r:r + ROPE, e, :], QC[3][r:r + ROPE, :], f32(k_hi[r:r + ROPE, e, :]),
                                      ALU.subtract).then_inc(s["abT_lo_kept"], 1)
                n0 = H * b
                pair["k"] = PAIRS * b
                turn_q(n0)
                split_k(n0, 0)
                split_q(n0, 0)
                dve.wait_ge(s["q_hi_kept"], n0 + 1)
                dve.tensor_tensor(q_lo[:, 0, :], q_rot[:, :], f32(q_hi[:, 0, :]), ALU.subtract)\
                   .then_inc(s["q_lo_kept"], 1)
                split_k(n0 + 1, 1)
                if not first:
                    finish(b - 1)
                row_max(n0, 0, 0)
                row_max(n0, 0, 1)
                normalise(n0, 0, 0)
                row_max(n0, 0, 2)
                normalise(n0, 0, 1)
                split_q(n0 + 1, 1)
                dve.wait_ge(s["q_done"], n0 + 2)
                split_ws(PAIRS * b + 1)
                row_max(n0, 0, 3)
                normalise(n0, 0, 2)
                normalise(n0, 0, 3)

            def heads(b):
                n0 = H * b
                pair["no"] = PAIRS * b
                period(n0, 0, True, False)
                period(n0 + 1, 1, True, False)
                with dve.Fori(1, PAIRS - 1) as i:
                    pair["no"] = PAIRS * b + i
                    for e in range(2):
                        period(H * b + 2 * i + e, e, False, False)
                for e in range(2):
                    period(n0 + H - 2 + e, e, False, True, more=False)

            def moments(b, t):
                dve.wait_ge(s["y_done"], (H - 1 + TT) * b + H - 1 + t + 1)
                dve.bn_stats(bn[:, t, :], Y[t][:, :]).then_inc(s["bn_done"], 1)
                dve.wait_ge(s["bn_done"], TT * b + t + 1)
                dve.memset(rs[:, t:t + 1], 0.0)
                dve.bn_aggr(mv[:, t, :], bn[:, t, :]).then_inc(s["aggregated"], 1)

            def finish(b):
                dve.wait_ge(s["sd_done"], b + 1)
                dve.reciprocal(rs[:, :], sd[:, :]).then_inc(s["rs_done"], 1)
                dve.wait_ge(s["rs_done"], b + 1)
                dve.wait_ge(s["x1_stored"], 16 * (b + 1))
                for t in range(TT):
                    dve.tensor_scalar(x1[:, t, :], Y[t][:, :], mv[:, t, 0:1], rs[:, t:t + 1], ALU.subtract,
                                      ALU.mult).then_inc(s["x1_done"], 1)

            def end(b, more):
                if more:
                    split_x(b + 1, 0)
                    split_x(b + 1, 1)
                keep_o(H * b + H - 1, 1)
                if more:
                    split_x(b + 1, 2)
                    split_x(b + 1, 3)
                    begin(b + 1, False)
                else:
                    for t in range(TT):
                        moments(b, t)
                    finish(b)

            for d in range(DT):
                split_x(0, d)
            split_ws(0)
            begin(0, True)
            with dve.Fori(0, B - 1) as b:
                heads(b)
                end(b, True)
            heads(B - 1)
            end(B - 1, False)

        @block.gpsimd
        def _(pool):
            pool.wait_ge(s["small_loaded"], 48)

            def split_ws(no):
                pool.wait_ge(s["ws_hi_kept"], no + 1)
                pool.tensor_tensor(ws_lo[:, :], ws_raw[:, :], f32(ws_hi[:, :]), ALU.subtract)\
                    .then_inc(s["ws_lo_kept"], 1)
                pool.wait_ge(s["ws_lo_kept"], no + 1)

            def turn_q(n, e):
                r = P // 2 if e == 0 else 0
                pool.wait_ge(s["q_kept"], n + 1)
                pool.tensor_tensor(q_rot[:, :], q_raw[:, :], tab[:, e, :], ALU.mult).then_inc(s["q_mults"], 1)
                pool.wait_ge(s["q_mults"], 2 * n + 1)
                pool.wait_ge(s["q_swapped"], n + 1)
                pool.tensor_tensor(q_sin[r:r + ROPE, :], q_swap[r:r + ROPE, :], tab[r:r + ROPE, 2, :], ALU.mult)\
                    .then_inc(s["q_mults"], 1)
                pool.wait_ge(s["q_mults"], 2 * n + 2)
                pool.tensor_tensor(q_rot[r:r + ROPE, :], q_rot[r:r + ROPE, :], q_sin[r:r + ROPE, :], ALU.add)\
                    .then_inc(s["q_turned"], 1)
                pool.wait_ge(s["q_turned"], n + 1)

            def split_q(n, e):
                pool.wait_ge(s["q_hi_kept"], n + 1)
                pool.tensor_tensor(q_lo[:, e, :], q_rot[:, :], f32(q_hi[:, e, :]), ALU.subtract)\
                    .then_inc(s["q_lo_kept"], 1)

            def split_k(n, e):
                r = e * NOPE
                pool.wait_ge(s["k_hi_kept"], n + 1)
                pool.tensor_tensor(k_lo[r:r + NOPE, e, :], k_raw[r:r + NOPE, :], f32(k_hi[r:r + NOPE, e, :]),
                                   ALU.subtract).then_inc(s["k_lo_kept"], 1)
                pool.wait_ge(s["k_lo_kept"], n + 1)

            def period(n, e, last, more=True):
                if not last:
                    turn_q(n + 2, e)
                if e == 1 and more:
                    split_ws(pair["no"] + 2)
                if not last:
                    split_k(n + 2, e)
                    split_q(n + 2, e)

            pair = {}

            def begin(b):
                n0 = H * b
                pool.wait_ge(s["c_split"], 2 * b + 1)
                pool.tensor_tensor(c_lo[:, :, :], qc[:, :, QR:QR + KVR], f32(c_hi[:, :, :]), ALU.subtract)\
                    .then_inc(s["c_split"], 1)
                split_k(n0, 0)
                split_k(n0 + 1, 1)
                pool.wait_ge(s["q_lo_kept"], n0 + 1)
                turn_q(n0 + 1, 1)
                split_q(n0 + 1, 1)
                pool.wait_ge(s["q_lo_kept"], n0 + 2)
                split_ws(PAIRS * b + 1)

            def heads(b):
                pair["no"] = PAIRS * b
                for e in range(2):
                    period(H * b + e, e, False)
                with pool.Fori(1, PAIRS - 1) as i:
                    pair["no"] = PAIRS * b + i
                    for e in range(2):
                        period(H * b + 2 * i + e, e, False)

            split_ws(0)
            begin(0)
            with pool.Fori(0, B - 1) as b:
                heads(b)
                begin(b + 1)
            heads(B - 1)


def cross_phase(nc, const, dram):
    ident = const["ident"]
    G = TT + 2
    with ExitStack() as ctx:
        m = Memory(nc, ctx)
        wq_hi, wq_lo = m.split("xwq", [P, DT, D])
        wo_hi, wo_lo = m.split("xwo", [P, DT, D])
        wkv = m.sb("xwkv", [P, CT, 4, D])
        rows = m.sb("xrows", [P, 6, D])
        ln_wb = m.sb("xln_wb", [P, 2, 3, HD])
        masks = m.sb("xmasks", [P, 2])
        kmask = m.sb("kmask", [P, 4])
        vmask = m.sb("vmask", [P, 2, P])
        eps = m.sb("xeps", [P, 2])
        first = m.sb("first", [P, P])
        x_in = m.sb("xx_in", [P, TT, D])
        xbo = m.sb("xbo", [P, TT, D])
        ctx_in = m.sb("ctx_in", [KEYS, CD])
        ctxT = m.sb("ctxT", [P, CT, P])
        xT_hi, xT_lo = m.split("xxT", [P, DT, T])
        ln = m.sb("ln", [P, G, D])
        sq = m.sb("sq", [P, 4, D])
        stat = m.sb("stat", [P, 4, G * XH])
        v_sel = m.sb("v_sel", [P, D])
        v_wide = m.sb("v_wide", [P, DT, 2, P])
        vb_hi, vb_lo = m.split("vb", [P, DT, 2, P])
        kT = m.sb("kT", [P, DT, KEYS])
        kb_hi, kb_lo = m.split("kb", [P, DT, 4, KEYS])
        qT_hi, qT_lo = m.split("xqT", [P, DT, T])
        ex = m.sb("ex", [P, TT, XH, KEYS])
        mx = m.sb("mx", [P, TT, 2, XH])
        sm = m.sb("sm", [P, TT, 2, XH])
        iv = m.sb("iv", [P, TT, 2, XH])
        pT_hi, pT_lo = m.split("xpT", [P, XH // 2, T])
        bn = m.sb("xbn", [P, TT, 6])
        mv = m.sb("xmv", [P, TT, 2])
        sd = m.sb("xsd", [P, TT])
        rs = m.sb("xrs", [P, TT])
        cT_hi, cT_lo = qT_hi, qT_lo
        k_wide = v_wide[:, :, :, :].rearrange("p d a (h k) -> p d (a h) k", k=KEYS)
        x2 = xbo
        groups = ((0, MAIN, 0), (MAIN, KEYS, 1))

        units = [(slice(TT, TT + 2), slice(TT * XH, G * XH))]
        units += [(slice(t, t + 1), slice(t * XH, (t + 1) * XH)) for t in range(TT)]
        U = len(units)

        def sq_of(u):
            return slice(0, 2) if u == 0 else slice(2 + u % 2, 3 + u % 2)

        G2 = [ctx.enter_context(nc.psum_tensor(f"G{i}", [P, 2, 512], F32)) for i in range(4)]
        Y = [G2[d // 2][:, d % 2, :] for d in range(4)]
        Z = [G2[2 + d // 2][:, d % 2, :] for d in range(4)]

        s = {n: m.sem("x_" + n) for n in (
            "wq_loaded", "wo_loaded", "small_loaded", "w_hi", "w_lo", "set", "cleared", "first_set",
            "x_loaded", "xbo_done", "turned_x", "turned_ctx", "ctx_kept", "hi", "lo", "q_done", "kv_done",
            "centred", "squared", "stats", "rooted", "scaled", "weighted", "normed",
            "v_masked", "v_steps", "vb_hi", "turned_k", "kT_kept", "k_steps", "kb_hi", "turned_q", "qT_hi", "qT_lo",
            "scores_done", "max_done", "sub_done", "exp_done", "sum_done", "inv_done", "probs_done",
            "turned_p", "pT_hi", "pT_lo", "ctx_done", "cT_hi", "cT_lo", "out_done", "added", "bn_done",
            "aggregated", "sd_done", "rs_done", "x2_done", "x2_stored")}

        block = ctx.enter_context(nc.Block())

        @block.sync
        def _(sp):
            sp.sem_inc(s["x2_stored"], 16)
            sp.dma_start(ln[:, 0:DT, :], dram["xwq"].rearrange("(k p) n -> p k n", p=P)).then_inc(s["wq_loaded"], 16)
            sp.dma_start(sq[:, 0:DT, :], dram["xwo"].rearrange("(k p) n -> p k n", p=P)).then_inc(s["wo_loaded"], 16)
            x1 = dram["x1"].rearrange("b (t p) d -> b p t d", p=P)
            sp.dma_start(wkv[:, :, :, :], dram["xwkv"].rearrange("(k p) j n -> p k j n", p=P))\
              .then_inc(s["small_loaded"], 16)
            sp.dma_start(rows[:, :, :], dram["xrows"].partition_broadcast(P)).then_inc(s["small_loaded"], 16)
            sp.dma_start(ln_wb[:, :, :, :], dram["xln_wb"].partition_broadcast(P)).then_inc(s["small_loaded"], 16)
            sp.dma_start(masks[:, :], dram["xmasks"]).then_inc(s["small_loaded"], 16)
            sp.dma_start(kmask[:, :], dram["kmask"]).then_inc(s["small_loaded"], 16)
            sp.dma_start(vmask[:, :, :], dram["vmask"]).then_inc(s["small_loaded"], 16)
            sp.dma_start(x_in[:, :, :], x1[0]).then_inc(s["x_loaded"], 16)
            sp.dma_start(ctx_in[:, :], dram["ctx"][0]).then_inc(s["x_loaded"], 16)
            with sp.Fori(0, B - 1) as b:
                sp.wait_ge(s["turned_ctx"], b + 1)
                sp.wait_ge(s["xbo_done"], b + 1)
                sp.dma_start(x_in[:, :, :], x1[b + 1]).then_inc(s["x_loaded"], 16)
                sp.dma_start(ctx_in[:, :], dram["ctx"][b + 1]).then_inc(s["x_loaded"], 16)
                sp.wait_ge(s["x2_done"], TT * (b + 1))
                sp.dma_start(dram["x2"].rearrange("b (t p) d -> b p t d", p=P)[b], x2[:, :, :])\
                  .then_inc(s["x2_stored"], 16)
            sp.wait_ge(s["x2_done"], TT * B)
            sp.dma_start(dram["x2"].rearrange("b (t p) d -> b p t d", p=P)[B - 1], x2[:, :, :])\
              .then_inc(s["x2_stored"], 16)
            sp.wait_ge(s["x2_stored"], 16 * (B + 1))

        @block.tensor
        def _(pe):
            pe.wait_ge(s["w_lo"], 2)
            pe.wait_ge(s["small_loaded"], 96)
            pe.wait_ge(s["first_set"], 1)

            def product(out, pairs, begun=False):
                steps = [p for lhsT, rhs in pairs for p in three(lhsT, rhs)]
                for j, (lhsT, rhs) in enumerate(steps):
                    mm = pe.matmul(out, lhsT, rhs, start=j == 0 and not begun, stop=j == len(steps) - 1)
                return mm

            def bias(out, row):
                pe.matmul(out, first[:, :], rows[:, row, :], start=True, stop=False)

            def turn_x(b, d):
                for t in range(TT):
                    mm = pe.transpose(Z[d][:, t * P:(t + 1) * P], x_in[:, t, d * P:(d + 1) * P], ident[:, :])
                mm.then_inc(s["turned_x"], 1)

            def turn_ctx():
                for k in range(CT):
                    mm = pe.transpose(Z[DT - 1][:, k * KEYS:(k + 1) * KEYS], ctx_in[:, k * P:(k + 1) * P],
                                      ident[0:KEYS, 0:KEYS])
                mm.then_inc(s["turned_ctx"], 1)

            def batch(b, more):
                pe.wait_ge(s["ctx_kept"], b + 1)
                for j in range(4):
                    pe.wait_ge(s["lo"], DT * b + j + 1)
                    bias(Z[j], 1 + j)
                    for k in range(CT):
                        mm = pe.matmul(Z[j], ctxT[:, k, :], wkv[:, k, j, :], start=False, stop=k == CT - 1)
                    mm.then_inc(s["kv_done"], 1)
                for t in range(TT):
                    if t == TT - 2:
                        pe.wait_ge(s["normed"], (U + 1) * b + 2)
                    pe.wait_ge(s["added"], TT * b + t + 1)
                    bias(Y[t], 0)
                    product(Y[t], [((xT_hi[:, d, t * P:(t + 1) * P], xT_lo[:, d, t * P:(t + 1) * P]),
                                    (wq_hi[:, d, :], wq_lo[:, d, :])) for d in range(DT)], begun=True)\
                        .then_inc(s["q_done"], 1)
                    if t == TT - 2:
                        for k in range(DT):
                            for g in range(2):
                                mm = pe.transpose(Z[0][:, (2 * k + g) * KEYS:(2 * k + g + 1) * KEYS],
                                                  ln[0:KEYS, TT + g, k * P:(k + 1) * P], ident[0:KEYS, 0:KEYS])
                        mm.then_inc(s["turned_k"], 1)

                def turn_q(t):
                    if t == 0:
                        pe.wait_ge(s["kT_kept"], b + 1)
                    pe.wait_ge(s["normed"], (U + 1) * b + 3 + t)
                    for d in range(DT):
                        mm = pe.transpose(Z[t][:, d * P:(d + 1) * P], ln[:, t, d * P:(d + 1) * P], ident[:, :])
                    mm.then_inc(s["turned_q"], 1)

                def scores(t):
                    if t < 2:
                        pe.wait_ge(s["centred"], U * b + 3 + 2 * t)
                        pe.wait_ge(s["k_steps"], 2 * (b + 1))
                    else:
                        pe.wait_ge(s["sub_done"], 2 * TT * b + 2 * (t - 1))
                    pe.wait_ge(s["qT_lo"], TT * b + t + 1)
                    for d in range(DT):
                        mm = product(G2[t % 2][:, d // 2, (d % 2) * 4 * KEYS:(d % 2 + 1) * 4 * KEYS],
                                     [((qT_hi[:, d, t * P:(t + 1) * P], qT_lo[:, d, t * P:(t + 1) * P]),
                                       (kb_hi[:, d, :, :].rearrange("p h k -> p (h k)"),
                                        kb_lo[:, d, :, :].rearrange("p h k -> p (h k)")))])
                    mm.then_inc(s["scores_done"], 1)

                def turn_probs(t):
                    pe.wait_ge(s["probs_done"], 2 * TT * b + 2 * t + 2)
                    if t == 0:
                        pe.wait_ge(s["qT_lo"], TT * (b + 1))
                    if t >= 2:
                        pe.wait_ge(s["pT_lo"], TT * b + t - 1)
                    for h2 in range(XH // 2):
                        mm = pe.transpose(
                            G2[2 + t % 2][:, h2 // 4, (h2 % 4) * P:(h2 % 4 + 1) * P],
                            ex[:, t, 2 * h2:2 * h2 + 2, :].rearrange("p h k -> p (h k)"), ident[:, :])
                    mm.then_inc(s["turned_p"], 1)

                turn_q(0)
                scores(0)
                turn_q(1)
                scores(1)
                turn_q(2)
                turn_q(3)
                scores(2)
                scores(3)
                for t in range(TT):
                    turn_probs(t)
                pe.wait_ge(s["pT_lo"], TT * (b + 1))
                for d in range(DT):
                    product(Z[d], [((vb_hi[:, d, j, :], vb_lo[:, d, j, :]),
                                    (pT_hi[:, 2 * d + j, :], pT_lo[:, 2 * d + j, :])) for j in range(2)])\
                        .then_inc(s["ctx_done"], 1)
                pe.wait_ge(s["cT_lo"], DT * (b + 1))
                if more:
                    pe.wait_ge(s["x_loaded"], 32 * (b + 2))
                for t in range(TT):
                    product(Y[t], [((cT_hi[:, d, t * P:(t + 1) * P], cT_lo[:, d, t * P:(t + 1) * P]),
                                    (wo_hi[:, d, :], wo_lo[:, d, :])) for d in range(DT)]).then_inc(s["out_done"], 1)
                    if more and t == 0:
                        turn_ctx()
                    elif more:
                        turn_x(b + 1, t - 1)
                if more:
                    pe.wait_ge(s["ctx_kept"], b + 2)
                    turn_x(b + 1, DT - 1)

            pe.wait_ge(s["x_loaded"], 32)
            turn_ctx()
            for d in range(DT):
                if d == DT - 1:
                    pe.wait_ge(s["ctx_kept"], 1)
                turn_x(0, d)
            with pe.Fori(0, B - 1) as b:
                batch(b, True)
            batch(B - 1, False)

        @block.scalar
        def _(act):
            act.wait_ge(s["wq_loaded"], 16)
            act.activation(wq_hi[:, :, :], ln[:, 0:DT, :], ACT.Copy).then_inc(s["w_hi"], 1)
            act.wait_ge(s["wo_loaded"], 16)
            act.activation(wo_hi[:, :, :], sq[:, 0:DT, :], ACT.Copy).then_inc(s["w_hi"], 1)
            act.wait_ge(s["set"], 1)
            act.wait_ge(s["w_lo"], 2)
            def keep_x(b, d):
                act.wait_ge(s["turned_x"], DT * b + d + 1)
                act.activation(xT_hi[:, d, :], Z[d], ACT.Copy).then_inc(s["hi"], 1)

            def keep_ctx(b):
                act.wait_ge(s["turned_ctx"], b + 1)
                for c in range(2):
                    op = act.activation(ctxT[:, :, c * KEYS:(c + 1) * KEYS],
                                        Z[DT - 1][:, 0:CT * KEYS].rearrange("p (k n) -> p k n", n=KEYS), ACT.Copy)
                op.then_inc(s["ctx_kept"], 1)

            def batch(b, more):
                def square(u):
                    g, _ = units[u]
                    act.wait_ge(s["centred"], U * b + u + 1)
                    act.activation(sq[:, sq_of(u), :], ln[:, g, :], ACT.Square).then_inc(s["squared"], 1)

                def root(u):
                    _, c = units[u]
                    act.wait_ge(s["stats"], 2 * U * b + 2 * u + 2)
                    act.activation(stat[:, 2, c], stat[:, 1, c], ACT.Sqrt, bias=eps[:, 0:1], scale=1.0 / HD)\
                       .then_inc(s["rooted"], 1)

                def keep_q(t):
                    act.wait_ge(s["turned_q"], TT * b + t + 1)
                    act.activation(qT_hi[:, :, t * P:(t + 1) * P], Z[t].rearrange("p (d q) -> p d q", q=P), ACT.Copy)\
                       .then_inc(s["qT_hi"], 1)

                def exponent(t):
                    act.wait_ge(s["sub_done"], 2 * TT * b + 2 * t + 2)
                    act.activation(ex[:, t, :, :], ex[:, t, :, :], ACT.Exp, scale=X_SCALE)\
                       .then_inc(s["exp_done"], 1)

                def keep_turned(t):
                    act.wait_ge(s["turned_p"], TT * b + t + 1)
                    act.activation(pT_hi[:, :, t * P:(t + 1) * P],
                                   G2[2 + t % 2][:, :, :].rearrange("p a (h q) -> p (a h) q", q=P), ACT.Copy)\
                       .then_inc(s["pT_hi"], 1)

                square(0)
                root(0)
                act.wait_ge(s["kv_done"], 4 * b + 3)
                act.activation(v_sel[:, :], Z[2], ACT.Copy, scale=masks[:, 0:1]).then_inc(s["v_masked"], 1)
                square(1)
                act.wait_ge(s["v_steps"], 3 * b + 2)
                act.activation(vb_hi[:, :, :, :], v_wide[:, :, :, :], ACT.Copy).then_inc(s["vb_hi"], 1)
                root(1)
                square(2)
                root(2)
                square(3)
                act.wait_ge(s["turned_k"], b + 1)
                for o, e, g in groups:
                    op = act.activation(kT[:, :, o:e],
                                        Z[0].rearrange("p (d g k) -> p d g k", g=2, k=KEYS)[:, :, g, o:e], ACT.Copy)
                op.then_inc(s["kT_kept"], 1)
                root(3)
                act.wait_ge(s["k_steps"], 2 * b + 1)
                act.activation(kb_hi[:, :, :, :], k_wide[:, :, :, :], ACT.Copy).then_inc(s["kb_hi"], 1)
                square(4)
                keep_q(0)
                root(4)
                keep_q(1)
                exponent(0)
                keep_q(2)
                exponent(1)
                keep_q(3)
                exponent(2)
                exponent(3)
                for t in range(TT):
                    keep_turned(t)
                for d in range(DT):
                    act.wait_ge(s["ctx_done"], DT * b + d + 1)
                    act.activation(cT_hi[:, d, :], Z[d], ACT.Copy).then_inc(s["cT_hi"], 1)
                if more:
                    keep_ctx(b + 1)
                    for d in range(DT):
                        keep_x(b + 1, d)
                act.wait_ge(s["aggregated"], TT * (b + 1))
                act.activation(sd[:, :], mv[:, :, 1], ACT.Sqrt, bias=eps[:, 1:2], scale=1.0).then_inc(s["sd_done"], 1)

            keep_ctx(0)
            for d in range(DT):
                keep_x(0, d)
            with act.Fori(0, B - 1) as b:
                batch(b, True)
            batch(B - 1, False)

        @block.vector
        def _(dve):
            dve.sem_inc(s["added"], TT)
            dve.memset(eps[:, 0:1], X_EPS)
            dve.memset(eps[:, 1:2], LN_EPS).then_inc(s["set"], 1)
            dve.wait_ge(s["w_hi"], 1)
            dve.tensor_tensor(wq_lo[:, :, :], ln[:, 0:DT, :], f32(wq_hi[:, :, :]), ALU.subtract).then_inc(s["w_lo"], 1)
            dve.wait_ge(s["w_hi"], 2)
            dve.tensor_tensor(wo_lo[:, :, :], sq[:, 0:DT, :], f32(wo_hi[:, :, :]), ALU.subtract).then_inc(s["w_lo"], 1)
            dve.wait_ge(s["small_loaded"], 96)
            dve.wait_ge(s["w_lo"], 2)

            def heads(ap):
                return ap.rearrange("p g (h d) -> p (g h) d", d=HD)

            def wide(ap, n):
                return ap.unsqueeze(2).to_broadcast([P, ap.shape[1], n])

            def split_x(b, d):
                dve.wait_ge(s["hi"], DT * b + d + 1)
                dve.tensor_tensor(xT_lo[:, d, :], Z[d], f32(xT_hi[:, d, :]), ALU.subtract).then_inc(s["lo"], 1)

            def batch(b, more):
                def centre(u):
                    g, c = units[u]
                    if u == 0:
                        dve.wait_ge(s["kv_done"], 4 * b + 2)
                        src = G2[2][:, :, :].rearrange("p a (h d) -> p (a h) d", d=HD)
                    else:
                        dve.wait_ge(s["q_done"], TT * b + u)
                        src = Y[u - 1].rearrange("p (h d) -> p h d", d=HD)
                    dve.tensor_reduce(stat[:, 0, c], src, AX.X, ALU.add).then_inc(s["stats"], 1)
                    dve.wait_ge(s["stats"], 2 * U * b + 2 * u + 1)
                    dve.scalar_tensor_tensor(out=heads(ln[:, g, :]), in0=wide(stat[:, 0, c], HD), scalar=-1.0 / HD,
                                             in1=src, op0=ALU.mult, op1=ALU.add).then_inc(s["centred"], 1)

                def sum_squares(u):
                    g, c = units[u]
                    dve.wait_ge(s["squared"], U * b + u + 1)
                    dve.tensor_reduce(stat[:, 1, c], heads(sq[:, sq_of(u), :]), AX.X, ALU.add).then_inc(s["stats"], 1)

                def scale(u):
                    g, c = units[u]
                    dve.wait_ge(s["rooted"], U * b + u + 1)
                    dve.reciprocal(stat[:, 3, c], stat[:, 2, c]).then_inc(s["scaled"], 1)
                    dve.wait_ge(s["scaled"], 2 * U * b + 2 * u + 1)
                    dve.tensor_tensor(heads(ln[:, g, :]), heads(ln[:, g, :]), wide(stat[:, 3, c], HD), ALU.mult)\
                       .then_inc(s["scaled"], 1)

                def split_q(t):
                    dve.wait_ge(s["qT_hi"], TT * b + t + 1)
                    dve.tensor_tensor(qT_lo[:, :, t * P:(t + 1) * P], Z[t].rearrange("p (d q) -> p d q", q=P),
                                      f32(qT_hi[:, :, t * P:(t + 1) * P]), ALU.subtract).then_inc(s["qT_lo"], 1)

                def shift(t):
                    scores = G2[t % 2][:, :, :].rearrange("p a (h k) -> p (a h) k", k=KEYS)
                    dve.wait_ge(s["scores_done"], TT * b + t + 1)
                    for o, e, g in groups:
                        dve.tensor_reduce(mx[:, t, g, :], scores[:, :, o:e], AX.X, ALU.max)\
                           .then_inc(s["max_done"], 1)
                    for o, e, g in groups:
                        dve.wait_ge(s["max_done"], 2 * TT * b + 2 * t + 1 + g)
                        dve.tensor_tensor(ex[:, t, :, o:e], scores[:, :, o:e], wide(mx[:, t, g, :], e - o),
                                          ALU.subtract).then_inc(s["sub_done"], 1)

                def invert(t):
                    dve.wait_ge(s["exp_done"], TT * b + t + 1)
                    for o, e, g in groups:
                        dve.tensor_reduce(sm[:, t, g, :], ex[:, t, :, o:e], AX.X, ALU.add)\
                           .then_inc(s["sum_done"], 1)
                    dve.wait_ge(s["sum_done"], 2 * TT * b + 2 * t + 2)
                    dve.reciprocal(iv[:, t, :, :], sm[:, t, :, :]).then_inc(s["inv_done"], 1)

                def keep_turned(t):
                    dve.wait_ge(s["pT_hi"], TT * b + t + 1)
                    dve.tensor_tensor(pT_lo[:, :, t * P:(t + 1) * P],
                                      G2[2 + t % 2][:, :, :].rearrange("p a (h q) -> p (a h) q", q=P),
                                      f32(pT_hi[:, :, t * P:(t + 1) * P]), ALU.subtract).then_inc(s["pT_lo"], 1)

                centre(0)
                sum_squares(0)
                scale(0)
                dve.wait_ge(s["v_masked"], b + 1)
                dve.wait_ge(s["kv_done"], 4 * b + 4)
                dve.scalar_tensor_tensor(out=v_sel[:, :], in0=Z[3], scalar=masks[:, 1:2], in1=v_sel[:, :],
                                         op0=ALU.mult, op1=ALU.add).then_inc(s["v_steps"], 1)
                centre(1)
                dve.wait_ge(s["v_steps"], 3 * b + 1)
                dve.tensor_tensor(
                    v_wide[:, :, :, :],
                    v_sel[:, :].rearrange("p (d c) -> p d c", d=DT).unsqueeze(2).to_broadcast([P, DT, 2, P]),
                    vmask[:, :, :].unsqueeze(1).to_broadcast([P, DT, 2, P]), ALU.mult).then_inc(s["v_steps"], 1)
                sum_squares(1)
                dve.wait_ge(s["vb_hi"], b + 1)
                dve.tensor_tensor(vb_lo[:, :, :, :], v_wide[:, :, :, :], f32(vb_hi[:, :, :, :]), ALU.subtract)\
                   .then_inc(s["v_steps"], 1)
                scale(1)
                centre(2)
                sum_squares(2)
                scale(2)
                centre(3)
                sum_squares(3)
                dve.wait_ge(s["kT_kept"], b + 1)
                dve.wait_ge(s["v_steps"], 3 * b + 3)
                dve.tensor_tensor(k_wide[:, :, :, :], kT[:, :, :].unsqueeze(2).to_broadcast([P, DT, 4, KEYS]),
                                  kmask[:, :].unsqueeze(1).unsqueeze(3).to_broadcast([P, DT, 4, KEYS]), ALU.mult)\
                   .then_inc(s["k_steps"], 1)
                scale(3)
                centre(4)
                dve.wait_ge(s["kb_hi"], b + 1)
                dve.tensor_tensor(kb_lo[:, :, :, :], k_wide[:, :, :, :], f32(kb_hi[:, :, :, :]), ALU.subtract)\
                   .then_inc(s["k_steps"], 1)
                sum_squares(4)
                split_q(0)
                scale(4)
                split_q(1)
                shift(0)
                split_q(2)
                shift(1)
                split_q(3)
                invert(0)
                shift(2)
                invert(1)
                shift(3)
                invert(2)
                keep_turned(0)
                invert(3)
                keep_turned(1)
                keep_turned(2)
                keep_turned(3)
                for d in range(DT):
                    dve.wait_ge(s["cT_hi"], DT * b + d + 1)
                    dve.tensor_tensor(cT_lo[:, d, :], Z[d], f32(cT_hi[:, d, :]), ALU.subtract).then_inc(s["cT_lo"], 1)
                for t in range(TT):
                    dve.wait_ge(s["out_done"], TT * b + t + 1)
                    dve.tensor_tensor(x2[:, t, :], Y[t], xbo[:, t, :], ALU.add).then_inc(s["added"], 1)
                    dve.wait_ge(s["added"], TT * (b + 1) + t + 1)
                    dve.bn_stats(bn[:, t, :], x2[:, t, :]).then_inc(s["bn_done"], 1)
                    dve.wait_ge(s["bn_done"], TT * b + t + 1)
                    dve.memset(rs[:, t:t + 1], 0.0)
                    dve.bn_aggr(mv[:, t, :], bn[:, t, :]).then_inc(s["aggregated"], 1)
                    if more and t:
                        split_x(b + 1, t - 1)
                if more:
                    split_x(b + 1, DT - 1)
                dve.wait_ge(s["sd_done"], b + 1)
                dve.reciprocal(rs[:, :], sd[:, :]).then_inc(s["rs_done"], 1)
                dve.wait_ge(s["rs_done"], b + 1)
                for t in range(TT):
                    dve.tensor_scalar(x2[:, t, :], x2[:, t, :], mv[:, t, 0:1], rs[:, t:t + 1], ALU.subtract,
                                      ALU.mult).then_inc(s["x2_done"], 1)

            for d in range(DT):
                split_x(0, d)
            with dve.Fori(0, B - 1) as b:
                batch(b, True)
            batch(B - 1, False)

        @block.gpsimd
        def _(pool):
            pool.memset(first[:, :], 0.0).then_inc(s["cleared"], 1)
            pool.wait_ge(s["cleared"], 1)
            pool.memset(first[0:1, :], 1.0).then_inc(s["first_set"], 1)
            pool.wait_ge(s["small_loaded"], 96)
            with pool.Fori(0, B) as b:
                parts = [(ln[:, TT + g, :], 1 + g, 0) for g in range(2)] + \
                    [(ln[:, t, :], 0, 1 + t) for t in range(TT)]
                for step, row in (("weighted", 0), ("normed", 1)):
                    for i, (part, c, u) in enumerate(parts[0:2]):
                        pool.wait_ge(s["scaled"], 2 * U * b + 2)
                        if row:
                            pool.wait_ge(s["weighted"], (U + 1) * b + i + 1)
                        part = part.rearrange("p (h d) -> p h d", d=HD)
                        pool.tensor_tensor(part, part, ln_wb[:, row, c:c + 1, :].to_broadcast([P, XH, HD]),
                                           (ALU.mult, ALU.add)[row]).then_inc(s[step], 1)
                for i, (part, c, u) in enumerate(parts[2:]):
                    part = part.rearrange("p (h d) -> p h d", d=HD)
                    pool.wait_ge(s["scaled"], 2 * U * b + 2 * u + 2)
                    pool.tensor_tensor(part, part, ln_wb[:, 0, c:c + 1, :].to_broadcast([P, XH, HD]), ALU.mult)\
                        .then_inc(s["weighted"], 1)
                    pool.wait_ge(s["weighted"], (U + 1) * b + 3 + i)
                    pool.tensor_tensor(part, part, ln_wb[:, 1, c:c + 1, :].to_broadcast([P, XH, HD]), ALU.add)\
                        .then_inc(s["normed"], 1)
                pool.wait_ge(s["x2_stored"], 16 * (b + 1))
                pool.wait_ge(s["x_loaded"], 32 * (b + 1))
                pool.tensor_tensor(xbo[:, :, :], x_in[:, :, :], rows[:, 5:6, :].to_broadcast([P, TT, D]), ALU.add)\
                    .then_inc(s["xbo_done"], 1)
                for t in range(TT):
                    pool.wait_ge(s["inv_done"], TT * b + t + 1)
                    for o, e, g in groups:
                        pool.tensor_tensor(ex[:, t, :, o:e], ex[:, t, :, o:e],
                                           iv[:, t, g, :].unsqueeze(2).to_broadcast([P, XH, e - o]), ALU.mult)\
                            .then_inc(s["probs_done"], 1)


def ffn_phase(nc, const, dram):
    ident = const["ident"]
    with ExitStack() as ctx:
        m = Memory(nc, ctx)
        acc = m.sb("acc", [P, B * TT, D])
        xT_hi, xT_lo = m.split("fxT", [P, DT, B * T])
        gu_raw = m.sb("gu_raw", [P, DT, 2 * EH])
        gu_hi, gu_lo = m.split("gu", [P, 2, DT, 2 * EH])
        dn_raw = m.sb("dn_raw", [P, HT, D])
        dn_hi, dn_lo = m.split("dn", [P, 2, HT, D])
        silu = m.sb("silu", [P, HT, T])
        h = m.sb("h", [P, HT, T])
        h_hi, h_lo = m.split("fh", [P, 2, HT, T])
        bias_raw = m.sb("bias_raw", [P, 2, HT])
        bias = m.sb("bias", [P, 2, 2, HT])
        wg_raw = m.sb("wg_raw", [P, DT, NG])
        wg_hi, wg_lo = m.split("wg", [P, DT, NG])
        bg = m.sb("bg", [P, NG])
        before = m.sb("before", [P, NG, NG])
        gate = m.sb("gate", [P, B * TT, NG])
        keep = m.sb("keep", [P, B * TT, NG])
        row = m.sb("row", [P, 3, B * TT])
        w = m.sb("w", [P, B * TT, NG])
        w3 = m.sb("w3", [P, B * TT, QUAD])
        w_hi = m.sb("w_hi", [P, B * TT, NG], F32R)
        quads = m.sb("quads", [P, 4])
        bd_raw = m.sb("bd_raw", [P, D])
        bd_hi = m.sb("bd_hi", [P, D], F32R)
        bd_mask = m.sb("bd_mask", [P, 2])
        bd3 = m.sb("bd3", [P, D], F32R)
        wT3 = m.sb("wT3", [P, B * TT, P], F32R)
        eps = m.sb("feps", [P, 1])
        bn = m.sb("fbn", [P, B * TT, 6])
        mv = m.sb("fmv", [P, B * TT, 2])
        sd = m.sb("fsd", [P, B * TT])
        rs = m.sb("frs", [P, B * TT])
        pairs = h[:, :, :].rearrange("p a (n i j) -> p (a n) i j", i=NG, j=NG)
        ties = silu[:, :, :].rearrange("p a (n i j) -> p (a n) i j", i=NG, j=NG)
        w_wide = h[:, :, :].rearrange("p a (n q r) -> p (a n) q r", q=4, r=QUAD)
        w_turned = silu[:, :, :].rearrange("p a (n c) -> p (a n) c", c=P)

        GU = m.banks("GU", 4)
        DN = m.banks("DN", TT)

        s = {n: m.sem("f_" + n) for n in (
            "x_loaded0", "x_loaded1", "x_loaded2", "x_loaded3", "small_loaded", "gu_loaded", "dn_loaded", "set",
            "turned_x", "xT_hi", "xT_lo", "wg_split", "gate_done", "route", "routed", "bd_steps", "wide_steps",
            "gu_hi", "gu_lo", "dn_hi", "dn_lo",
            "gate_up_done", "silu_done", "h_done", "h_hi", "h_lo", "down_done", "acc_done",
            "bn_done", "aggregated", "sd_done", "rs_done", "out_done", "stored")}

        EXPERTS = N_EXP - 2
        block = ctx.enter_context(nc.Block())

        @block.sync
        def _(sp):
            x2 = dram["x2"].rearrange("b (t p) d -> b p t d", p=P)
            for c in range(B):
                sp.dma_start(acc[:, c * TT:(c + 1) * TT, :], x2[c]).then_inc(s[f"x_loaded{c}"], 16)
            for dst, name in ((wg_raw[:, :, :], "wg"), (quads[:, :], "quads"),
                              (bd_raw[:, :], "bd"), (bd_mask[:, :], "bd_mask")):
                src = dram[name].rearrange("(k p) n -> p k n", p=P) if name == "wg" else dram[name]
                sp.dma_start(dst, src).then_inc(s["small_loaded"], 16)
            sp.dma_start(bg[:, :], dram["bg"].partition_broadcast(P)).then_inc(s["small_loaded"], 16)
            sp.dma_start(before[:, :, :], dram["before"].partition_broadcast(P)).then_inc(s["small_loaded"], 16)

            def load(k, gu, dn, width=2 * EH):
                sp.dma_start(bias_raw[:, :, :], dram["fbias"][k]).then_inc(s["gu_loaded"], 16)
                sp.dma_start(gu_raw[:, :, 0:width], gu.rearrange("(k p) n -> p k n", p=P)).then_inc(s["gu_loaded"], 16)
                sp.dma_start(dn_raw[:, :, :], dn.rearrange("(k p) n -> p k n", p=P)).then_inc(s["dn_loaded"], 16)

            load(0, dram["wgu"][0], dram["wdn"][0])
            with sp.Fori(1, EXPERTS) as k:
                sp.wait_ge(s["gu_lo"], k)
                sp.wait_ge(s["dn_lo"], k)
                load(k, dram["wgu"][k], dram["wdn"][k])
            for j in range(2):
                sp.wait_ge(s["gu_lo"], EXPERTS + j)
                sp.wait_ge(s["dn_lo"], EXPERTS + j)
                load(EXPERTS + j, dram["wsu"][j], dram["wsd"][j], EH)
            for c in range(B):
                sp.wait_ge(s["out_done"], TT * (c + 1))
                sp.dma_start(dram["out"][c].rearrange("(t p) d -> p t d", p=P), acc[:, c * TT:(c + 1) * TT, :])\
                  .then_inc(s["stored"], 16)
            sp.wait_ge(s["stored"], 16 * B)

        @block.tensor
        def _(pe):
            def turn_x(c):
                pe.wait_ge(s[f"x_loaded{c}"], 16)
                for d in range(DT):
                    if c:
                        pe.wait_ge(s["xT_lo"], DT * (c - 1) + d + 1)
                    for t in range(TT):
                        mm = pe.transpose(GU[d][:, t * P:(t + 1) * P], acc[:, c * TT + t, d * P:(d + 1) * P],
                                          ident[:, :])
                    mm.then_inc(s["turned_x"], 1)

            def logits(c):
                pe.wait_ge(s["xT_lo"], DT * (c + 1))
                for n in range(c * TT, (c + 1) * TT):
                    for d in range(DT):
                        for j, (lhsT, rhs) in enumerate(three(
                                (xT_hi[:, d, n * P:(n + 1) * P], xT_lo[:, d, n * P:(n + 1) * P]),
                                (wg_hi[:, d, :], wg_lo[:, d, :]))):
                            mm = pe.matmul(DN[0][:, n * NG:(n + 1) * NG], lhsT, rhs, start=d == 0 and j == 0,
                                           stop=d == DT - 1 and j == 2)
                mm.then_inc(s["gate_done"], 1)

            pe.wait_ge(s["wg_split"], 2)
            for c in range(B):
                turn_x(c)
                if c:
                    logits(c - 1)
            logits(B - 1)

            def gate_up(n, k, j, c, a, shared, first=False):
                if c == 0 and a == 0:
                    pe.wait_ge(s["gu_lo"], k + 1)
                if not first:
                    pe.wait_ge(s["silu_done"], 2 * n + a - 1)
                    if not shared:
                        pe.wait_ge(s["h_done"], 2 * n + a - 1)
                for u in range(1 if shared else 2):
                    o = u * EH + a * P
                    steps = [p for d in range(DT) for p in three(
                        (gu_hi[:, j, d, o:o + P], gu_lo[:, j, d, o:o + P]),
                        (xT_hi[:, d, c * T:(c + 1) * T], xT_lo[:, d, c * T:(c + 1) * T]))]
                    for i, (lhsT, rhs) in enumerate(steps):
                        mm = pe.matmul(GU[2 * a + u][:, :], lhsT, rhs, start=i == 0, stop=i == len(steps) - 1)
                mm.then_inc(s["gate_up_done"], 1)

            def down(n, k, j, c, t, bias=False, first=False):
                if t == 0:
                    pe.wait_ge(s["h_lo"], 2 * n + 2)
                    if c == 0:
                        pe.wait_ge(s["dn_lo"], k + 1)
                if not first:
                    pe.wait_ge(s["acc_done"], TT * (n - 1) + t + 1)
                elif t == 0:
                    pe.wait_ge(s["route"], 1)
                steps = [p for a in range(HT) for p in three(
                    (h_hi[:, c % 2, a, t * P:(t + 1) * P], h_lo[:, c % 2, a, t * P:(t + 1) * P]),
                    (dn_hi[:, j, a, :], dn_lo[:, j, a, :]))]
                if bias:
                    steps.append((wT3[:, c * TT + t, :], bd3[:, :]))
                for i, (lhsT, rhs) in enumerate(steps):
                    mm = pe.matmul(DN[t][:, :], lhsT, rhs, start=i == 0, stop=i == len(steps) - 1)
                mm.then_inc(s["down_done"], 1)

            def steps(n0, k0, shared, next_shared, first=False, last=False):
                for j in range(2):
                    for c in range(B):
                        n = n0 + j * B + c
                        end = j == 1 and c == B - 1
                        nj, nc_ = (j, c + 1) if c < B - 1 else (1 - j, 0)
                        nk = k0 + j + (c == B - 1)
                        for a in range(HT):
                            if not (last and end):
                                gate_up(n + 1, nk, nj, nc_, a, next_shared if end else shared)
                            for t in (2 * a, 2 * a + 1):
                                down(n, k0 + j, j, c, t, bias=shared and j == 1, first=first and j == 0 and c == 0)

            for a in range(HT):
                gate_up(0, 0, 0, 0, a, False, first=True)
            steps(0, 0, False, False, first=True)
            with pe.Fori(1, EXPERTS // 2 - 1) as i:
                steps(2 * B * i, 2 * i, False, False)
            steps(2 * B * (EXPERTS // 2 - 1), EXPERTS - 2, False, True)
            pe.wait_ge(s["wide_steps"], 8)
            steps(B * EXPERTS, EXPERTS, True, True, last=True)

        @block.scalar
        def _(act):
            for n in range(B * DT):
                act.wait_ge(s["turned_x"], n + 1)
                c, d = divmod(n, DT)
                act.activation(xT_hi[:, d, c * T:(c + 1) * T], GU[d][:, :], ACT.Copy).then_inc(s["xT_hi"], 1)
            act.wait_ge(s["route"], 6)
            act.activation(w[:, :, :], gate[:, :, :], ACT.Exp).then_inc(s["routed"], 1)
            act.wait_ge(s["small_loaded"], 16 * 6)
            act.wait_ge(s["wide_steps"], 8)

            def hidden(n, j, a, shared, first=False):
                act.wait_ge(s["gate_up_done"], 2 * n + a + 1)
                if shared:
                    act.wait_ge(s["h_lo"], 2 * n + a - 1)
                dst = h if shared else silu
                act.activation(dst[:, a, :], GU[2 * a][:, :], ACT.Silu, bias=bias[:, j, 0, a:a + 1], scale=1.0)\
                   .then_inc(s["silu_done"], 1)

            def finish(c):
                act.wait_ge(s["aggregated"], TT * (c + 1))
                act.activation(sd[:, c * TT:(c + 1) * TT], mv[:, c * TT:(c + 1) * TT, 1], ACT.Sqrt,
                               bias=eps[:, 0:1], scale=1.0).then_inc(s["sd_done"], 1)

            def steps(n0, k0, shared, next_shared, last=False):
                for j in range(2):
                    for c in range(B):
                        end = j == 1 and c == B - 1
                        for a in range(0 if last and end else HT):
                            hidden(n0 + j * B + c + 1, j if c < B - 1 else 1 - j, a, next_shared if end else shared)
                        if last and j == 1:
                            finish(c)

            for a in range(HT):
                hidden(0, 0, a, False)
            with act.Fori(0, EXPERTS // 2 - 1) as i:
                steps(2 * B * i, 2 * i, False, False)
            steps(2 * B * (EXPERTS // 2 - 1), EXPERTS - 2, False, True)
            steps(B * EXPERTS, EXPERTS, True, True, last=True)

        @block.vector
        def _(dve):
            dve.memset(eps[:, :], LN_EPS).then_inc(s["set"], 1)
            dve.memset(w3[:, :, :], 0.0).then_inc(s["set"], 1)
            dve.wait_ge(s["small_loaded"], 16 * 6)
            dve.tensor_copy(wg_hi[:, :, :], wg_raw[:, :, :]).then_inc(s["wg_split"], 1)
            dve.wait_ge(s["wg_split"], 1)
            dve.tensor_tensor(wg_lo[:, :, :], wg_raw[:, :, :], f32(wg_hi[:, :, :]), ALU.subtract)\
               .then_inc(s["wg_split"], 1)

            def split_gu(k, j, width=2 * EH):
                dve.wait_ge(s["gu_loaded"], 32 * (k + 1))
                dve.tensor_copy(bias[:, j, :, :], bias_raw[:, :, :])
                dve.tensor_copy(gu_hi[:, j, :, 0:width], gu_raw[:, :, 0:width]).then_inc(s["gu_hi"], 1)

            def split_dn(k, j):
                dve.wait_ge(s["dn_loaded"], 16 * (k + 1))
                dve.tensor_copy(dn_hi[:, j, :, :], dn_raw[:, :, :]).then_inc(s["dn_hi"], 1)

            split_gu(0, 0)
            split_dn(0, 0)
            for n in range(B * DT):
                dve.wait_ge(s["xT_hi"], n + 1)
                c, d = divmod(n, DT)
                dve.tensor_tensor(xT_lo[:, d, c * T:(c + 1) * T], GU[d][:, :], f32(xT_hi[:, d, c * T:(c + 1) * T]),
                                  ALU.subtract).then_inc(s["xT_lo"], 1)

            N = B * TT
            cube = [P, N, NG, NG]
            dve.wait_ge(s["gate_done"], B)
            dve.tensor_tensor(gate[:, :, :], DN[0][:, 0:N * NG].rearrange("p (n e) -> p n e", e=NG),
                              bg[:, :].unsqueeze(1).to_broadcast([P, N, NG]), ALU.add).then_inc(s["route"], 1)
            dve.wait_ge(s["route"], 1)
            other, own = gate[:, :, :].unsqueeze(2).to_broadcast(cube), gate[:, :, :].unsqueeze(3).to_broadcast(cube)
            dve.tensor_tensor(pairs[:, :, :, :], other, own, ALU.is_gt).then_inc(s["route"], 1)
            dve.tensor_tensor(ties[:, :, :, :], other, own, ALU.is_equal).then_inc(s["route"], 1)
            dve.tensor_reduce(row[:, 0, :], gate[:, :, :], AX.X, ALU.max).then_inc(s["route"], 1)
            dve.wait_ge(s["route"], 4)
            dve.tensor_tensor(ties[:, :, :, :], ties[:, :, :, :], before[:, :, :].unsqueeze(1).to_broadcast(cube),
                              ALU.mult).then_inc(s["route"], 1)
            dve.tensor_tensor(gate[:, :, :], gate[:, :, :], row[:, 0, :].unsqueeze(2).to_broadcast([P, N, NG]),
                              ALU.subtract).then_inc(s["route"], 1)
            dve.wait_ge(s["route"], 5)
            dve.tensor_tensor(pairs[:, :, :, :], pairs[:, :, :, :], ties[:, :, :, :], ALU.add).then_inc(s["route"], 1)
            dve.wait_ge(s["route"], 7)
            dve.tensor_reduce(keep[:, :, :], pairs[:, :, :, :], AX.X, ALU.add).then_inc(s["route"], 1)
            dve.wait_ge(s["route"], 8)
            dve.tensor_scalar(keep[:, :, :], keep[:, :, :], TOP - 0.5, None, ALU.is_lt).then_inc(s["route"], 1)
            dve.wait_ge(s["route"], 9)
            dve.wait_ge(s["routed"], 1)
            dve.tensor_tensor(w[:, :, :], w[:, :, :], keep[:, :, :], ALU.mult).then_inc(s["route"], 1)
            dve.wait_ge(s["route"], 10)
            dve.tensor_reduce(row[:, 1, :], w[:, :, :], AX.X, ALU.add).then_inc(s["route"], 1)
            dve.wait_ge(s["route"], 11)
            dve.reciprocal(row[:, 2, :], row[:, 1, :]).then_inc(s["route"], 1)
            dve.wait_ge(s["route"], 12)
            dve.tensor_tensor(w[:, :, :], w[:, :, :], row[:, 2, :].unsqueeze(2).to_broadcast([P, N, NG]), ALU.mult)\
               .then_inc(s["route"], 1)
            dve.wait_ge(s["route"], 13)
            dve.memset(w[:, :, TOP:TOP + 1], 1.0).then_inc(s["route"], 1)
            dve.memset(w[:, :, TOP + 1:NG], 0.0).then_inc(s["route"], 1)
            dve.wait_ge(s["route"], 15)
            dve.wait_ge(s["set"], 2)
            dve.tensor_copy(w_hi[:, :, :], w[:, :, :]).then_inc(s["wide_steps"], 1)
            dve.wait_ge(s["wide_steps"], 1)
            for j in range(2):
                dve.tensor_copy(w3[:, :, j * NG:(j + 1) * NG], f32(w_hi[:, :, :])).then_inc(s["wide_steps"], 1)
            dve.tensor_tensor(w3[:, :, 2 * NG:3 * NG], w[:, :, :], f32(w_hi[:, :, :]), ALU.subtract)\
               .then_inc(s["wide_steps"], 1)
            dve.wait_ge(s["wide_steps"], 4)
            for q in range(2):
                half = slice(q * N // 2, (q + 1) * N // 2)
                dve.tensor_tensor(w_wide[:, :, :, :], w3[:, half, :].unsqueeze(2).to_broadcast([P, N // 2, 4, QUAD]),
                                  quads[:, :].unsqueeze(1).unsqueeze(3).to_broadcast([P, N // 2, 4, QUAD]), ALU.mult)\
                   .then_inc(s["bd_steps"], 1)
                dve.wait_ge(s["bd_steps"], 2 * q + 1)
                dve.transpose(w_turned[:, :, :].rearrange("p n c -> p (n c)"),
                              w_wide[:, :, :, :].rearrange("p n q r -> p (n q r)")).then_inc(s["bd_steps"], 1)
                dve.wait_ge(s["bd_steps"], 2 * q + 2)
                dve.tensor_copy(wT3[:, half, :], w_turned[:, :, :]).then_inc(s["wide_steps"], 1)
                dve.wait_ge(s["wide_steps"], 5 + q)
            dve.tensor_copy(bd_hi[:, :], bd_raw[:, :]).then_inc(s["bd_steps"], 1)
            dve.wait_ge(s["bd_steps"], 5)
            dve.tensor_tensor(bd_raw[:, :], bd_raw[:, :], f32(bd_hi[:, :]), ALU.subtract).then_inc(s["bd_steps"], 1)
            dve.wait_ge(s["bd_steps"], 6)
            dve.tensor_scalar(bd_raw[:, :], bd_raw[:, :], bd_mask[:, 1:2], None, ALU.mult).then_inc(s["wide_steps"], 1)
            dve.wait_ge(s["wide_steps"], 7)
            dve.scalar_tensor_tensor(out=bd3[:, :], in0=f32(bd_hi[:, :]), scalar=bd_mask[:, 0:1], in1=bd_raw[:, :],
                                     op0=ALU.mult, op1=ALU.add).then_inc(s["wide_steps"], 1)

            def hidden(n, j, a, par, shared, first=False):
                dve.wait_ge(s["silu_done"], 2 * n + a + 1)
                if not shared:
                    if not first:
                        dve.wait_ge(s["h_lo"], 2 * n + a - 1)
                    dve.scalar_tensor_tensor(out=h[:, a, :], in0=GU[2 * a + 1][:, :], scalar=bias[:, j, 1, a:a + 1],
                                             in1=silu[:, a, :], op0=ALU.add, op1=ALU.mult).then_inc(s["h_done"], 1)
                    dve.wait_ge(s["h_done"], 2 * n + a + 1)
                dve.tensor_copy(h_hi[:, par, a, :], h[:, a, :]).then_inc(s["h_hi"], 1)

            def accumulate(n, k, c, t, shared):
                dve.wait_ge(s["down_done"], TT * n + t + 1)
                tile = acc[:, c * TT + t, :]
                if shared:
                    dve.tensor_tensor(tile, DN[t][:, :], tile, ALU.add).then_inc(s["acc_done"], 1)
                else:
                    dve.scalar_tensor_tensor(out=tile, in0=DN[t][:, :], scalar=w[:, c * TT + t, bass.ts(k, 1)], in1=tile,
                                             op0=ALU.mult, op1=ALU.add).then_inc(s["acc_done"], 1)

            def finish(c):
                n = B * N_EXP - B + c
                for t in range(TT):
                    i = c * TT + t
                    dve.wait_ge(s["acc_done"], TT * n + t + 1)
                    dve.bn_stats(bn[:, i, :], acc[:, i, :]).then_inc(s["bn_done"], 1)
                    dve.wait_ge(s["bn_done"], i + 1)
                    dve.bn_aggr(mv[:, i, :], bn[:, i, :]).then_inc(s["aggregated"], 1)
                dve.wait_ge(s["sd_done"], c + 1)
                dve.reciprocal(rs[:, c * TT:(c + 1) * TT], sd[:, c * TT:(c + 1) * TT]).then_inc(s["rs_done"], 1)
                dve.wait_ge(s["rs_done"], c + 1)
                for t in range(TT):
                    i = c * TT + t
                    dve.tensor_scalar(acc[:, i, :], acc[:, i, :], mv[:, i, 0:1], rs[:, i:i + 1], ALU.subtract,
                                      ALU.mult).then_inc(s["out_done"], 1)

            def steps(n0, k0, shared, next_shared, last=False):
                for j in range(2):
                    for c in range(B):
                        n = n0 + j * B + c
                        end = j == 1 and c == B - 1
                        for a in range(HT):
                            if not (last and end):
                                hidden(n + 1, j if c < B - 1 else 1 - j, a, (c + 1) % 2,
                                       next_shared if end else shared)
                            for t in (2 * a, 2 * a + 1):
                                accumulate(n, k0 + j, c, t, shared)
                        if not (last and j == 1):
                            width = EH if shared or (next_shared and j == 1) else 2 * EH
                            if c == 0:
                                split_gu(k0 + j + 1, 1 - j, width)
                            if c == 1:
                                split_dn(k0 + j + 1, 1 - j)
                        if last and j == 1:
                            finish(c)

            for a in range(HT):
                hidden(0, 0, a, 0, False, first=True)
            with dve.Fori(0, EXPERTS // 2 - 1) as i:
                steps(2 * B * i, 2 * i, False, False)
            steps(2 * B * (EXPERTS // 2 - 1), EXPERTS - 2, False, True)
            steps(B * EXPERTS, EXPERTS, True, True, last=True)

        @block.gpsimd
        def _(pool):
            def split_gu(k, j, width=2 * EH):
                pool.wait_ge(s["gu_hi"], k + 1)
                pool.tensor_tensor(gu_lo[:, j, :, 0:width], gu_raw[:, :, 0:width], f32(gu_hi[:, j, :, 0:width]),
                                   ALU.subtract).then_inc(s["gu_lo"], 1)

            def split_dn(k, j):
                pool.wait_ge(s["dn_hi"], k + 1)
                pool.tensor_tensor(dn_lo[:, j, :, :], dn_raw[:, :, :], f32(dn_hi[:, j, :, :]), ALU.subtract)\
                    .then_inc(s["dn_lo"], 1)

            def low(n, a, par):
                pool.wait_ge(s["h_hi"], 2 * n + a + 1)
                pool.tensor_tensor(h_lo[:, par, a, :], h[:, a, :], f32(h_hi[:, par, a, :]), ALU.subtract)\
                    .then_inc(s["h_lo"], 1)

            def steps(n0, k0, shared, next_shared, last=False):
                for j in range(2):
                    for c in range(B):
                        if last and j == 1 and c == B - 1:
                            continue
                        for a in range(HT):
                            low(n0 + j * B + c + 1, a, (c + 1) % 2)
                        if not (last and j == 1):
                            width = EH if shared or (next_shared and j == 1) else 2 * EH
                            if c == 0:
                                split_gu(k0 + j + 1, 1 - j, width)
                            if c == 1:
                                split_dn(k0 + j + 1, 1 - j)

            split_gu(0, 0)
            split_dn(0, 0)
            for a in range(HT):
                low(0, a, 0)
            with pool.Fori(0, EXPERTS // 2 - 1) as i:
                steps(2 * B * i, 2 * i, False, False)
            steps(2 * B * (EXPERTS // 2 - 1), EXPERTS - 2, False, True)
            steps(B * EXPERTS, EXPERTS, True, True, last=True)


def build(nc, dram):
    with ExitStack() as ctx:
        const = constants(nc, ctx)
        attention_phase(nc, const, dram)
        cross_phase(nc, const, dram)
        ffn_phase(nc, const, dram)


def rope_tables():
    inv_freq = np.float32(1.0) / np.float32(10000.0) ** (np.arange(0, ROPE, 2, dtype=np.float32) / np.float32(ROPE))
    freqs = np.outer(np.arange(T, dtype=np.float32), inv_freq).astype(np.float32)
    cos, sin = np.cos(freqs).T, np.sin(freqs).T
    one = np.ones((ROPE, T), np.float32)
    even = np.concatenate([one, cos, cos])
    odd = np.concatenate([cos, cos, one])
    signed = np.concatenate([-sin, sin, -sin, sin])
    by_dim = np.stack([even, odd, signed], axis=1).astype(np.float32)
    tok = np.stack([np.cos(freqs), np.sin(freqs)], axis=1).astype(np.float32)
    return np.ascontiguousarray(by_dim), np.ascontiguousarray(tok.reshape(TT, P, 2, HALF).transpose(1, 0, 2, 3))


def cross_masks():
    p = np.arange(P)
    main = p % KEYS < MAIN
    head = p // HD == np.arange(P // HD)[:, None]
    half, own = np.arange(2)[:, None], p[:, None, None] // KEYS
    cols = (p // HD == 2 * half[None] + own)
    masks = {"xmasks": np.stack([main, ~main], axis=1), "kmask": head.T, "vmask": cols}
    return {n: v.astype(np.float32) for n, v in masks.items()}


def ffn_masks():
    p, e = np.arange(P), np.arange(NG)
    part = p % QUAD // NG
    masks = {"before": e[None, :] < e[:, None], "quads": p[:, None] // QUAD == np.arange(4),
             "bd_mask": np.stack([(part == 0) | (part == 2), part == 1], axis=1)}
    return {n: v.astype(np.float32) for n, v in masks.items()}


def lay_out(inputs):
    a = {n: np.asarray(v) for n, v in inputs.items()}
    out = {"x": a["x"]}
    out["wa"] = np.concatenate([a["L0_attn_wq_a"], a["L0_attn_wkv_a"]], axis=1)
    kv = a["L0_attn_wkv_b"].reshape(KVR, H, NOPE + VD)
    out["wv"] = kv[:, :, NOPE:].transpose(1, 0, 2)
    out["wo"] = a["L0_attn_wo"].reshape(H, VD, D)
    q = a["L0_attn_wq_b"].reshape(QR, PAIRS, 2, 2, DK // 2)
    q = np.stack([q[:, :, 0], q[:, :, 1, ::-1]], axis=2).reshape(QR, PAIRS, 2 * DK).transpose(1, 0, 2)
    k = kv[:, :, :NOPE].reshape(KVR, PAIRS, 2 * NOPE).transpose(1, 0, 2)
    rest = np.zeros((PAIRS, P, 2 * DK), np.float32)
    rest[:, :QR2] = q[:, P:]
    out["ws"] = np.concatenate([q[:, :P], rest, k], axis=2)
    qn = a["L0_attn_q_a_norm_w"]
    rest = np.zeros(P, np.float32)
    rest[:QR2] = qn[P:]
    out["norm_w"] = np.stack([qn[:P], rest, a["L0_attn_kv_a_norm_w"]], axis=1)
    out["rope_T"], out["rope_tok"] = rope_tables()
    out["ctx"] = a["ctx_1024"]
    out["xwq"], out["xwo"] = a["L0_xattn_Wq"], a["L0_xattn_Wo"]
    wk_dca, wv_dca = a["L0_xattn_Wkv_dca"][:, :D], a["L0_xattn_Wkv_dca"][:, D:]
    bk_dca, bv_dca = a["L0_xattn_bkv_dca"][:D], a["L0_xattn_bkv_dca"][D:]
    w = np.concatenate([a["L0_xattn_Wk"], a["L0_xattn_Wv"]], axis=1).reshape(CD, XH, 2, HD)
    bias = np.concatenate([a["L0_xattn_bk"], a["L0_xattn_bv"]]).reshape(XH, 2, HD)
    wk, wv = w[:, :, 0].reshape(CD, D), w[:, :, 1].reshape(CD, D)
    bk, bv = bias[:, 0].reshape(D), bias[:, 1].reshape(D)
    out["xwkv"] = np.stack([wk, wk_dca, wv, wv_dca], axis=1)
    out["xrows"] = np.stack([a["L0_xattn_bq"], bk, bk_dca, bv, bv_dca, a["L0_xattn_bo"]])
    out["xln_wb"] = np.stack([np.stack([a[f"L0_xattn_{n}_{p}"] for n in ("qn", "kn", "kn_dca")]) for p in "wb"])
    out.update(cross_masks())
    f = {n[7:]: v for n, v in a.items() if n.startswith("L0_ffn_")}
    out["wg"], out["bg"] = f["Wg"], f["bg"]
    out["wgu"], out["wdn"] = np.concatenate([f["Wgate"], f["Wup"]], axis=2), f["Wdown"]
    out["wsu"] = f["Ws_up"].reshape(D, 2, EH).transpose(1, 0, 2)
    out["wsd"] = f["Ws_down"].reshape(2, EH, D)
    none = np.zeros((2, EH), np.float32)
    by_gate = np.concatenate([f["bgate"], f["bs_up"].reshape(2, EH)])
    by_up = np.concatenate([f["bup"], none])
    out["fbias"] = np.stack([by_gate, by_up]).reshape(2, N_EXP, HT, P).transpose(1, 3, 0, 2)
    rest = np.zeros((1, D), np.float32)
    down = np.concatenate([f["bdown"], f["bs_down"][None], rest])
    rest = np.zeros((QUAD - 3 * NG, D), np.float32)
    out["bd"] = np.concatenate([down, down, down, rest] * 4)
    out.update(ffn_masks())
    return {n: np.ascontiguousarray(v) for n, v in out.items()}


def kernel(**inputs):
    import concourse.bacc as bacc
    from concourse.bass_utils import run_bass_kernel_spmd

    nc = bacc.Bacc("TRN2", target_bir_lowering=False, num_devices=1)
    arrays = {f"in_{n}_dram": v for n, v in lay_out(inputs).items()}
    dram = {n[3:-5]: nc.dram_tensor(n, v.shape, mybir.dt.from_np(v.dtype), kind="ExternalInput").ap()
            for n, v in arrays.items()}
    dram["x1"] = nc.dram_tensor("x1_dram", (B, T, D), F32, kind="Internal").ap()
    dram["x2"] = nc.dram_tensor("x2_dram", (B, T, D), F32, kind="Internal").ap()
    dram["out"] = nc.dram_tensor("out_0_dram", (B, T, D), F32, kind="ExternalOutput").ap()
    build(nc, dram)
    r = run_bass_kernel_spmd(nc, [arrays], core_ids=[0])
    return r.results[0]["out_0_dram"]
```

```python
from contextlib import ExitStack

import concourse.bass as bass
import numpy as np
from concourse import mybir

F32 = mybir.dt.float32
F32R = mybir.dt.float32r
ACT = mybir.ActivationFunctionType
ALU = mybir.AluOpType
AX = mybir.AxisListType

P = 128
B, T, D = 4, 512, 512
TT = T // P
DT = D // P

H, DK, ROPE, NOPE, VD = 16, 128, 64, 64, 128
KVR, QR = 128, 192
QR2 = QR - P
HALF = ROPE // 2
A_SCALE = float(DK) ** -0.5
A_EPS = float(np.finfo(np.float32).eps)
AW = QR + KVR + ROPE
PAIRS = H // 2
STAGE = 2 * DK + 2 * DK + 2 * NOPE

XH, HD = 16, 32
KEYS, DCA = 64, 16
MAIN = KEYS - DCA
CD = 256
CT = CD // P
X_SCALE = float(HD) ** -0.5
X_EPS = 1e-06

N_EXP, TOP, NG = 8, 6, 8
EH = 256
HT = EH // P
QUAD = 32

LN_EPS = 1e-05


class Memory:

    def __init__(self, nc, ctx):
        self.nc, self.ctx = nc, ctx

    def sb(self, name, shape, dt=F32):
        return self.ctx.enter_context(self.nc.sbuf_tensor(name, shape, dt))

    def split(self, name, shape):
        return self.sb(name + "_hi", shape, F32R), self.sb(name + "_lo", shape, F32R)

    def banks(self, name, n):
        return [self.ctx.enter_context(self.nc.psum_tensor(f"{name}{i}", [P, 512], F32)) for i in range(n)]

    def sem(self, name):
        return self.ctx.enter_context(self.nc.semaphore(name))


def f32(ap):
    return ap.bitcast(F32)


def three(hi_lo_lhsT, hi_lo_rhs):
    (lh, ll), (rh, rl) = hi_lo_lhsT, hi_lo_rhs
    return [(lh, rh), (lh, rl), (ll, rh)]


def constants(nc, ctx):
    ident = ctx.enter_context(nc.sbuf_tensor("ident", [P, P], F32))
    with ExitStack() as inner:
        m = Memory(nc, inner)
        made = m.sem("ident_made")
        block = inner.enter_context(nc.Block())

        @block.gpsimd
        def _(pool):
            pool.memset(ident[:, :], 0.0).then_inc(made, 1)
            pool.wait_ge(made, 1)
            pool.affine_select(out=ident[:, :], in_=ident[:, :], compare_op=ALU.not_equal, fill=1.0, base=0,
                               pattern=[[-1, P]], channel_multiplier=1).then_inc(made, 1)
            pool.wait_ge(made, 2)

    return {"ident": ident}


def attention_phase(nc, const, dram):
    ident = const["ident"]
    with ExitStack() as ctx:
        m = Memory(nc, ctx)
        wa_hi, wa_lo = m.split("wa", [P, DT, AW])
        wvo_hi, wvo_lo = m.split("wvo", [P, H, D])
        norm_w = m.sb("norm_w", [P, 3])
        tab = m.sb("tab", [P, 3, T])
        ktab = m.sb("ktab", [P, TT, 2, HALF])
        eps_a = m.sb("eps_a", [P, 2])
        x_in = m.sb("x_in", [P, TT, D])
        qc = m.sb("qc", [P, TT, AW])
        ssq = m.sb("ssq", [P, TT, 2])
        rms = m.sb("rms", [P, TT, 2])
        rstd = m.sb("rstd", [P, TT, 2])
        kpe = m.sb("kpe", [P, TT, 2 * ROPE])
        ktmp = m.sb("ktmp", [P, 4, TT, HALF])
        qaT_hi, qaT_lo = m.split("qaT", [P, 2, T])
        cT_hi, cT_lo = m.split("cT", [P, T])
        c_hi, c_lo = m.split("c", [P, TT, KVR])
        ws_raw = m.sb("ws_raw", [P, STAGE])
        ws_hi, ws_lo = m.split("ws", [P, STAGE])
        q_raw = m.sb("q_raw", [P, T])
        q_swap = m.sb("q_swap", [P, T])
        q_sin = m.sb("q_sin", [P, T])
        q_rot = m.sb("q_rot", [P, T])
        q_hi, q_lo = m.split("q", [P, 2, T])
        k_raw = m.sb("k_raw", [P, T])
        k_hi, k_lo = m.split("k", [P, 2, T])
        probs = m.sb("probs", [P, TT, T])
        pT_hi, pT_lo = m.split("pT", [P, 2, TT, T])
        o_hi, o_lo = m.split("o", [P, 2, T])
        x1 = const["result"]
        wa_raw = qc
        VO = 4
        wo_in = [[probs[:, k, :] for k in range(VO)], [q_raw[:, :], q_swap[:, :], q_sin[:, :], q_rot[:, :]]]
        wv_in = [k_raw[:, :].rearrange("p (k n) -> p k n", k=VO),
                 ws_raw[:, 0:VO * VD].rearrange("p (k n) -> p k n", k=VO)]
        wvT = [kpe[:, :, :], ktmp[:, :, :, :].rearrange("p j t n -> p j (t n)")]
        sq_junk = q_sin
        xT_hi, xT_lo = pT_hi[:, 0, :, :], pT_lo[:, 0, :, :]
        neg_max = m.sb("neg_max", [P, 2, TT])
        total = m.sb("total", [P, 2, TT])
        inv = m.sb("inv", [P, 2, TT])
        bn = m.sb("bn", [P, TT, 6])
        mv = m.sb("mv", [P, TT, 2])
        sd = m.sb("sd", [P, TT])
        rs = m.sb("rs", [P, TT])

        Y = m.banks("Y", TT)
        S = m.banks("S", 2)
        (TR,) = m.banks("TR", 1)
        (M,) = m.banks("M", 1)
        QC = [S[0], S[1], TR, M]

        s = {n: m.sem(n) for n in (
            "wa_loaded", "small_loaded", "vo_loaded0", "vo_loaded1", "wa_split", "set",
            "wv_turned", "wvT_kept", "wvo_done", "wvo_hi_kept", "wvo_lo_kept",
            "x_loaded", "xT_done", "xT_hi_kept", "xT_lo_kept", "qc_done", "squared", "rooted",
            "inverted", "scaled", "pe_kept", "c_split", "k_mults", "k_rot", "abT_done", "abT_hi_kept", "abT_lo_kept",
            "ws_loaded", "ws_hi_kept", "ws_lo_kept", "seeded",
            "q_done", "q_kept", "q_swapped", "q_mults", "q_turned", "q_hi_kept", "q_lo_kept",
            "k_done", "k_kept", "k_hi_kept", "k_lo_kept",
            "scores_done", "max_done", "exp_done", "inv_done", "probs_done", "turned", "pT_hi_kept", "pT_lo_kept",
            "pv_done", "o_hi_kept", "o_lo_kept", "y_done",
            "bn_done", "aggregated", "sd_done", "rs_done", "x1_done")}
        s["x1_stored"] = const["x1_stored"]

        block = ctx.enter_context(nc.Block())

        @block.sync
        def _(sp):
            def vo_weights(j, g):
                done = s[f"vo_loaded{j}"]
                heads = dram["wv"].rearrange("(g k) p n -> g p k n", k=VO)[g]
                sp.dma_start(wv_in[j], heads).then_inc(done, 16)
                if j == 0:
                    sp.dma_start(probs[:, :, :], dram["wo"].rearrange("(g k) p n -> g p k n", k=VO)[g])\
                      .then_inc(done, 16)
                else:
                    for k in range(VO):
                        sp.dma_start(wo_in[j][k], dram["wo"].rearrange("(g k) p n -> k g p n", k=VO)[k][g])\
                          .then_inc(done, 16)

            vo_weights(0, 0)
            sp.dma_start(norm_w[:, :], dram["norm_w"]).then_inc(s["small_loaded"], 16)
            vo_weights(1, 1)
            sp.dma_start(wa_raw[:, :, :], dram["wa"].rearrange("(k p) n -> p k n", p=P)).then_inc(s["wa_loaded"], 16)
            with sp.Fori(1, H // (2 * VO)) as i:
                for j in range(2):
                    sp.wait_ge(s["wvo_done"], 2 * VO * i + VO * j - VO)
                    vo_weights(j, 2 * i + j)
            sp.dma_start(x_in[:, :, :], dram["x"][0].rearrange("(t p) d -> p t d", p=P)).then_inc(s["x_loaded"], 16)
            sp.dma_start(tab[:, :, :], dram["rope_T"]).then_inc(s["small_loaded"], 16)
            sp.dma_start(ktab[:, :, :, :], dram["rope_tok"]).then_inc(s["small_loaded"], 16)
            sp.wait_ge(s["wv_turned"], H // VO)
            sp.dma_start(ws_raw[:, :], dram["ws"][0]).then_inc(s["ws_loaded"], 16)

            def batch(b, more):
                x_tokens = dram["x"].rearrange("b (t p) d -> b p t d", p=P)
                if more:
                    sp.wait_ge(s["seeded"], b + 1)
                    sp.dma_start(x_in[:, :, :], x_tokens[b + 1]).then_inc(s["x_loaded"], 16)
                with sp.Fori(0, PAIRS - 1) as i:
                    sp.wait_ge(s["ws_lo_kept"], PAIRS * b + i + 1)
                    sp.dma_start(ws_raw[:, :], dram["ws"][i + 1]).then_inc(s["ws_loaded"], 16)
                sp.wait_ge(s["ws_lo_kept"], PAIRS * b + PAIRS)
                sp.dma_start(ws_raw[:, :], dram["ws"][0]).then_inc(s["ws_loaded"], 16)
                sp.wait_ge(s["x1_done"], TT * (b + 1))
                sp.dma_start(dram["x1"].rearrange("b (t p) d -> b p t d", p=P)[b], x1[:, :, :])\
                  .then_inc(s["x1_stored"], 16)

            sp.sem_inc(s["x1_stored"], 16)
            with sp.Fori(0, B - 1) as b:
                batch(b, True)
            batch(B - 1, False)

        @block.tensor
        def _(pe):
            with pe.Fori(0, H // (2 * VO)) as i:
                for j in range(2):
                    g = 2 * i + j
                    pe.wait_ge(s[f"vo_loaded{j}"], (32 if j == 0 else 16 * (1 + VO)) * (i + 1))
                    for k in range(VO):
                        mm = pe.transpose(TR[:, k * KVR:(k + 1) * KVR], wv_in[j][:, k, :], ident[:, :])
                    mm.then_inc(s["wv_turned"], 1)
                    pe.wait_ge(s["wvT_kept"], g + 1)
                    for k in range(VO):
                        pe.wait_ge(s["wvo_lo_kept"], VO * g + k + 1)
                        pe.matmul(Y[k][:, :], wvT[j][:, k, :], wo_in[j][k], start=True, stop=True)\
                          .then_inc(s["wvo_done"], 1)
            pe.wait_ge(s["wvo_lo_kept"], H + VO)

            def q_project(n, h_buf):
                e = h_buf
                steps = three((ws_hi[:, e * DK:(e + 1) * DK], ws_lo[:, e * DK:(e + 1) * DK]),
                              (qaT_hi[:, 0, :], qaT_lo[:, 0, :]))
                o = 2 * DK + e * DK
                steps += three((ws_hi[0:QR2, o:o + DK], ws_lo[0:QR2, o:o + DK]),
                               (qaT_hi[0:QR2, 1, :], qaT_lo[0:QR2, 1, :]))
                for j, (lhsT, rhs) in enumerate(steps):
                    mm = pe.matmul(M[:, :], lhsT, rhs, start=j == 0, stop=j == len(steps) - 1)
                mm.then_inc(s["q_done"], 1)

            def k_project():
                o = 4 * DK
                for j, (lhsT, rhs) in enumerate(three((ws_hi[:, o:o + DK], ws_lo[:, o:o + DK]),
                                                      (cT_hi[:, :], cT_lo[:, :]))):
                    mm = pe.matmul(M[:, :], lhsT, rhs, start=j == 0, stop=j == 2)
                mm.then_inc(s["k_done"], 1)

            def scores(n, e, t, free):
                if t == 0:
                    pe.wait_ge(s["q_lo_kept"], n + 1)
                    pe.wait_ge(s["k_lo_kept"], n + 1)
                if free:
                    pe.wait_ge(s["exp_done"], TT * n + t - 1)
                for j, (lhsT, rhs) in enumerate(three(
                        (q_hi[:, e, t * P:(t + 1) * P], q_lo[:, e, t * P:(t + 1) * P]),
                        (k_hi[:, e, :], k_lo[:, e, :]))):
                    mm = pe.matmul(S[t % 2][:, :], lhsT, rhs, start=j == 0, stop=j == 2)
                mm.then_inc(s["scores_done"], 1)

            def turn(n, t, free=True):
                pe.wait_ge(s["probs_done"], TT * n + t + 1)
                if free:
                    pe.wait_ge(s["pT_lo_kept"], TT * n + t)
                for k in range(TT):
                    mm = pe.transpose(TR[:, k * P:(k + 1) * P], probs[:, t, k * P:(k + 1) * P], ident[:, :])
                mm.then_inc(s["turned"], 1)

            def weigh(n, e, ks):
                if ks[0] == 0:
                    pe.wait_ge(s["pT_lo_kept"], TT * n + TT)
                for k in ks:
                    for j, (lhsT, rhs) in enumerate(three((c_hi[:, k, :], c_lo[:, k, :]),
                                                          (pT_hi[:, e, k, :], pT_lo[:, e, k, :]))):
                        mm = pe.matmul(M[:, :], lhsT, rhs, start=k == 0 and j == 0, stop=k == TT - 1 and j == 2)
                if ks[-1] == TT - 1:
                    mm.then_inc(s["pv_done"], 1)

            def output(n, h, e, t, last=False):
                if t == 0:
                    pe.wait_ge(s["o_lo_kept"], n + 1)
                for j, (lhsT, rhs) in enumerate(three(
                        (o_hi[:, e, t * P:(t + 1) * P], o_lo[:, e, t * P:(t + 1) * P]),
                        (wvo_hi[:, h, :], wvo_lo[:, h, :]))):
                    mm = pe.matmul(Y[t][:, :], lhsT, rhs, start=False, stop=last and j == 2)
                if t == TT - 1 or last:
                    mm.then_inc(s["y_done"], 1)

            def period(n, h, e, first, last):
                for t in range(TT):
                    turn(n, t)
                    if not (last and e == 1):
                        scores(n + 1, 1 - e, t, True)
                    if t == 0 and not last:
                        pe.wait_ge(s["ws_lo_kept"], pair["no"] + 2)
                        if first and e == 0:
                            pe.wait_ge(s["q_kept"], n + 2)
                        elif first:
                            pe.wait_ge(s["k_kept"], pair["no"] + 2)
                        else:
                            pe.wait_ge(s["o_lo_kept"], n - 1)
                        q_project(n + 2, e)
                    if t == 1 and e == 0 and not last:
                        pe.wait_ge(s["q_kept"], n + 3)
                        k_project()
                    if t >= 2 and not (first and e == 0):
                        if t == 2 and last:
                            pe.wait_ge(s["o_lo_kept"], n - 1)
                        elif t == 2 and e == 0:
                            pe.wait_ge(s["k_kept"], pair["no"] + 2)
                        elif t == 2:
                            pe.wait_ge(s["q_kept"], n + 3)
                        weigh(n - 1, 1 - e, range(2 * (t - 2), 2 * (t - 2) + 2))
                    if not first:
                        output(n - 2, h - 2, e, t)

            pair = {}

            pe.wait_ge(s["wa_split"], 2)

            def turn_x(b, d):
                if d >= 2:
                    pe.wait_ge(s["xT_lo_kept"], DT * b + d - 1)
                for t in range(TT):
                    mm = pe.transpose(S[d % 2][:, t * P:(t + 1) * P], x_in[:, t, d * P:(d + 1) * P], ident[:, :])
                mm.then_inc(s["xT_done"], 1)

            def project_x(b):
                pe.wait_ge(s["xT_lo_kept"], DT * (b + 1))
                for t in range(TT):
                    for d in range(DT):
                        for j, (lhsT, rhs) in enumerate(three(
                                (xT_hi[:, d, t * P:(t + 1) * P], xT_lo[:, d, t * P:(t + 1) * P]),
                                (wa_hi[:, d, :], wa_lo[:, d, :]))):
                            mm = pe.matmul(QC[t][:, 0:AW], lhsT, rhs, start=d == 0 and j == 0,
                                           stop=d == DT - 1 and j == 2)
                    mm.then_inc(s["qc_done"], 1)

            def begin(b, first):
                pe.wait_ge(s["scaled"], 2 * TT * (b + 1))
                for t in range(TT):
                    pe.transpose(QC[0][:, t * P:(t + 1) * P], qc[:, t, 0:P], ident[:, :])
                for t in range(TT):
                    pe.transpose(QC[1][0:QR2, t * P:(t + 1) * P], qc[:, t, P:QR], ident[:, :])
                for t in range(TT):
                    mm = pe.transpose(QC[2][:, t * P:(t + 1) * P], qc[:, t, QR:QR + KVR], ident[:, :])
                mm.then_inc(s["abT_done"], 1)
                pe.wait_ge(s["k_rot"], 2 * (b + 1))
                for t in range(TT):
                    mm = pe.transpose(QC[3][:, t * P:(t + 1) * P], kpe[:, t, :], ident[:, :])
                mm.then_inc(s["abT_done"], 1)

                pe.wait_ge(s["abT_lo_kept"], 5 * (b + 1))
                pe.wait_ge(s["ws_lo_kept"], PAIRS * b + 1)
                n0 = H * b
                q_project(n0, 0)
                pe.wait_ge(s["q_kept"], n0 + 1)
                k_project()
                pe.wait_ge(s["k_kept"], PAIRS * b + 1)
                q_project(n0 + 1, 1)
                for t in range(TT):
                    scores(n0, 0, t, t >= 2)
                    if t == 1:
                        if not first:
                            pe.wait_ge(s["x1_done"], TT * b)
                        for u in range(TT):
                            mm = pe.matmul(Y[u][:, :], ident[:, :], x_in[:, u, :], start=True, stop=False)
                        mm.then_inc(s["seeded"], 1)

            def heads(b):
                n0 = H * b
                pair["no"] = PAIRS * b
                period(n0, 0, 0, True, False)
                pe.wait_ge(s["c_split"], 2 * (b + 1))
                period(n0 + 1, 1, 1, True, False)
                with pe.Fori(1, PAIRS - 1) as i:
                    pair["no"] = PAIRS * b + i
                    for e in range(2):
                        period(H * b + 2 * i + e, 2 * i + e, e, False, False)
                for e in range(2):
                    period(n0 + H - 2 + e, H - 2 + e, e, False, True)

            def end(b, more):
                n0 = H * b
                if more:
                    pe.wait_ge(s["x_loaded"], 16 * (b + 2))
                    pe.wait_ge(s["exp_done"], TT * (n0 + H))
                    turn_x(b + 1, 0)
                    turn_x(b + 1, 1)
                pe.wait_ge(s["o_lo_kept"], n0 + H - 1)
                weigh(n0 + H - 1, 1, range(TT))
                if more:
                    turn_x(b + 1, 2)
                    turn_x(b + 1, 3)
                for t in range(TT):
                    output(n0 + H - 2, H - 2, 0, t)
                if more:
                    pe.wait_ge(s["o_lo_kept"], n0 + H)
                    project_x(b + 1)
                for t in range(TT):
                    output(n0 + H - 1, H - 1, 1, t, last=True)
                if more:
                    begin(b + 1, False)

            pe.wait_ge(s["x_loaded"], 16)
            for d in range(DT):
                turn_x(0, d)
            project_x(0)
            begin(0, True)
            with pe.Fori(0, B - 1) as b:
                heads(b)
                end(b, True)
            heads(B - 1)
            end(B - 1, False)

        @block.scalar
        def _(act):
            act.wait_ge(s["small_loaded"], 16)
            act.wait_ge(s["set"], 1)
            with act.Fori(0, H // (2 * VO)) as i:
                for j in range(2):
                    g = 2 * i + j
                    act.wait_ge(s["wv_turned"], g + 1)
                    act.activation(wvT[j], TR[:, :].rearrange("p (k n) -> p k n", k=VO), ACT.Copy)\
                       .then_inc(s["wvT_kept"], 1)
                    for k in range(VO):
                        act.wait_ge(s["wvo_done"], VO * g + k + 1)
                        act.activation(wvo_hi[:, VO * g + k, :], Y[k][:, :], ACT.Copy, scale=norm_w[:, 2:3])\
                           .then_inc(s["wvo_hi_kept"], 1)
            act.wait_ge(s["small_loaded"], 48)

            def keep_q(n):
                act.wait_ge(s["q_done"], n + 1)
                act.activation(q_raw[:, :], M[:, :], ACT.Copy, scale=A_SCALE).then_inc(s["q_kept"], 1)

            def swap_q(n, e):
                r = P // 2 if e == 0 else 0
                act.wait_ge(s["q_kept"], n + 1)
                act.activation(q_swap[r:r + HALF, :], q_raw[r + HALF:r + ROPE, :], ACT.Copy)
                act.activation(q_swap[r + HALF:r + ROPE, :], q_raw[r:r + HALF, :], ACT.Copy)\
                   .then_inc(s["q_swapped"], 1)

            def keep_k(no):
                act.wait_ge(s["k_done"], no + 1)
                act.activation(k_raw[:, :], M[:, :], ACT.Copy).then_inc(s["k_kept"], 1)

            def keep_o(n, e):
                act.wait_ge(s["pv_done"], n + 1)
                act.activation(o_hi[:, e, :], M[:, :], ACT.Copy).then_inc(s["o_hi_kept"], 1)

            def softmax(n, e, t):
                act.wait_ge(s["max_done"], TT * n + t + 1)
                act.activation(probs[:, t, :], S[t % 2][:, :], ACT.Exp, bias=neg_max[:, e, t:t + 1], scale=1.0,
                               accum_out=total[:, e, t:t + 1]).then_inc(s["exp_done"], 1)

            def keep_turned(n, e, t):
                act.wait_ge(s["turned"], TT * n + t + 1)
                act.activation(pT_hi[:, e, :, t * P:(t + 1) * P], TR[:, :].rearrange("p (k q) -> p k q", k=TT),
                               ACT.Copy).then_inc(s["pT_hi_kept"], 1)

            def period(n, e, first, last):
                for t in range(TT):
                    keep_turned(n, e, t)
                    if t == 1 and not last:
                        swap_q(n + 2, e)
                    if t == 1 and e == 0 and not last:
                        act.wait_ge(s["k_lo_kept"], n + 2)
                        keep_k(pair["no"] + 1)
                    if t == 3 and not (first and e == 0):
                        keep_o(n - 1, 1 - e)
                    if not (last and e == 1):
                        softmax(n + 1, 1 - e, t)
                    if t == 0 and not last:
                        act.wait_ge(s["q_lo_kept"], n + 2)
                        keep_q(n + 2)

            pair = {}

            def keep_x(b, d):
                act.wait_ge(s["xT_done"], DT * b + d + 1)
                act.activation(xT_hi[:, d, :], S[d % 2][:, :], ACT.Copy).then_inc(s["xT_hi_kept"], 1)

            def root_mean_squares(b, t):
                act.wait_ge(s["qc_done"], TT * b + t + 1)
                parts = ((0, QR), (QR, KVR))
                for j, (o, w) in enumerate(parts):
                    act.activation(sq_junk[:, o:o + w], QC[t][:, o:o + w], ACT.Square,
                                   accum_out=ssq[:, t, j:j + 1]).then_inc(s["squared"], 1)
                for j, (o, w) in enumerate(parts):
                    act.wait_ge(s["squared"], 2 * TT * b + 2 * t + 1 + j)
                    act.activation(rms[:, t, j:j + 1], ssq[:, t, j:j + 1], ACT.Sqrt, bias=eps_a[:, 0:1],
                                   scale=1.0 / w).then_inc(s["rooted"], 1)

            def begin(b, first):
                act.wait_ge(s["scaled"], 2 * TT * (b + 1))
                act.activation(c_hi[:, :, :], qc[:, :, QR:QR + KVR], ACT.Copy).then_inc(s["c_split"], 1)
                act.wait_ge(s["abT_done"], 2 * b + 1)
                act.activation(qaT_hi[:, 0, :], QC[0][:, :], ACT.Copy, scale=norm_w[:, 0:1])\
                   .then_inc(s["abT_hi_kept"], 1)
                act.activation(qaT_hi[0:QR2, 1, :], QC[1][0:QR2, :], ACT.Copy, scale=norm_w[0:QR2, 1:2])\
                   .then_inc(s["abT_hi_kept"], 1)
                act.activation(cT_hi[:, :], QC[2][:, :], ACT.Copy, scale=norm_w[:, 2:3])\
                   .then_inc(s["abT_hi_kept"], 1)
                act.wait_ge(s["abT_done"], 2 * b + 2)
                for e, r in ((0, ROPE), (1, 0)):
                    act.activation(k_hi[r:r + ROPE, e, :], QC[3][r:r + ROPE, :], ACT.Copy)\
                       .then_inc(s["abT_hi_kept"], 1)
                if not first:
                    deviation(b - 1)
                n0 = H * b
                keep_q(n0)
                swap_q(n0, 0)
                keep_k(PAIRS * b)
                act.wait_ge(s["q_lo_kept"], n0 + 1)
                keep_q(n0 + 1)
                swap_q(n0 + 1, 1)
                for t in range(TT):
                    softmax(n0, 0, t)

            def heads(b):
                n0 = H * b
                pair["no"] = PAIRS * b
                period(n0, 0, True, False)
                period(n0 + 1, 1, True, False)
                with act.Fori(1, PAIRS - 1) as i:
                    pair["no"] = PAIRS * b + i
                    for e in range(2):
                        period(H * b + 2 * i + e, e, False, False)
                for e in range(2):
                    period(n0 + H - 2 + e, e, False, True)

            def deviation(b):
                act.wait_ge(s["aggregated"], TT * (b + 1))
                act.activation(sd[:, :], mv[:, :, 1], ACT.Sqrt, bias=eps_a[:, 1:2], scale=1.0)\
                   .then_inc(s["sd_done"], 1)

            def end(b, more):
                if more:
                    keep_x(b + 1, 0)
                    keep_x(b + 1, 1)
                keep_o(H * b + H - 1, 1)
                if more:
                    keep_x(b + 1, 2)
                    keep_x(b + 1, 3)
                    for t in range(TT):
                        root_mean_squares(b + 1, t)
                    begin(b + 1, False)
                else:
                    deviation(b)

            pair = {}
            for d in range(DT):
                keep_x(0, d)
            for t in range(TT):
                root_mean_squares(0, t)
            begin(0, True)
            with act.Fori(0, B - 1) as b:
                heads(b)
                end(b, True)
            heads(B - 1)
            end(B - 1, False)

        @block.vector
        def _(dve):
            dve.sem_inc(s["wvo_lo_kept"], VO)
            dve.memset(eps_a[:, 0:1], A_EPS)
            dve.memset(eps_a[:, 1:2], LN_EPS).then_inc(s["set"], 1)
            dve.wait_ge(s["small_loaded"], 16)
            with dve.Fori(0, H // (2 * VO)) as i:
                for j in range(2):
                    for k in range(VO):
                        h = 2 * VO * i + VO * j + k
                        dve.wait_ge(s["wvo_hi_kept"], h + 1)
                        dve.scalar_tensor_tensor(out=wvo_lo[:, h, :], in0=Y[k][:, :], scalar=norm_w[:, 2:3],
                                                 in1=f32(wvo_hi[:, h, :]), op0=ALU.mult, op1=ALU.subtract)\
                           .then_inc(s["wvo_lo_kept"], 1)
            dve.wait_ge(s["wa_loaded"], 16)
            dve.tensor_copy(wa_hi[:, :, :], wa_raw[:, :, :]).then_inc(s["wa_split"], 1)
            dve.wait_ge(s["wa_split"], 1)
            dve.tensor_tensor(wa_lo[:, :, :], wa_raw[:, :, :], f32(wa_hi[:, :, :]), ALU.subtract)\
               .then_inc(s["wa_split"], 1)

            def split_ws(no):
                dve.wait_ge(s["ws_loaded"], 16 * (no + 1))
                dve.tensor_copy(ws_hi[:, :], ws_raw[:, :]).then_inc(s["ws_hi_kept"], 1)

            def split_q(n, e):
                dve.wait_ge(s["q_turned"], n + 1)
                dve.tensor_copy(q_hi[:, e, :], q_rot[:, :]).then_inc(s["q_hi_kept"], 1)

            def split_k(n, e):
                r = e * NOPE
                dve.wait_ge(s["k_kept"], pair["k"] + 1)
                dve.tensor_copy(k_hi[r:r + NOPE, e, :], k_raw[r:r + NOPE, :]).then_inc(s["k_hi_kept"], 1)

            def row_max(n, e, t):
                dve.wait_ge(s["scores_done"], TT * n + t + 1)
                dve.tensor_reduce(neg_max[:, e, t:t + 1], S[t % 2][:, :], AX.X, ALU.max, negate=True)\
                   .then_inc(s["max_done"], 1)

            def normalise(n, e, t):
                dve.wait_ge(s["exp_done"], TT * n + t + 1)
                dve.reciprocal(inv[:, e, t:t + 1], total[:, e, t:t + 1]).then_inc(s["inv_done"], 1)
                dve.wait_ge(s["inv_done"], TT * n + t + 1)
                dve.tensor_scalar(probs[:, t, :], probs[:, t, :], inv[:, e, t:t + 1], None, ALU.mult)\
                   .then_inc(s["probs_done"], 1)

            def keep_turned(n, e, t):
                dve.wait_ge(s["pT_hi_kept"], TT * n + t + 1)
                dve.tensor_tensor(pT_lo[:, e, :, t * P:(t + 1) * P], TR[:, :].rearrange("p (k q) -> p k q", k=TT),
                                  f32(pT_hi[:, e, :, t * P:(t + 1) * P]), ALU.subtract)\
                   .then_inc(s["pT_lo_kept"], 1)

            def keep_o(n, e):
                dve.wait_ge(s["o_hi_kept"], n + 1)
                dve.tensor_tensor(o_lo[:, e, :], M[:, :], f32(o_hi[:, e, :]), ALU.subtract)\
                   .then_inc(s["o_lo_kept"], 1)

            def period(n, e, first, last, more=True):
                for t in range(TT):
                    keep_turned(n, e, t)
                    if not (last and e == 1):
                        row_max(n + 1, 1 - e, t)
                        if t == 2 and not last:
                            pair["k"] = pair["no"] + 1
                            split_k(n + 2, e)
                        if t == 3 and not (first and e == 0):
                            keep_o(n - 1, 1 - e)
                        normalise(n + 1, 1 - e, t)
                    if t == 2 and not last:
                        split_q(n + 2, e)
                    if t == 1 and e == 1 and more:
                        dve.wait_ge(s["q_done"], n + 3)
                        split_ws(pair["no"] + 2)
                    if t == 3 and last and e == 1:
                        keep_o(n - 1, 1 - e)

            pair = {}
            dve.wait_ge(s["small_loaded"], 48)

            def split_x(b, d):
                dve.wait_ge(s["xT_hi_kept"], DT * b + d + 1)
                dve.tensor_tensor(xT_lo[:, d, :], S[d % 2][:, :], f32(xT_hi[:, d, :]), ALU.subtract)\
                   .then_inc(s["xT_lo_kept"], 1)

            def scale(b, t):
                dve.wait_ge(s["rooted"], 2 * TT * b + 2 * t + 2)
                dve.reciprocal(rstd[:, t, :], rms[:, t, :]).then_inc(s["inverted"], 1)
                dve.tensor_copy(qc[:, t, QR + KVR:AW], QC[t][:, QR + KVR:AW]).then_inc(s["pe_kept"], 1)
                dve.wait_ge(s["inverted"], TT * b + t + 1)
                for j, (o, w) in enumerate(((0, QR), (QR, KVR))):
                    dve.tensor_scalar(qc[:, t, o:o + w], QC[t][:, o:o + w], rstd[:, t, j:j + 1], None, ALU.mult)\
                       .then_inc(s["scaled"], 1)

            def turn_k(b):
                dve.wait_ge(s["pe_kept"], TT * (b + 1))
                k1, k2 = qc[:, :, QR + KVR:QR + KVR + HALF], qc[:, :, QR + KVR + HALF:AW]
                for j, (k, c) in enumerate(((k1, 0), (k2, 1), (k1, 1), (k2, 0))):
                    dve.tensor_tensor(ktmp[:, j, :, :], k, ktab[:, :, c, :], ALU.mult).then_inc(s["k_mults"], 1)
                dve.wait_ge(s["k_mults"], 4 * (b + 1))
                for c in range(2):
                    o = c * ROPE
                    dve.tensor_tensor(kpe[:, :, o:o + HALF], ktmp[:, 0, :, :], ktmp[:, 1, :, :], ALU.subtract)
                    dve.tensor_tensor(kpe[:, :, o + HALF:o + ROPE], ktmp[:, 2, :, :], ktmp[:, 3, :, :], ALU.add)\
                       .then_inc(s["k_rot"], 1)

            def turn_q(n):
                r = P // 2
                dve.wait_ge(s["q_kept"], n + 1)
                dve.tensor_tensor(q_rot[:, :], q_raw[:, :], tab[:, 0, :], ALU.mult).then_inc(s["q_mults"], 1)
                dve.wait_ge(s["q_swapped"], n + 1)
                dve.tensor_tensor(q_sin[r:r + ROPE, :], q_swap[r:r + ROPE, :], tab[r:r + ROPE, 2, :], ALU.mult)\
                   .then_inc(s["q_mults"], 1)
                dve.wait_ge(s["q_mults"], 2 * n + 2)
                dve.tensor_tensor(q_rot[r:r + ROPE, :], q_rot[r:r + ROPE, :], q_sin[r:r + ROPE, :], ALU.add)\
                   .then_inc(s["q_turned"], 1)

            def begin(b, first):
                for t in range(TT):
                    scale(b, t)
                turn_k(b)
                if not first:
                    for t in range(TT):
                        moments(b - 1, t)
                for j, (dst, hi, src, w) in enumerate((
                        (qaT_lo[:, 0, :], qaT_hi[:, 0, :], QC[0][:, :], norm_w[:, 0:1]),
                        (qaT_lo[0:QR2, 1, :], qaT_hi[0:QR2, 1, :], QC[1][0:QR2, :], norm_w[0:QR2, 1:2]),
                        (cT_lo[:, :], cT_hi[:, :], QC[2][:, :], norm_w[:, 2:3]))):
                    dve.wait_ge(s["abT_hi_kept"], 5 * b + j + 1)
                    dve.scalar_tensor_tensor(out=dst, in0=src, scalar=w, in1=f32(hi), op0=ALU.mult,
                                             op1=ALU.subtract).then_inc(s["abT_lo_kept"], 1)
                for e, r in ((0, ROPE), (1, 0)):
                    dve.wait_ge(s["abT_hi_kept"], 5 * b + 4 + e)
                    dve.tensor_tensor(k_lo[r:r + ROPE, e, :], QC[3][r:r + ROPE, :], f32(k_hi[r:r + ROPE, e, :]),
                                      ALU.subtract).then_inc(s["abT_lo_kept"], 1)
                n0 = H * b
                pair["k"] = PAIRS * b
                turn_q(n0)
                split_k(n0, 0)
                split_q(n0, 0)
                dve.wait_ge(s["q_hi_kept"], n0 + 1)
                dve.tensor_tensor(q_lo[:, 0, :], q_rot[:, :], f32(q_hi[:, 0, :]), ALU.subtract)\
                   .then_inc(s["q_lo_kept"], 1)
                split_k(n0 + 1, 1)
                if not first:
                    finish(b - 1)
                row_max(n0, 0, 0)
                row_max(n0, 0, 1)
                normalise(n0, 0, 0)
                row_max(n0, 0, 2)
                normalise(n0, 0, 1)
                split_q(n0 + 1, 1)
                dve.wait_ge(s["q_done"], n0 + 2)
                split_ws(PAIRS * b + 1)
                row_max(n0, 0, 3)
                normalise(n0, 0, 2)
                normalise(n0, 0, 3)

            def heads(b):
                n0 = H * b
                pair["no"] = PAIRS * b
                period(n0, 0, True, False)
                period(n0 + 1, 1, True, False)
                with dve.Fori(1, PAIRS - 1) as i:
                    pair["no"] = PAIRS * b + i
                    for e in range(2):
                        period(H * b + 2 * i + e, e, False, False)
                for e in range(2):
                    period(n0 + H - 2 + e, e, False, True, more=False)

            def moments(b, t):
                dve.wait_ge(s["y_done"], (H - 1 + TT) * b + H - 1 + t + 1)
                dve.bn_stats(bn[:, t, :], Y[t][:, :]).then_inc(s["bn_done"], 1)
                dve.wait_ge(s["bn_done"], TT * b + t + 1)
                dve.memset(rs[:, t:t + 1], 0.0)
                dve.bn_aggr(mv[:, t, :], bn[:, t, :]).then_inc(s["aggregated"], 1)

            def finish(b):
                dve.wait_ge(s["sd_done"], b + 1)
                dve.reciprocal(rs[:, :], sd[:, :]).then_inc(s["rs_done"], 1)
                dve.wait_ge(s["rs_done"], b + 1)
                dve.wait_ge(s["x1_stored"], 16 * (b + 1))
                for t in range(TT):
                    dve.tensor_scalar(x1[:, t, :], Y[t][:, :], mv[:, t, 0:1], rs[:, t:t + 1], ALU.subtract,
                                      ALU.mult).then_inc(s["x1_done"], 1)

            def end(b, more):
                if more:
                    split_x(b + 1, 0)
                    split_x(b + 1, 1)
                keep_o(H * b + H - 1, 1)
                if more:
                    split_x(b + 1, 2)
                    split_x(b + 1, 3)
                    begin(b + 1, False)
                else:
                    for t in range(TT):
                        moments(b, t)
                    finish(b)

            for d in range(DT):
                split_x(0, d)
            split_ws(0)
            begin(0, True)
            with dve.Fori(0, B - 1) as b:
                heads(b)
                end(b, True)
            heads(B - 1)
            end(B - 1, False)

        @block.gpsimd
        def _(pool):
            pool.wait_ge(s["small_loaded"], 48)

            def split_ws(no):
                pool.wait_ge(s["ws_hi_kept"], no + 1)
                pool.tensor_tensor(ws_lo[:, :], ws_raw[:, :], f32(ws_hi[:, :]), ALU.subtract)\
                    .then_inc(s["ws_lo_kept"], 1)
                pool.wait_ge(s["ws_lo_kept"], no + 1)

            def turn_q(n, e):
                r = P // 2 if e == 0 else 0
                pool.wait_ge(s["q_kept"], n + 1)
                pool.tensor_tensor(q_rot[:, :], q_raw[:, :], tab[:, e, :], ALU.mult).then_inc(s["q_mults"], 1)
                pool.wait_ge(s["q_mults"], 2 * n + 1)
                pool.wait_ge(s["q_swapped"], n + 1)
                pool.tensor_tensor(q_sin[r:r + ROPE, :], q_swap[r:r + ROPE, :], tab[r:r + ROPE, 2, :], ALU.mult)\
                    .then_inc(s["q_mults"], 1)
                pool.wait_ge(s["q_mults"], 2 * n + 2)
                pool.tensor_tensor(q_rot[r:r + ROPE, :], q_rot[r:r + ROPE, :], q_sin[r:r + ROPE, :], ALU.add)\
                    .then_inc(s["q_turned"], 1)
                pool.wait_ge(s["q_turned"], n + 1)

            def split_q(n, e):
                pool.wait_ge(s["q_hi_kept"], n + 1)
                pool.tensor_tensor(q_lo[:, e, :], q_rot[:, :], f32(q_hi[:, e, :]), ALU.subtract)\
                    .then_inc(s["q_lo_kept"], 1)

            def split_k(n, e):
                r = e * NOPE
                pool.wait_ge(s["k_hi_kept"], n + 1)
                pool.tensor_tensor(k_lo[r:r + NOPE, e, :], k_raw[r:r + NOPE, :], f32(k_hi[r:r + NOPE, e, :]),
                                   ALU.subtract).then_inc(s["k_lo_kept"], 1)
                pool.wait_ge(s["k_lo_kept"], n + 1)

            def period(n, e, last, more=True):
                if not last:
                    turn_q(n + 2, e)
                if e == 1 and more:
                    split_ws(pair["no"] + 2)
                if not last:
                    split_k(n + 2, e)
                    split_q(n + 2, e)

            pair = {}

            def begin(b):
                n0 = H * b
                pool.wait_ge(s["c_split"], 2 * b + 1)
                pool.tensor_tensor(c_lo[:, :, :], qc[:, :, QR:QR + KVR], f32(c_hi[:, :, :]), ALU.subtract)\
                    .then_inc(s["c_split"], 1)
                split_k(n0, 0)
                split_k(n0 + 1, 1)
                pool.wait_ge(s["q_lo_kept"], n0 + 1)
                turn_q(n0 + 1, 1)
                split_q(n0 + 1, 1)
                pool.wait_ge(s["q_lo_kept"], n0 + 2)
                split_ws(PAIRS * b + 1)

            def heads(b):
                pair["no"] = PAIRS * b
                for e in range(2):
                    period(H * b + e, e, False)
                with pool.Fori(1, PAIRS - 1) as i:
                    pair["no"] = PAIRS * b + i
                    for e in range(2):
                        period(H * b + 2 * i + e, e, False)

            split_ws(0)
            begin(0)
            with pool.Fori(0, B - 1) as b:
                heads(b)
                begin(b + 1)
            heads(B - 1)


def cross_phase(nc, const, dram):
    ident = const["ident"]
    G = TT + 2
    with ExitStack() as ctx:
        m = Memory(nc, ctx)
        wq_hi, wq_lo = m.split("xwq", [P, DT, D])
        wo_hi, wo_lo = m.split("xwo", [P, DT, D])
        wkv = m.sb("xwkv", [P, CT, 4, D])
        rows = m.sb("xrows", [P, 6, D])
        ln_wb = m.sb("xln_wb", [P, 2, 3, HD])
        masks = m.sb("xmasks", [P, 2])
        kmask = m.sb("kmask", [P, 4])
        vmask = m.sb("vmask", [P, 2, P])
        eps = m.sb("xeps", [P, 2])
        first = m.sb("first", [P, P])
        x_in = m.sb("xx_in", [P, TT, D])
        xbo = const["result"]
        ctx_in = m.sb("ctx_in", [KEYS, CD])
        ctxT = m.sb("ctxT", [P, CT, P])
        xT_hi, xT_lo = m.split("xxT", [P, DT, T])
        ln = m.sb("ln", [P, G, D])
        sq = m.sb("sq", [P, 4, D])
        stat = m.sb("stat", [P, 4, G * XH])
        v_sel = m.sb("v_sel", [P, D])
        v_wide = m.sb("v_wide", [P, DT, 2, P])
        vb_hi, vb_lo = m.split("vb", [P, DT, 2, P])
        kT = m.sb("kT", [P, DT, KEYS])
        kb_hi, kb_lo = m.split("kb", [P, DT, 4, KEYS])
        qT_hi, qT_lo = m.split("xqT", [P, DT, T])
        ex = m.sb("ex", [P, TT, XH, KEYS])
        mx = m.sb("mx", [P, TT, 2, XH])
        sm = m.sb("sm", [P, TT, 2, XH])
        iv = m.sb("iv", [P, TT, 2, XH])
        pT_hi, pT_lo = m.split("xpT", [P, XH // 2, T])
        bn = m.sb("xbn", [P, TT, 6])
        mv = m.sb("xmv", [P, TT, 2])
        sd = m.sb("xsd", [P, TT])
        rs = m.sb("xrs", [P, TT])
        cT_hi, cT_lo = qT_hi, qT_lo
        wo_raw = ex[:, 0:2, :, :].rearrange("p t h k -> p (t h k)").rearrange("p (d n) -> p d n", d=DT)
        k_wide = v_wide[:, :, :, :].rearrange("p d a (h k) -> p d (a h) k", k=KEYS)
        x2 = xbo
        groups = ((0, MAIN, 0), (MAIN, KEYS, 1))

        units = [(slice(TT, TT + 2), slice(TT * XH, G * XH))]
        units += [(slice(t, t + 1), slice(t * XH, (t + 1) * XH)) for t in range(TT)]
        U = len(units)

        def sq_of(u):
            return slice(0, 2) if u == 0 else slice(2 + u % 2, 3 + u % 2)

        G2 = [ctx.enter_context(nc.psum_tensor(f"G{i}", [P, 2, 512], F32)) for i in range(4)]
        Y = [G2[d // 2][:, d % 2, :] for d in range(4)]
        Z = [G2[2 + d // 2][:, d % 2, :] for d in range(4)]

        s = {n: m.sem("x_" + n) for n in (
            "wq_loaded", "wo_loaded", "wkv_loaded", "small_loaded", "w_hi", "w_lo", "set", "first_set",
            "x_loaded", "xbo_done", "turned_x", "turned_ctx", "ctx_kept", "hi", "lo", "q_done", "kv_done",
            "centred", "squared", "stats", "rooted", "scaled", "weighted", "normed",
            "v_masked", "v_steps", "vb_hi", "turned_k", "kT_kept", "k_steps", "kb_hi", "turned_q", "qT_hi", "qT_lo",
            "scores_done", "max_done", "sub_done", "exp_done", "sum_done", "inv_done", "probs_done",
            "turned_p", "pT_hi", "pT_lo", "ctx_done", "cT_hi", "cT_lo", "out_done", "added", "bn_done",
            "aggregated", "sd_done", "rs_done", "x2_done")}
        s["x1_stored"], s["x2_stored"] = const["x1_stored"], const["x2_stored"]

        block = ctx.enter_context(nc.Block())

        @block.sync
        def _(sp):
            sp.sem_inc(s["x2_stored"], 16)
            x1 = dram["x1"].rearrange("b (t p) d -> b p t d", p=P)
            sp.wait_ge(s["x1_stored"], 32)
            sp.dma_start(x_in[:, :, :], x1[0]).then_inc(s["x_loaded"], 16)
            sp.dma_start(ctx_in[:, :], dram["ctx"][0]).then_inc(s["x_loaded"], 16)
            sp.dma_start(wkv[:, :, :, :], dram["xwkv"].rearrange("(k p) j n -> p k j n", p=P))\
              .then_inc(s["wkv_loaded"], 16)
            sp.wait_ge(s["first_set"], 2)
            sp.dma_start(rows[0:1, 0:5, :], dram["xrows"][0:5].unsqueeze(0)).then_inc(s["wkv_loaded"], 16)
            sp.dma_start(ln[:, 0:DT, :], dram["xwq"].rearrange("(k p) n -> p k n", p=P)).then_inc(s["wq_loaded"], 16)
            sp.dma_start(wo_raw, dram["xwo"].rearrange("(k p) n -> p k n", p=P)).then_inc(s["wo_loaded"], 16)
            sp.dma_start(rows[:, 5, :], dram["xrows"][5].partition_broadcast(P)).then_inc(s["small_loaded"], 16)
            sp.dma_start(ln_wb[:, :, :, :], dram["xln_wb"].partition_broadcast(P)).then_inc(s["small_loaded"], 16)
            sp.dma_start(masks[:, :], dram["xmasks"]).then_inc(s["small_loaded"], 16)
            sp.dma_start(kmask[:, :], dram["kmask"]).then_inc(s["small_loaded"], 16)
            sp.dma_start(vmask[:, :, :], dram["vmask"]).then_inc(s["small_loaded"], 16)
            with sp.Fori(0, B - 1) as b:
                sp.wait_ge(s["turned_ctx"], b + 1)
                sp.wait_ge(s["xbo_done"], b + 1)
                sp.wait_ge(s["x1_stored"], 16 * (b + 3))
                sp.dma_start(x_in[:, :, :], x1[b + 1]).then_inc(s["x_loaded"], 16)
                sp.dma_start(ctx_in[:, :], dram["ctx"][b + 1]).then_inc(s["x_loaded"], 16)
                sp.wait_ge(s["x2_done"], TT * (b + 1))
                sp.dma_start(dram["x2"].rearrange("b (t p) d -> b p t d", p=P)[b], x2[:, :, :])\
                  .then_inc(s["x2_stored"], 16)
            sp.wait_ge(s["x2_done"], TT * B)
            sp.dma_start(dram["x2"].rearrange("b (t p) d -> b p t d", p=P)[B - 1], x2[:, :, :])\
              .then_inc(s["x2_stored"], 16)

        @block.tensor
        def _(pe):

            def product(out, pairs, begun=False):
                steps = [p for lhsT, rhs in pairs for p in three(lhsT, rhs)]
                for j, (lhsT, rhs) in enumerate(steps):
                    mm = pe.matmul(out, lhsT, rhs, start=j == 0 and not begun, stop=j == len(steps) - 1)
                return mm

            def bias(out, row):
                pe.matmul(out, first[:, :], rows[:, row, :], start=True, stop=False)

            def turn_x(b, d):
                for t in range(TT):
                    mm = pe.transpose(Y[d][:, t * P:(t + 1) * P], x_in[:, t, d * P:(d + 1) * P], ident[:, :])
                mm.then_inc(s["turned_x"], 1)

            def turn_ctx():
                for k in range(CT):
                    mm = pe.transpose(Y[DT - 1][:, k * KEYS:(k + 1) * KEYS], ctx_in[:, k * P:(k + 1) * P],
                                      ident[0:KEYS, 0:KEYS])
                mm.then_inc(s["turned_ctx"], 1)

            def project_ctx(b, j):
                if j == 0:
                    pe.wait_ge(s["ctx_kept"], b + 1)
                pe.wait_ge(s["lo"], DT * b + j + 1)
                bias(Y[j], 1 + j)
                for k in range(CT):
                    mm = pe.matmul(Y[j], ctxT[:, k, :], wkv[:, k, j, :], start=False, stop=k == CT - 1)
                mm.then_inc(s["kv_done"], 1)

            def project_q(b, t):
                if t == 0:
                    pe.wait_ge(s["w_lo"], 1)
                    pe.wait_ge(s["lo"], DT * (b + 1))
                bias(Z[t], 0)
                product(Z[t], [((xT_hi[:, d, t * P:(t + 1) * P], xT_lo[:, d, t * P:(t + 1) * P]),
                                (wq_hi[:, d, :], wq_lo[:, d, :])) for d in range(DT)], begun=True)\
                    .then_inc(s["q_done"], 1)

            def turn_k():
                for k in range(DT):
                    for g in range(2):
                        mm = pe.transpose(Y[0][:, (2 * k + g) * KEYS:(2 * k + g + 1) * KEYS],
                                          ln[0:KEYS, TT + g, k * P:(k + 1) * P], ident[0:KEYS, 0:KEYS])
                mm.then_inc(s["turned_k"], 1)

            def turn_q(b, t):
                if t == 0:
                    pe.wait_ge(s["kT_kept"], b + 1)
                pe.wait_ge(s["normed"], (U + 1) * b + 3 + t)
                for d in range(DT):
                    mm = pe.transpose(Y[t][:, d * P:(d + 1) * P], ln[:, t, d * P:(d + 1) * P], ident[:, :])
                mm.then_inc(s["turned_q"], 1)

            def scores(b, t):
                if t < 2:
                    pe.wait_ge(s["centred"], U * b + 3 + 2 * t)
                    pe.wait_ge(s["k_steps"], 2 * (b + 1))
                    pe.wait_ge(s["qT_lo"], TT * b + t + 1)
                else:
                    pe.wait_ge(s["qT_lo"], TT * (b + 1))
                for d in range(DT):
                    mm = product(G2[(t + 2) % 4][:, d // 2, (d % 2) * 4 * KEYS:(d % 2 + 1) * 4 * KEYS],
                                 [((qT_hi[:, d, t * P:(t + 1) * P], qT_lo[:, d, t * P:(t + 1) * P]),
                                   (kb_hi[:, d, :, :].rearrange("p h k -> p (h k)"),
                                    kb_lo[:, d, :, :].rearrange("p h k -> p (h k)")))])
                mm.then_inc(s["scores_done"], 1)

            def turn_probs(b, t):
                pe.wait_ge(s["probs_done"], 2 * TT * b + 2 * t + 2)
                if t >= 2:
                    pe.wait_ge(s["pT_lo"], TT * b + t - 1)
                for h2 in range(XH // 2):
                    mm = pe.transpose(
                        G2[2 + t % 2][:, h2 // 4, (h2 % 4) * P:(h2 % 4 + 1) * P],
                        ex[:, t, 2 * h2:2 * h2 + 2, :].rearrange("p h k -> p (h k)"), ident[:, :])
                mm.then_inc(s["turned_p"], 1)

            def attend(b, d):
                if d == 0:
                    pe.wait_ge(s["pT_lo"], TT * (b + 1))
                product(Z[d], [((vb_hi[:, d, j, :], vb_lo[:, d, j, :]),
                                (pT_hi[:, 2 * d + j, :], pT_lo[:, 2 * d + j, :])) for j in range(2)])\
                    .then_inc(s["ctx_done"], 1)

            def output(b, t):
                product(Y[t], [((cT_hi[:, d, t * P:(t + 1) * P], cT_lo[:, d, t * P:(t + 1) * P]),
                                (wo_hi[:, d, :], wo_lo[:, d, :])) for d in range(DT)]).then_inc(s["out_done"], 1)

            def batch(b, more):
                turn_q(b, 0)
                scores(b, 0)
                turn_q(b, 1)
                scores(b, 1)
                turn_q(b, 2)
                turn_q(b, 3)
                scores(b, 2)
                turn_probs(b, 0)
                scores(b, 3)
                turn_probs(b, 1)
                if more:
                    pe.wait_ge(s["x_loaded"], 32 * (b + 2))
                    pe.wait_ge(s["sub_done"], 2 * TT * b + 6)
                    turn_x(b + 1, 0)
                    pe.wait_ge(s["sub_done"], 2 * TT * b + 8)
                    turn_x(b + 1, 1)
                    turn_ctx()
                    turn_x(b + 1, 2)
                turn_probs(b, 2)
                if more:
                    pe.wait_ge(s["ctx_kept"], b + 2)
                    turn_x(b + 1, 3)
                turn_probs(b, 3)
                if more:
                    project_ctx(b + 1, 0)
                    project_ctx(b + 1, 1)
                for d in range(DT):
                    attend(b, d)
                if more:
                    project_ctx(b + 1, 2)
                    project_ctx(b + 1, 3)
                pe.wait_ge(s["w_lo"], 2)
                pe.wait_ge(s["cT_lo"], DT * (b + 1))
                for t in range(TT):
                    if more:
                        if t == 0:
                            pe.wait_ge(s["centred"], U * (b + 1) + 1)
                        elif t == 2:
                            pe.wait_ge(s["v_masked"], b + 2)
                        elif t == 3:
                            pe.wait_ge(s["v_steps"], 3 * (b + 1) + 1)
                            pe.wait_ge(s["normed"], (U + 1) * (b + 1) + 2)
                            pe.wait_ge(s["added"], TT * b + 1)
                    output(b, t)
                    if more:
                        if t == TT - 1:
                            turn_k()
                        project_q(b + 1, t)

            pe.wait_ge(s["x_loaded"], 32)
            turn_x(0, 0)
            turn_x(0, 1)
            turn_ctx()
            turn_x(0, 2)
            pe.wait_ge(s["ctx_kept"], 1)
            turn_x(0, 3)
            pe.wait_ge(s["wkv_loaded"], 32)
            pe.wait_ge(s["first_set"], 3)
            for j in range(4):
                project_ctx(0, j)
            for t in range(TT):
                if t == TT - 1:
                    pe.wait_ge(s["normed"], 2)
                    turn_k()
                project_q(0, t)
            with pe.Fori(0, B - 1) as b:
                batch(b, True)
            batch(B - 1, False)

        @block.scalar
        def _(act):
            def keep_x(b, d):
                act.wait_ge(s["turned_x"], DT * b + d + 1)
                act.activation(xT_hi[:, d, :], Y[d], ACT.Copy).then_inc(s["hi"], 1)

            def keep_ctx(b):
                act.wait_ge(s["turned_ctx"], b + 1)
                for c in range(2):
                    op = act.activation(ctxT[:, :, c * KEYS:(c + 1) * KEYS],
                                        Y[DT - 1][:, 0:CT * KEYS].rearrange("p (k n) -> p k n", n=KEYS), ACT.Copy)
                op.then_inc(s["ctx_kept"], 1)

            def square(b, u):
                g, _ = units[u]
                act.wait_ge(s["centred"], U * b + u + 1)
                act.activation(sq[:, sq_of(u), :], ln[:, g, :], ACT.Square).then_inc(s["squared"], 1)

            def root(b, u):
                _, c = units[u]
                act.wait_ge(s["stats"], 2 * U * b + 2 * u + 2)
                act.activation(stat[:, 2, c], stat[:, 1, c], ACT.Sqrt, bias=eps[:, 0:1], scale=1.0 / HD)\
                   .then_inc(s["rooted"], 1)

            def keep_q(b, t):
                act.wait_ge(s["turned_q"], TT * b + t + 1)
                act.activation(qT_hi[:, :, t * P:(t + 1) * P], Y[t].rearrange("p (d q) -> p d q", q=P), ACT.Copy)\
                   .then_inc(s["qT_hi"], 1)

            def exponent(b, t):
                act.wait_ge(s["sub_done"], 2 * TT * b + 2 * t + 2)
                act.activation(ex[:, t, :, :], ex[:, t, :, :], ACT.Exp, scale=X_SCALE)\
                   .then_inc(s["exp_done"], 1)

            def keep_turned(b, t):
                act.wait_ge(s["turned_p"], TT * b + t + 1)
                act.activation(pT_hi[:, :, t * P:(t + 1) * P],
                               G2[2 + t % 2][:, :, :].rearrange("p a (h q) -> p (a h) q", q=P), ACT.Copy)\
                   .then_inc(s["pT_hi"], 1)

            def mask_values(b):
                act.wait_ge(s["kv_done"], 4 * b + 3)
                act.activation(v_sel[:, :], Y[2], ACT.Copy, scale=masks[:, 0:1]).then_inc(s["v_masked"], 1)

            def keep_values(b):
                act.wait_ge(s["v_steps"], 3 * b + 2)
                act.activation(vb_hi[:, :, :, :], v_wide[:, :, :, :], ACT.Copy).then_inc(s["vb_hi"], 1)

            def keep_turned_k(b):
                act.wait_ge(s["turned_k"], b + 1)
                for o, e, g in groups:
                    op = act.activation(kT[:, :, o:e],
                                        Y[0].rearrange("p (d g k) -> p d g k", g=2, k=KEYS)[:, :, g, o:e], ACT.Copy)
                op.then_inc(s["kT_kept"], 1)

            def keep_keys(b):
                act.wait_ge(s["k_steps"], 2 * b + 1)
                act.activation(kb_hi[:, :, :, :], k_wide[:, :, :, :], ACT.Copy).then_inc(s["kb_hi"], 1)

            def keep_attended(b, d):
                act.wait_ge(s["ctx_done"], DT * b + d + 1)
                act.activation(cT_hi[:, d, :], Z[d], ACT.Copy).then_inc(s["cT_hi"], 1)

            def deviation(b):
                act.wait_ge(s["aggregated"], TT * (b + 1))
                act.activation(sd[:, :], mv[:, :, 1], ACT.Sqrt, bias=eps[:, 1:2], scale=1.0).then_inc(s["sd_done"], 1)

            def begin(b, first):
                square(b, 0)
                if not first:
                    keep_attended(b - 1, 0)
                    keep_attended(b - 1, 1)
                root(b, 0)
                if not first:
                    keep_attended(b - 1, 2)
                    keep_attended(b - 1, 3)
                mask_values(b)
                keep_values(b)
                square(b, 1)
                root(b, 1)
                square(b, 2)
                root(b, 2)
                square(b, 3)
                keep_turned_k(b)
                root(b, 3)
                keep_keys(b)
                if not first:
                    deviation(b - 1)
                square(b, 4)

            def batch(b, more):
                keep_q(b, 0)
                root(b, 4)
                keep_q(b, 1)
                exponent(b, 0)
                keep_q(b, 2)
                exponent(b, 1)
                keep_q(b, 3)
                exponent(b, 2)
                keep_turned(b, 0)
                exponent(b, 3)
                keep_turned(b, 1)
                if more:
                    keep_x(b + 1, 0)
                    keep_x(b + 1, 1)
                    keep_ctx(b + 1)
                    keep_x(b + 1, 2)
                keep_turned(b, 2)
                if more:
                    keep_x(b + 1, 3)
                keep_turned(b, 3)
                if more:
                    begin(b + 1, False)
                else:
                    for d in range(DT):
                        keep_attended(b, d)
                    deviation(b)

            keep_x(0, 0)
            keep_x(0, 1)
            keep_ctx(0)
            keep_x(0, 2)
            keep_x(0, 3)
            act.wait_ge(s["wq_loaded"], 16)
            act.activation(wq_hi[:, :, :], ln[:, 0:DT, :], ACT.Copy).then_inc(s["w_hi"], 1)
            act.wait_ge(s["wo_loaded"], 16)
            act.activation(wo_hi[:, :, :], wo_raw, ACT.Copy).then_inc(s["w_hi"], 1)
            act.wait_ge(s["set"], 1)
            act.wait_ge(s["small_loaded"], 80)
            begin(0, True)
            with act.Fori(0, B - 1) as b:
                batch(b, True)
            batch(B - 1, False)

        @block.vector
        def _(dve):
            dve.memset(eps[:, 0:1], X_EPS)
            dve.memset(eps[:, 1:2], LN_EPS).then_inc(s["set"], 1)

            def heads(ap):
                return ap.rearrange("p g (h d) -> p (g h) d", d=HD)

            def wide(ap, n):
                return ap.unsqueeze(2).to_broadcast([P, ap.shape[1], n])

            def split_x(b, d):
                dve.wait_ge(s["hi"], DT * b + d + 1)
                dve.tensor_tensor(xT_lo[:, d, :], Y[d], f32(xT_hi[:, d, :]), ALU.subtract).then_inc(s["lo"], 1)

            def centre(b, u):
                g, c = units[u]
                if u == 0:
                    dve.wait_ge(s["kv_done"], 4 * b + 2)
                    src = G2[0][:, :, :].rearrange("p a (h d) -> p (a h) d", d=HD)
                else:
                    dve.wait_ge(s["q_done"], TT * b + u)
                    src = Z[u - 1].rearrange("p (h d) -> p h d", d=HD)
                dve.tensor_reduce(stat[:, 0, c], src, AX.X, ALU.add).then_inc(s["stats"], 1)
                dve.wait_ge(s["stats"], 2 * U * b + 2 * u + 1)
                dve.scalar_tensor_tensor(out=heads(ln[:, g, :]), in0=wide(stat[:, 0, c], HD), scalar=-1.0 / HD,
                                         in1=src, op0=ALU.mult, op1=ALU.add).then_inc(s["centred"], 1)

            def sum_squares(b, u):
                g, c = units[u]
                dve.wait_ge(s["squared"], U * b + u + 1)
                dve.tensor_reduce(stat[:, 1, c], heads(sq[:, sq_of(u), :]), AX.X, ALU.add).then_inc(s["stats"], 1)

            def scale(b, u):
                g, c = units[u]
                dve.wait_ge(s["rooted"], U * b + u + 1)
                dve.reciprocal(stat[:, 3, c], stat[:, 2, c]).then_inc(s["scaled"], 1)
                dve.wait_ge(s["scaled"], 2 * U * b + 2 * u + 1)
                dve.tensor_tensor(heads(ln[:, g, :]), heads(ln[:, g, :]), wide(stat[:, 3, c], HD), ALU.mult)\
                   .then_inc(s["scaled"], 1)

            def split_q(b, t):
                dve.wait_ge(s["qT_hi"], TT * b + t + 1)
                dve.tensor_tensor(qT_lo[:, :, t * P:(t + 1) * P], Y[t].rearrange("p (d q) -> p d q", q=P),
                                  f32(qT_hi[:, :, t * P:(t + 1) * P]), ALU.subtract).then_inc(s["qT_lo"], 1)

            def shift(b, t):
                scores = G2[(t + 2) % 4][:, :, :].rearrange("p a (h k) -> p (a h) k", k=KEYS)
                dve.wait_ge(s["scores_done"], TT * b + t + 1)
                for o, e, g in groups:
                    dve.tensor_reduce(mx[:, t, g, :], scores[:, :, o:e], AX.X, ALU.max)\
                       .then_inc(s["max_done"], 1)
                for o, e, g in groups:
                    dve.wait_ge(s["max_done"], 2 * TT * b + 2 * t + 1 + g)
                    dve.tensor_tensor(ex[:, t, :, o:e], scores[:, :, o:e], wide(mx[:, t, g, :], e - o),
                                      ALU.subtract).then_inc(s["sub_done"], 1)

            def invert(b, t):
                dve.wait_ge(s["exp_done"], TT * b + t + 1)
                for o, e, g in groups:
                    dve.tensor_reduce(sm[:, t, g, :], ex[:, t, :, o:e], AX.X, ALU.add)\
                       .then_inc(s["sum_done"], 1)
                dve.wait_ge(s["sum_done"], 2 * TT * b + 2 * t + 2)
                dve.reciprocal(iv[:, t, :, :], sm[:, t, :, :]).then_inc(s["inv_done"], 1)

            def keep_turned(b, t):
                dve.wait_ge(s["pT_hi"], TT * b + t + 1)
                dve.tensor_tensor(pT_lo[:, :, t * P:(t + 1) * P],
                                  G2[2 + t % 2][:, :, :].rearrange("p a (h q) -> p (a h) q", q=P),
                                  f32(pT_hi[:, :, t * P:(t + 1) * P]), ALU.subtract).then_inc(s["pT_lo"], 1)

            def join_values(b):
                dve.wait_ge(s["v_masked"], b + 1)
                dve.wait_ge(s["kv_done"], 4 * b + 4)
                dve.scalar_tensor_tensor(out=v_sel[:, :], in0=Y[3], scalar=masks[:, 1:2], in1=v_sel[:, :],
                                         op0=ALU.mult, op1=ALU.add).then_inc(s["v_steps"], 1)

            def spread_values(b):
                dve.wait_ge(s["v_steps"], 3 * b + 1)
                dve.tensor_tensor(
                    v_wide[:, :, :, :],
                    v_sel[:, :].rearrange("p (d c) -> p d c", d=DT).unsqueeze(2).to_broadcast([P, DT, 2, P]),
                    vmask[:, :, :].unsqueeze(1).to_broadcast([P, DT, 2, P]), ALU.mult).then_inc(s["v_steps"], 1)

            def split_values(b):
                dve.wait_ge(s["vb_hi"], b + 1)
                dve.tensor_tensor(vb_lo[:, :, :, :], v_wide[:, :, :, :], f32(vb_hi[:, :, :, :]), ALU.subtract)\
                   .then_inc(s["v_steps"], 1)

            def spread_keys(b):
                dve.wait_ge(s["kT_kept"], b + 1)
                dve.wait_ge(s["v_steps"], 3 * b + 3)
                dve.tensor_tensor(k_wide[:, :, :, :], kT[:, :, :].unsqueeze(2).to_broadcast([P, DT, 4, KEYS]),
                                  kmask[:, :].unsqueeze(1).unsqueeze(3).to_broadcast([P, DT, 4, KEYS]), ALU.mult)\
                   .then_inc(s["k_steps"], 1)

            def split_keys(b):
                dve.wait_ge(s["kb_hi"], b + 1)
                dve.tensor_tensor(kb_lo[:, :, :, :], k_wide[:, :, :, :], f32(kb_hi[:, :, :, :]), ALU.subtract)\
                   .then_inc(s["k_steps"], 1)

            def split_attended(b, d):
                dve.wait_ge(s["cT_hi"], DT * b + d + 1)
                dve.tensor_tensor(cT_lo[:, d, :], Z[d], f32(cT_hi[:, d, :]), ALU.subtract).then_inc(s["cT_lo"], 1)

            def residual(b, t):
                dve.wait_ge(s["out_done"], TT * b + t + 1)
                dve.tensor_tensor(x2[:, t, :], Y[t], xbo[:, t, :], ALU.add).then_inc(s["added"], 1)
                dve.wait_ge(s["added"], TT * b + t + 1)
                dve.bn_stats(bn[:, t, :], x2[:, t, :]).then_inc(s["bn_done"], 1)
                dve.wait_ge(s["bn_done"], TT * b + t + 1)
                dve.memset(rs[:, t:t + 1], 0.0)
                dve.bn_aggr(mv[:, t, :], bn[:, t, :]).then_inc(s["aggregated"], 1)

            def finish(b):
                dve.wait_ge(s["sd_done"], b + 1)
                dve.reciprocal(rs[:, :], sd[:, :]).then_inc(s["rs_done"], 1)
                dve.wait_ge(s["rs_done"], b + 1)
                for t in range(TT):
                    dve.tensor_scalar(x2[:, t, :], x2[:, t, :], mv[:, t, 0:1], rs[:, t:t + 1], ALU.subtract,
                                      ALU.mult).then_inc(s["x2_done"], 1)

            def begin(b, first):
                centre(b, 0)
                if not first:
                    split_attended(b - 1, 0)
                sum_squares(b, 0)
                if not first:
                    split_attended(b - 1, 1)
                scale(b, 0)
                if not first:
                    split_attended(b - 1, 2)
                    split_attended(b - 1, 3)
                join_values(b)
                spread_values(b)
                if not first:
                    residual(b - 1, 0)
                split_values(b)
                centre(b, 1)
                for t in range(1, TT):
                    sum_squares(b, t)
                    if not first:
                        residual(b - 1, t)
                    if t == TT - 1:
                        spread_keys(b)
                    scale(b, t)
                    if t < TT - 1:
                        centre(b, t + 1)
                if not first:
                    finish(b - 1)
                centre(b, 4)
                split_keys(b)
                sum_squares(b, 4)

            def batch(b, more):
                split_q(b, 0)
                scale(b, 4)
                split_q(b, 1)
                shift(b, 0)
                split_q(b, 2)
                shift(b, 1)
                split_q(b, 3)
                invert(b, 0)
                shift(b, 2)
                invert(b, 1)
                keep_turned(b, 0)
                shift(b, 3)
                invert(b, 2)
                keep_turned(b, 1)
                invert(b, 3)
                if more:
                    for d in range(DT - 1):
                        split_x(b + 1, d)
                keep_turned(b, 2)
                if more:
                    split_x(b + 1, DT - 1)
                keep_turned(b, 3)
                if more:
                    begin(b + 1, False)
                else:
                    for d in range(DT):
                        split_attended(b, d)
                    for t in range(TT):
                        residual(b, t)
                    finish(b)

            for d in range(DT):
                split_x(0, d)
            dve.wait_ge(s["w_hi"], 1)
            dve.tensor_tensor(wq_lo[:, :, :], ln[:, 0:DT, :], f32(wq_hi[:, :, :]), ALU.subtract).then_inc(s["w_lo"], 1)
            dve.wait_ge(s["w_hi"], 2)
            dve.tensor_tensor(wo_lo[:, :, :], wo_raw, f32(wo_hi[:, :, :]), ALU.subtract).then_inc(s["w_lo"], 1)
            dve.wait_ge(s["small_loaded"], 80)
            dve.wait_ge(s["w_lo"], 2)
            begin(0, True)
            with dve.Fori(0, B - 1) as b:
                batch(b, True)
            batch(B - 1, False)

        @block.gpsimd
        def _(pool):
            pool.memset(first[:, :], 0.0).then_inc(s["first_set"], 1)
            pool.wait_ge(s["first_set"], 1)
            pool.memset(rows[:, 0:5, :], 0.0).then_inc(s["first_set"], 1)
            pool.wait_ge(s["first_set"], 2)
            pool.memset(first[0:1, :], 1.0).then_inc(s["first_set"], 1)
            pool.wait_ge(s["small_loaded"], 80)
            pool.wait_ge(s["x1_stored"], 16 * (B + 1))
            def normalise(b):
                parts = [(ln[:, TT + g, :], 1 + g, 0) for g in range(2)] + \
                    [(ln[:, t, :], 0, 1 + t) for t in range(TT)]
                for step, row in (("weighted", 0), ("normed", 1)):
                    for i, (part, c, u) in enumerate(parts[0:2]):
                        pool.wait_ge(s["scaled"], 2 * U * b + 2)
                        if row:
                            pool.wait_ge(s["weighted"], (U + 1) * b + i + 1)
                        part = part.rearrange("p (h d) -> p h d", d=HD)
                        pool.tensor_tensor(part, part, ln_wb[:, row, c:c + 1, :].to_broadcast([P, XH, HD]),
                                           (ALU.mult, ALU.add)[row]).then_inc(s[step], 1)
                for i, (part, c, u) in enumerate(parts[2:]):
                    part = part.rearrange("p (h d) -> p h d", d=HD)
                    pool.wait_ge(s["scaled"], 2 * U * b + 2 * u + 2)
                    pool.tensor_tensor(part, part, ln_wb[:, 0, c:c + 1, :].to_broadcast([P, XH, HD]), ALU.mult)\
                        .then_inc(s["weighted"], 1)
                    pool.wait_ge(s["weighted"], (U + 1) * b + 3 + i)
                    pool.tensor_tensor(part, part, ln_wb[:, 1, c:c + 1, :].to_broadcast([P, XH, HD]), ALU.add)\
                        .then_inc(s["normed"], 1)

            def residual(b):
                pool.wait_ge(s["x2_stored"], 16 * (b + 1))
                pool.wait_ge(s["x_loaded"], 32 * (b + 1))
                pool.tensor_tensor(xbo[:, :, :], x_in[:, :, :], rows[:, 5:6, :].to_broadcast([P, TT, D]), ALU.add)\
                    .then_inc(s["xbo_done"], 1)

            def probabilities(b):
                for t in range(TT):
                    pool.wait_ge(s["inv_done"], TT * b + t + 1)
                    for o, e, g in groups:
                        pool.tensor_tensor(ex[:, t, :, o:e], ex[:, t, :, o:e],
                                           iv[:, t, g, :].unsqueeze(2).to_broadcast([P, XH, e - o]), ALU.mult)\
                            .then_inc(s["probs_done"], 1)

            normalise(0)
            with pool.Fori(0, B - 1) as b:
                residual(b)
                probabilities(b)
                normalise(b + 1)
            residual(B - 1)
            probabilities(B - 1)


def ffn_phase(nc, const, dram):
    ident = const["ident"]
    with ExitStack() as ctx:
        m = Memory(nc, ctx)
        acc = m.sb("acc", [P, B * TT, D])
        xT_hi, xT_lo = m.split("fxT", [P, DT, B * T])
        gu_raw = m.sb("gu_raw", [P, DT, 2 * EH])
        gu_hi, gu_lo = m.split("gu", [P, 2, DT, 2 * EH])
        dn_raw = m.sb("dn_raw", [P, HT, D])
        dn_hi, dn_lo = m.split("dn", [P, 2, HT, D])
        silu = m.sb("silu", [P, HT, T])
        h = m.sb("h", [P, HT, T])
        h_hi, h_lo = m.split("fh", [P, 2, HT, T])
        bias_raw = m.sb("bias_raw", [P, 2, HT])
        bias = m.sb("bias", [P, 2, 2, HT])
        bg = m.sb("bg", [P, NG])
        before = m.sb("before", [P, NG, NG])
        gate = m.sb("gate", [P, B * TT, NG])
        keep = m.sb("keep", [P, B * TT, NG])
        row = m.sb("row", [P, 3, B * TT])
        w = m.sb("w", [P, B * TT, NG])
        w3 = m.sb("w3", [P, B * TT, QUAD])
        quads = m.sb("quads", [P, 4])
        bd_raw = m.sb("bd_raw", [P, D])
        bd_hi = m.sb("bd_hi", [P, D], F32R)
        bd_mask = m.sb("bd_mask", [P, 2])
        bd3 = m.sb("bd3", [P, D], F32R)
        wT3 = m.sb("wT3", [P, B * TT, P], F32R)
        eps = m.sb("feps", [P, 1])
        mv = m.sb("fmv", [P, B * TT, 2])
        sd = m.sb("fsd", [P, B * TT])
        rs = m.sb("frs", [P, B * TT])
        compared = const["result"][:, :, :].rearrange("p t d -> p (t d)").rearrange("p (j n) -> p j n", j=2)
        pairs, ties = [compared[:, j, :].rearrange("p (n i j) -> p n i j", i=NG, j=NG) for j in range(2)]
        w_wide = compared[:, 0, :].rearrange("p (n q r) -> p n q r", q=4, r=QUAD)
        w_turned = compared[:, 1, :]
        w_hi = bd3[:, 0:B * TT * NG].rearrange("p (n e) -> p n e", e=NG)
        wg_wide, wg_hi, wg_lo = [b.rearrange("p (k n) -> p k n", k=DT)
                                 for b in (h[:, 0, :], h_hi[:, 0, 0, :], h_lo[:, 0, 0, :])]
        bn = keep[:, :, 0:6]

        GU = m.banks("GU", 4)
        DN = m.banks("DN", TT)

        s = {n: m.sem("f_" + n) for n in (
            "x_loaded0", "x_loaded1", "x_loaded2", "x_loaded3", "wg_loaded", "small_loaded", "gu_loaded", "dn_loaded", "set",
            "turned_x", "xT_hi", "xT_lo", "wg_split", "logits_done", "logits_kept",
            "gate_done", "route", "routed", "w_split", "w_spread", "w_blocks", "wT3_kept", "bd_steps",
            "gu_hi", "gu_lo", "dn_hi", "dn_lo",
            "gate_up_done", "silu_done", "h_done", "h_hi", "h_lo", "down_done", "acc_done",
            "bn_done", "aggregated", "sd_done", "rs_done", "out_done", "stored")}

        EXPERTS = N_EXP - 2
        block = ctx.enter_context(nc.Block())

        @block.sync
        def _(sp):
            x2 = dram["x2"].rearrange("b (t p) d -> b p t d", p=P)
            def load_x(c):
                sp.wait_ge(const["x2_stored"], 16 * (c + 2))
                sp.dma_start(acc[:, c * TT:(c + 1) * TT, :], x2[c]).then_inc(s[f"x_loaded{c}"], 16)

            load_x(0)
            sp.wait_ge(s["set"], 3)
            sp.dma_start(wg_wide[:, :, 0:NG], dram["wg"].rearrange("(k p) n -> p k n", p=P))              .then_inc(s["wg_loaded"], 16)
            load_x(1)
            for dst, name in ((quads[:, :], "quads"), (bd_raw[:, :], "bd"), (bd_mask[:, :], "bd_mask")):
                sp.dma_start(dst, dram[name]).then_inc(s["small_loaded"], 16)
            sp.dma_start(bg[:, :], dram["bg"].partition_broadcast(P)).then_inc(s["small_loaded"], 16)
            sp.dma_start(before[:, :, :], dram["before"].partition_broadcast(P)).then_inc(s["small_loaded"], 16)
            load_x(2)

            def load(k, gu, dn, width=2 * EH):
                sp.dma_start(bias_raw[:, :, :], dram["fbias"][k]).then_inc(s["gu_loaded"], 16)
                sp.dma_start(gu_raw[:, :, 0:width], gu.rearrange("(k p) n -> p k n", p=P)).then_inc(s["gu_loaded"], 16)
                sp.dma_start(dn_raw[:, :, :], dn.rearrange("(k p) n -> p k n", p=P)).then_inc(s["dn_loaded"], 16)

            load(0, dram["wgu"][0], dram["wdn"][0])
            load_x(3)
            with sp.Fori(1, EXPERTS) as k:
                sp.wait_ge(s["gu_lo"], k)
                sp.wait_ge(s["dn_lo"], k)
                load(k, dram["wgu"][k], dram["wdn"][k])
            for j in range(2):
                sp.wait_ge(s["gu_lo"], EXPERTS + j)
                sp.wait_ge(s["dn_lo"], EXPERTS + j)
                load(EXPERTS + j, dram["wsu"][j], dram["wsd"][j], EH)
            for c in range(B):
                sp.wait_ge(s["out_done"], TT * (c + 1))
                sp.dma_start(dram["out"][c].rearrange("(t p) d -> p t d", p=P), acc[:, c * TT:(c + 1) * TT, :])\
                  .then_inc(s["stored"], 16)
            sp.wait_ge(s["stored"], 16 * B)

        @block.tensor
        def _(pe):
            def turn_x(c):
                pe.wait_ge(s[f"x_loaded{c}"], 16)
                for d in range(DT):
                    if c:
                        pe.wait_ge(s["xT_lo"], DT * (c - 1) + d + 1)
                    for t in range(TT):
                        mm = pe.transpose(GU[d][:, t * P:(t + 1) * P], acc[:, c * TT + t, d * P:(d + 1) * P],
                                          ident[:, :])
                    mm.then_inc(s["turned_x"], 1)

            def logits(c):
                pe.wait_ge(s["xT_lo"], DT * (c + 1))
                if c >= 2:
                    pe.wait_ge(s["logits_kept"], c - 1)
                for d in range(DT):
                    for j, (lhsT, rhs) in enumerate(three(
                            (wg_hi[:, d, :], wg_lo[:, d, :]),
                            (xT_hi[:, d, c * T:(c + 1) * T], xT_lo[:, d, c * T:(c + 1) * T]))):
                        mm = pe.matmul(DN[1 + c % 2][:, :], lhsT, rhs, start=d == 0 and j == 0,
                                       stop=d == DT - 1 and j == 2)
                mm.then_inc(s["logits_done"], 1)

            def turn_logits(c):
                pe.wait_ge(s["logits_kept"], c + 1)
                for n in range(c * TT, (c + 1) * TT):
                    t = n % TT
                    mm = pe.transpose(DN[0][:, n * NG:(n + 1) * NG], silu[0:NG, c % 2, t * P:(t + 1) * P],
                                      ident[0:NG, 0:NG])
                mm.then_inc(s["gate_done"], 1)

            turn_x(0)
            pe.wait_ge(s["wg_split"], 2)
            for c in range(1, B + 1):
                if c < B:
                    turn_x(c)
                logits(c - 1)
                if c >= 2:
                    turn_logits(c - 2)
            turn_logits(B - 1)

            def gate_up(n, k, j, c, a, shared, first=False):
                if c == 0 and a == 0:
                    pe.wait_ge(s["gu_lo"], k + 1)
                if not first:
                    pe.wait_ge(s["silu_done"], 2 * n + a - 1)
                    if not shared:
                        pe.wait_ge(s["h_done"], 2 * n + a - 1)
                for u in range(1 if shared else 2):
                    o = u * EH + a * P
                    steps = [p for d in range(DT) for p in three(
                        (gu_hi[:, j, d, o:o + P], gu_lo[:, j, d, o:o + P]),
                        (xT_hi[:, d, c * T:(c + 1) * T], xT_lo[:, d, c * T:(c + 1) * T]))]
                    for i, (lhsT, rhs) in enumerate(steps):
                        mm = pe.matmul(GU[2 * a + u][:, :], lhsT, rhs, start=i == 0, stop=i == len(steps) - 1)
                mm.then_inc(s["gate_up_done"], 1)

            def down(n, k, j, c, t, bias=False, first=False):
                if t == 0:
                    pe.wait_ge(s["h_lo"], 2 * n + 2)
                    if c == 0:
                        pe.wait_ge(s["dn_lo"], k + 1)
                if not first:
                    pe.wait_ge(s["acc_done"], TT * (n - 1) + t + 1)
                elif t == 0:
                    pe.wait_ge(s["route"], 1)
                steps = [p for a in range(HT) for p in three(
                    (h_hi[:, c % 2, a, t * P:(t + 1) * P], h_lo[:, c % 2, a, t * P:(t + 1) * P]),
                    (dn_hi[:, j, a, :], dn_lo[:, j, a, :]))]
                if bias:
                    if c == 0 and t == 0:
                        pe.wait_ge(s["wT3_kept"], 2)
                        pe.wait_ge(s["bd_steps"], 4)
                    steps.append((wT3[:, c * TT + t, :], bd3[:, :]))
                for i, (lhsT, rhs) in enumerate(steps):
                    mm = pe.matmul(DN[t][:, :], lhsT, rhs, start=i == 0, stop=i == len(steps) - 1)
                mm.then_inc(s["down_done"], 1)

            def steps(n0, k0, shared, next_shared, first=False, last=False):
                for j in range(2):
                    for c in range(B):
                        n = n0 + j * B + c
                        end = j == 1 and c == B - 1
                        nj, nc_ = (j, c + 1) if c < B - 1 else (1 - j, 0)
                        nk = k0 + j + (c == B - 1)
                        for a in range(HT):
                            if not (last and end):
                                gate_up(n + 1, nk, nj, nc_, a, next_shared if end else shared)
                            for t in (2 * a, 2 * a + 1):
                                down(n, k0 + j, j, c, t, bias=shared and j == 1, first=first and j == 0 and c == 0)

            for a in range(HT):
                gate_up(0, 0, 0, 0, a, False, first=True)
            steps(0, 0, False, False, first=True)
            with pe.Fori(1, EXPERTS // 2 - 1) as i:
                steps(2 * B * i, 2 * i, False, False)
            steps(2 * B * (EXPERTS // 2 - 1), EXPERTS - 2, False, True)
            steps(B * EXPERTS, EXPERTS, True, True, last=True)

        @block.scalar
        def _(act):
            for c in range(B + 1):
                for d in range(DT if c < B else 0):
                    act.wait_ge(s["turned_x"], DT * c + d + 1)
                    act.activation(xT_hi[:, d, c * T:(c + 1) * T], GU[d][:, :], ACT.Copy).then_inc(s["xT_hi"], 1)
                if c:
                    act.wait_ge(s["logits_done"], c)
                    if c >= 3:
                        act.wait_ge(s["gate_done"], c - 2)
                    act.activation(silu[0:NG, (c - 1) % 2, :], DN[1 + (c - 1) % 2][0:NG, :], ACT.Copy)\
                       .then_inc(s["logits_kept"], 1)
            act.wait_ge(s["route"], 6)
            act.activation(w[:, :, :], gate[:, :, :], ACT.Exp).then_inc(s["routed"], 1)

            def hidden(n, j, a, shared, first=False):
                act.wait_ge(s["gate_up_done"], 2 * n + a + 1)
                if shared:
                    act.wait_ge(s["h_lo"], 2 * n + a - 1)
                dst = h if shared else silu
                act.activation(dst[:, a, :], GU[2 * a][:, :], ACT.Silu, bias=bias[:, j, 0, a:a + 1], scale=1.0)\
                   .then_inc(s["silu_done"], 1)

            def finish(c):
                act.wait_ge(s["aggregated"], TT * (c + 1))
                act.activation(sd[:, c * TT:(c + 1) * TT], mv[:, c * TT:(c + 1) * TT, 1], ACT.Sqrt,
                               bias=eps[:, 0:1], scale=1.0).then_inc(s["sd_done"], 1)

            def steps(n0, k0, shared, next_shared, last=False):
                for j in range(2):
                    for c in range(B):
                        end = j == 1 and c == B - 1
                        for a in range(0 if last and end else HT):
                            hidden(n0 + j * B + c + 1, j if c < B - 1 else 1 - j, a, next_shared if end else shared)
                        if last and j == 1:
                            finish(c)

            def keep_weights(q):
                act.wait_ge(s["w_blocks"], q + 1)
                act.activation(wT3[:, q * B * TT // 2:(q + 1) * B * TT // 2, :],
                               w_turned.rearrange("p (n c) -> p n c", c=P), ACT.Copy).then_inc(s["wT3_kept"], 1)

            for a in range(HT):
                hidden(0, 0, a, False)
            with act.Fori(0, EXPERTS // 2 - 1) as i:
                steps(2 * B * i, 2 * i, False, False)
            keep_weights(0)
            steps(2 * B * (EXPERTS // 2 - 1), EXPERTS - 2, False, True)
            keep_weights(1)
            steps(B * EXPERTS, EXPERTS, True, True, last=True)

        @block.vector
        def _(dve):
            dve.memset(eps[:, :], LN_EPS).then_inc(s["set"], 1)
            dve.memset(w3[:, :, :], 0.0).then_inc(s["set"], 1)
            dve.memset(wg_wide[:, :, :], 0.0).then_inc(s["set"], 1)
            dve.wait_ge(s["wg_loaded"], 16)
            dve.tensor_copy(wg_hi[:, :, :], wg_wide[:, :, :]).then_inc(s["wg_split"], 1)
            dve.wait_ge(s["wg_split"], 1)
            dve.tensor_tensor(wg_lo[:, :, :], wg_wide[:, :, :], f32(wg_hi[:, :, :]), ALU.subtract)\
               .then_inc(s["wg_split"], 1)

            def split_gu(k, j, width=2 * EH):
                dve.wait_ge(s["gu_loaded"], 32 * (k + 1))
                dve.tensor_copy(bias[:, j, :, :], bias_raw[:, :, :])
                dve.tensor_copy(gu_hi[:, j, :, 0:width], gu_raw[:, :, 0:width]).then_inc(s["gu_hi"], 1)

            def split_dn(k, j):
                dve.wait_ge(s["dn_loaded"], 16 * (k + 1))
                dve.tensor_copy(dn_hi[:, j, :, :], dn_raw[:, :, :]).then_inc(s["dn_hi"], 1)

            for n in range(B * DT):
                if n == 2 * DT:
                    split_gu(0, 0)
                if n == 3 * DT:
                    split_dn(0, 0)
                dve.wait_ge(s["xT_hi"], n + 1)
                c, d = divmod(n, DT)
                dve.tensor_tensor(xT_lo[:, d, c * T:(c + 1) * T], GU[d][:, :], f32(xT_hi[:, d, c * T:(c + 1) * T]),
                                  ALU.subtract).then_inc(s["xT_lo"], 1)

            def hidden(n, j, a, par, shared, first=False):
                dve.wait_ge(s["silu_done"], 2 * n + a + 1)
                if not shared:
                    if not first:
                        dve.wait_ge(s["h_lo"], 2 * n + a - 1)
                    dve.scalar_tensor_tensor(out=h[:, a, :], in0=GU[2 * a + 1][:, :], scalar=bias[:, j, 1, a:a + 1],
                                             in1=silu[:, a, :], op0=ALU.add, op1=ALU.mult).then_inc(s["h_done"], 1)
                    dve.wait_ge(s["h_done"], 2 * n + a + 1)
                dve.tensor_copy(h_hi[:, par, a, :], h[:, a, :]).then_inc(s["h_hi"], 1)

            N = B * TT
            cube = [P, N, NG, NG]
            dve.wait_ge(s["gate_done"], B)
            dve.wait_ge(const["x2_stored"], 16 * (B + 1))
            dve.wait_ge(s["small_loaded"], 16 * 5)
            dve.tensor_tensor(gate[:, :, :], DN[0][:, 0:N * NG].rearrange("p (n e) -> p n e", e=NG),
                              bg[:, :].unsqueeze(1).to_broadcast([P, N, NG]), ALU.add).then_inc(s["route"], 1)
            dve.wait_ge(s["route"], 1)
            other, own = gate[:, :, :].unsqueeze(2).to_broadcast(cube), gate[:, :, :].unsqueeze(3).to_broadcast(cube)
            dve.tensor_tensor(pairs[:, :, :, :], other, own, ALU.is_gt).then_inc(s["route"], 1)
            dve.tensor_tensor(ties[:, :, :, :], other, own, ALU.is_equal).then_inc(s["route"], 1)
            dve.tensor_reduce(row[:, 0, :], gate[:, :, :], AX.X, ALU.max).then_inc(s["route"], 1)
            dve.wait_ge(s["route"], 4)
            dve.tensor_tensor(ties[:, :, :, :], ties[:, :, :, :], before[:, :, :].unsqueeze(1).to_broadcast(cube),
                              ALU.mult).then_inc(s["route"], 1)
            dve.tensor_tensor(gate[:, :, :], gate[:, :, :], row[:, 0, :].unsqueeze(2).to_broadcast([P, N, NG]),
                              ALU.subtract).then_inc(s["route"], 1)
            dve.wait_ge(s["route"], 5)
            dve.tensor_tensor(pairs[:, :, :, :], pairs[:, :, :, :], ties[:, :, :, :], ALU.add).then_inc(s["route"], 1)
            dve.wait_ge(s["route"], 7)
            dve.tensor_reduce(keep[:, :, :], pairs[:, :, :, :], AX.X, ALU.add).then_inc(s["route"], 1)
            dve.wait_ge(s["route"], 8)
            dve.tensor_scalar(keep[:, :, :], keep[:, :, :], TOP - 0.5, None, ALU.is_lt).then_inc(s["route"], 1)
            dve.wait_ge(s["route"], 9)
            hidden(0, 0, 0, 0, False, first=True)
            dve.wait_ge(s["routed"], 1)
            dve.tensor_tensor(w[:, :, :], w[:, :, :], keep[:, :, :], ALU.mult).then_inc(s["route"], 1)
            dve.wait_ge(s["route"], 10)
            dve.tensor_reduce(row[:, 1, :], w[:, :, :], AX.X, ALU.add).then_inc(s["route"], 1)
            dve.wait_ge(s["route"], 11)
            dve.reciprocal(row[:, 2, :], row[:, 1, :]).then_inc(s["route"], 1)
            dve.wait_ge(s["route"], 12)
            dve.tensor_tensor(w[:, :, :], w[:, :, :], row[:, 2, :].unsqueeze(2).to_broadcast([P, N, NG]), ALU.mult)\
               .then_inc(s["route"], 1)
            dve.wait_ge(s["route"], 13)
            dve.memset(w[:, :, TOP:TOP + 1], 1.0).then_inc(s["route"], 1)
            dve.memset(w[:, :, TOP + 1:NG], 0.0).then_inc(s["route"], 1)

            def turn_weights(q):
                dve.wait_ge(s["w_spread"], q + 1)
                if q:
                    dve.wait_ge(s["wT3_kept"], 1)
                dve.transpose(w_turned, w_wide.rearrange("p n q r -> p (n q r)")).then_inc(s["w_blocks"], 1)

            def split_biases():
                dve.tensor_copy(bd_hi[:, :], bd_raw[:, :]).then_inc(s["bd_steps"], 1)
                dve.wait_ge(s["bd_steps"], 1)
                dve.tensor_tensor(bd_raw[:, :], bd_raw[:, :], f32(bd_hi[:, :]), ALU.subtract)\
                   .then_inc(s["bd_steps"], 1)
                dve.wait_ge(s["bd_steps"], 2)
                dve.tensor_scalar(bd_raw[:, :], bd_raw[:, :], bd_mask[:, 1:2], None, ALU.mult)\
                   .then_inc(s["bd_steps"], 1)
                dve.wait_ge(s["bd_steps"], 3)
                dve.scalar_tensor_tensor(out=bd3[:, :], in0=f32(bd_hi[:, :]), scalar=bd_mask[:, 0:1],
                                         in1=bd_raw[:, :], op0=ALU.mult, op1=ALU.add).then_inc(s["bd_steps"], 1)

            def accumulate(n, k, c, t, shared):
                dve.wait_ge(s["down_done"], TT * n + t + 1)
                tile = acc[:, c * TT + t, :]
                if shared:
                    dve.tensor_tensor(tile, DN[t][:, :], tile, ALU.add).then_inc(s["acc_done"], 1)
                else:
                    dve.scalar_tensor_tensor(out=tile, in0=DN[t][:, :], scalar=w[:, c * TT + t, bass.ts(k, 1)], in1=tile,
                                             op0=ALU.mult, op1=ALU.add).then_inc(s["acc_done"], 1)

            def finish(c):
                n = B * N_EXP - B + c
                for t in range(TT):
                    i = c * TT + t
                    dve.wait_ge(s["acc_done"], TT * n + t + 1)
                    dve.bn_stats(bn[:, i, :], acc[:, i, :]).then_inc(s["bn_done"], 1)
                    dve.wait_ge(s["bn_done"], i + 1)
                    dve.bn_aggr(mv[:, i, :], bn[:, i, :]).then_inc(s["aggregated"], 1)
                dve.wait_ge(s["sd_done"], c + 1)
                dve.reciprocal(rs[:, c * TT:(c + 1) * TT], sd[:, c * TT:(c + 1) * TT]).then_inc(s["rs_done"], 1)
                dve.wait_ge(s["rs_done"], c + 1)
                for t in range(TT):
                    i = c * TT + t
                    dve.tensor_scalar(acc[:, i, :], acc[:, i, :], mv[:, i, 0:1], rs[:, i:i + 1], ALU.subtract,
                                      ALU.mult).then_inc(s["out_done"], 1)

            def steps(n0, k0, shared, next_shared, last=False):
                for j in range(2):
                    for c in range(B):
                        n = n0 + j * B + c
                        end = j == 1 and c == B - 1
                        for a in range(HT):
                            if not (last and end):
                                hidden(n + 1, j if c < B - 1 else 1 - j, a, (c + 1) % 2,
                                       next_shared if end else shared)
                            for t in (2 * a, 2 * a + 1):
                                accumulate(n, k0 + j, c, t, shared)
                        if not (last and j == 1):
                            width = EH if shared or (next_shared and j == 1) else 2 * EH
                            if c == 0:
                                split_gu(k0 + j + 1, 1 - j, width)
                            if c == 1:
                                split_dn(k0 + j + 1, 1 - j)
                        if last and j == 1:
                            finish(c)

            hidden(0, 0, 1, 0, False, first=True)
            with dve.Fori(0, EXPERTS // 2 - 1) as i:
                steps(2 * B * i, 2 * i, False, False)
            turn_weights(0)
            split_biases()
            steps(2 * B * (EXPERTS // 2 - 1), EXPERTS - 2, False, True)
            turn_weights(1)
            steps(B * EXPERTS, EXPERTS, True, True, last=True)

        @block.gpsimd
        def _(pool):
            def split_gu(k, j, width=2 * EH):
                pool.wait_ge(s["gu_hi"], k + 1)
                pool.tensor_tensor(gu_lo[:, j, :, 0:width], gu_raw[:, :, 0:width], f32(gu_hi[:, j, :, 0:width]),
                                   ALU.subtract).then_inc(s["gu_lo"], 1)

            def split_dn(k, j):
                pool.wait_ge(s["dn_hi"], k + 1)
                pool.tensor_tensor(dn_lo[:, j, :, :], dn_raw[:, :, :], f32(dn_hi[:, j, :, :]), ALU.subtract)\
                    .then_inc(s["dn_lo"], 1)

            def low(n, a, par):
                pool.wait_ge(s["h_hi"], 2 * n + a + 1)
                pool.tensor_tensor(h_lo[:, par, a, :], h[:, a, :], f32(h_hi[:, par, a, :]), ALU.subtract)\
                    .then_inc(s["h_lo"], 1)

            def steps(n0, k0, shared, next_shared, last=False):
                for j in range(2):
                    for c in range(B):
                        if last and j == 1 and c == B - 1:
                            continue
                        for a in range(HT):
                            low(n0 + j * B + c + 1, a, (c + 1) % 2)
                        if not (last and j == 1):
                            width = EH if shared or (next_shared and j == 1) else 2 * EH
                            if c == 0:
                                split_gu(k0 + j + 1, 1 - j, width)
                            if c == 1:
                                split_dn(k0 + j + 1, 1 - j)

            split_gu(0, 0)
            split_dn(0, 0)
            for a in range(HT):
                low(0, a, 0)
            pool.wait_ge(s["route"], 15)
            pool.wait_ge(s["set"], 2)
            pool.tensor_copy(w_hi[:, :, :], w[:, :, :]).then_inc(s["w_split"], 1)
            pool.wait_ge(s["w_split"], 1)
            for j in range(2):
                pool.tensor_copy(w3[:, :, j * NG:(j + 1) * NG], f32(w_hi[:, :, :])).then_inc(s["w_split"], 1)
            pool.tensor_tensor(w3[:, :, 2 * NG:3 * NG], w[:, :, :], f32(w_hi[:, :, :]), ALU.subtract)\
                .then_inc(s["w_split"], 1)
            pool.wait_ge(s["w_split"], 4)

            def spread_weights(q):
                n = B * TT // 2
                pool.tensor_tensor(w_wide, w3[:, q * n:(q + 1) * n, :].unsqueeze(2).to_broadcast([P, n, 4, QUAD]),
                                   quads[:, :].unsqueeze(1).unsqueeze(3).to_broadcast([P, n, 4, QUAD]), ALU.mult)\
                    .then_inc(s["w_spread"], 1)

            spread_weights(0)
            with pool.Fori(0, EXPERTS // 2 - 1) as i:
                steps(2 * B * i, 2 * i, False, False)
            pool.wait_ge(s["w_blocks"], 1)
            spread_weights(1)
            steps(2 * B * (EXPERTS // 2 - 1), EXPERTS - 2, False, True)
            steps(B * EXPERTS, EXPERTS, True, True, last=True)


def build(nc, dram):
    with ExitStack() as ctx:
        const = constants(nc, ctx)
        const["result"] = ctx.enter_context(nc.sbuf_tensor("result", [P, TT, D], F32))
        for name in ("x1_stored", "x2_stored"):
            const[name] = ctx.enter_context(nc.semaphore(name))
        attention_phase(nc, const, dram)
        cross_phase(nc, const, dram)
        ffn_phase(nc, const, dram)


def rope_tables():
    inv_freq = np.float32(1.0) / np.float32(10000.0) ** (np.arange(0, ROPE, 2, dtype=np.float32) / np.float32(ROPE))
    freqs = np.outer(np.arange(T, dtype=np.float32), inv_freq).astype(np.float32)
    cos, sin = np.cos(freqs).T, np.sin(freqs).T
    one = np.ones((ROPE, T), np.float32)
    even = np.concatenate([one, cos, cos])
    odd = np.concatenate([cos, cos, one])
    signed = np.concatenate([-sin, sin, -sin, sin])
    by_dim = np.stack([even, odd, signed], axis=1).astype(np.float32)
    tok = np.stack([np.cos(freqs), np.sin(freqs)], axis=1).astype(np.float32)
    return np.ascontiguousarray(by_dim), np.ascontiguousarray(tok.reshape(TT, P, 2, HALF).transpose(1, 0, 2, 3))


def cross_masks():
    p = np.arange(P)
    main = p % KEYS < MAIN
    head = p // HD == np.arange(P // HD)[:, None]
    half, own = np.arange(2)[:, None], p[:, None, None] // KEYS
    cols = (p // HD == 2 * half[None] + own)
    masks = {"xmasks": np.stack([main, ~main], axis=1), "kmask": head.T, "vmask": cols}
    return {n: v.astype(np.float32) for n, v in masks.items()}


def ffn_masks():
    p, e = np.arange(P), np.arange(NG)
    part = p % QUAD // NG
    masks = {"before": e[None, :] < e[:, None], "quads": p[:, None] // QUAD == np.arange(4),
             "bd_mask": np.stack([(part == 0) | (part == 2), part == 1], axis=1)}
    return {n: v.astype(np.float32) for n, v in masks.items()}


def lay_out(inputs):
    a = {n: np.asarray(v) for n, v in inputs.items()}
    out = {"x": a["x"]}
    out["wa"] = np.concatenate([a["L0_attn_wq_a"], a["L0_attn_wkv_a"]], axis=1)
    kv = a["L0_attn_wkv_b"].reshape(KVR, H, NOPE + VD)
    out["wv"] = kv[:, :, NOPE:].transpose(1, 0, 2)
    out["wo"] = a["L0_attn_wo"].reshape(H, VD, D)
    q = a["L0_attn_wq_b"].reshape(QR, PAIRS, 2, 2, DK // 2)
    q = np.stack([q[:, :, 0], q[:, :, 1, ::-1]], axis=2).reshape(QR, PAIRS, 2 * DK).transpose(1, 0, 2)
    k = kv[:, :, :NOPE].reshape(KVR, PAIRS, 2 * NOPE).transpose(1, 0, 2)
    rest = np.zeros((PAIRS, P, 2 * DK), np.float32)
    rest[:, :QR2] = q[:, P:]
    out["ws"] = np.concatenate([q[:, :P], rest, k], axis=2)
    qn = a["L0_attn_q_a_norm_w"]
    rest = np.zeros(P, np.float32)
    rest[:QR2] = qn[P:]
    out["norm_w"] = np.stack([qn[:P], rest, a["L0_attn_kv_a_norm_w"]], axis=1)
    out["rope_T"], out["rope_tok"] = rope_tables()
    out["ctx"] = a["ctx_1024"]
    out["xwq"], out["xwo"] = a["L0_xattn_Wq"], a["L0_xattn_Wo"]
    wk_dca, wv_dca = a["L0_xattn_Wkv_dca"][:, :D], a["L0_xattn_Wkv_dca"][:, D:]
    bk_dca, bv_dca = a["L0_xattn_bkv_dca"][:D], a["L0_xattn_bkv_dca"][D:]
    w = np.concatenate([a["L0_xattn_Wk"], a["L0_xattn_Wv"]], axis=1).reshape(CD, XH, 2, HD)
    bias = np.concatenate([a["L0_xattn_bk"], a["L0_xattn_bv"]]).reshape(XH, 2, HD)
    wk, wv = w[:, :, 0].reshape(CD, D), w[:, :, 1].reshape(CD, D)
    bk, bv = bias[:, 0].reshape(D), bias[:, 1].reshape(D)
    out["xwkv"] = np.stack([wk, wk_dca, wv, wv_dca], axis=1)
    out["xrows"] = np.stack([a["L0_xattn_bq"], bk, bk_dca, bv, bv_dca, a["L0_xattn_bo"]])
    out["xln_wb"] = np.stack([np.stack([a[f"L0_xattn_{n}_{p}"] for n in ("qn", "kn", "kn_dca")]) for p in "wb"])
    out.update(cross_masks())
    f = {n[7:]: v for n, v in a.items() if n.startswith("L0_ffn_")}
    out["wg"], out["bg"] = f["Wg"], f["bg"]
    out["wgu"], out["wdn"] = np.concatenate([f["Wgate"], f["Wup"]], axis=2), f["Wdown"]
    out["wsu"] = f["Ws_up"].reshape(D, 2, EH).transpose(1, 0, 2)
    out["wsd"] = f["Ws_down"].reshape(2, EH, D)
    none = np.zeros((2, EH), np.float32)
    by_gate = np.concatenate([f["bgate"], f["bs_up"].reshape(2, EH)])
    by_up = np.concatenate([f["bup"], none])
    out["fbias"] = np.stack([by_gate, by_up]).reshape(2, N_EXP, HT, P).transpose(1, 3, 0, 2)
    rest = np.zeros((1, D), np.float32)
    down = np.concatenate([f["bdown"], f["bs_down"][None], rest])
    rest = np.zeros((QUAD - 3 * NG, D), np.float32)
    out["bd"] = np.concatenate([down, down, down, rest] * 4)
    out.update(ffn_masks())
    return {n: np.ascontiguousarray(v) for n, v in out.items()}


def kernel(**inputs):
    import concourse.bacc as bacc
    from concourse.bass_utils import run_bass_kernel_spmd

    nc = bacc.Bacc("TRN2", target_bir_lowering=False, num_devices=1)
    arrays = {f"in_{n}_dram": v for n, v in lay_out(inputs).items()}
    dram = {n[3:-5]: nc.dram_tensor(n, v.shape, mybir.dt.from_np(v.dtype), kind="ExternalInput").ap()
            for n, v in arrays.items()}
    dram["x1"] = nc.dram_tensor("x1_dram", (B, T, D), F32, kind="Internal").ap()
    dram["x2"] = nc.dram_tensor("x2_dram", (B, T, D), F32, kind="Internal").ap()
    dram["out"] = nc.dram_tensor("out_0_dram", (B, T, D), F32, kind="ExternalOutput").ap()
    build(nc, dram)
    r = run_bass_kernel_spmd(nc, [arrays], core_ids=[0])
    return r.results[0]["out_0_dram"]
```
